# Optimizing a Trainium2 kernel written in Bass

```python
import numpy as np
import jax
import jax.numpy as jnp

def _softmax(x, axis=-1):
    return jax.nn.softmax(x, axis=axis)

def _gelu(x):
    return jax.nn.gelu(x, approximate=True)

def _silu(x):
    return jax.nn.silu(x)

def _sigmoid(x):
    return jax.nn.sigmoid(x)

def _layernorm(x, axis=-1, eps=1e-05):
    m = jnp.mean(x, axis=axis, keepdims=True)
    v = jnp.var(x, axis=axis, keepdims=True)
    return (x - m) / jnp.sqrt(v + eps)

def _scatter_add(tgt, idx, src, axis=0):
    return tgt.at[idx].add(src)

def _segment_sum(src, seg, n):
    return jax.ops.segment_sum(src, seg, n)
kernel_name = 'mk_early_fusion_embed_d1_tok_img768_r4_4d7ee8'

def setup_inputs(seed: int=0):
    np.random.seed(seed)
    _w = jnp.asarray

    def _rec_inputs():
        import jax
        import jax.numpy as jnp
        _rk = jax.random.key(seed)
        x = -0.000356955 + 1 * jax.random.normal(jax.random.fold_in(_rk, 1), (16, 3, 224, 224), jnp.float32)
        x_txt = jax.random.randint(jax.random.fold_in(_rk, 51), (16, 512), 0, 127999, jnp.int32)
        return (x, x_txt)
    x, x_txt = _rec_inputs()

    def _L0_tok_setup():
        import jax, jax.numpy as jnp
        import numpy as np
        PH = PW = 16

        def _patchify(x):
            B, C, H, Wd = x.shape
            nh, nw = (H // PH, Wd // PW)
            x = x.reshape(B, C, nh, PH, nw, PW)
            x = x.transpose(0, 2, 4, 3, 5, 1)
            return x.reshape(B, nh * nw, PH * PW * C)
        key = jax.random.key(seed)
        k1, k2, k3, k4, k5 = jax.random.split(key, 5)
        B, C, H, W_img = (128, 3, 224, 224)
        D = 192
        n_patches = H // PH * (W_img // PW)
        return {'x': jax.random.normal(k1, (B, C, H, W_img), dtype=jnp.float32), 'W': jax.random.normal(k2, (C * PH * PW, D), dtype=jnp.float32) * 0.02, 'b': jax.random.normal(k3, (D,), dtype=jnp.float32) * 0.02, 'cls': jax.random.normal(k4, (1, D), dtype=jnp.float32), 'pos_embed': jax.random.normal(k5, (1, n_patches + 1, D), dtype=jnp.float32) * 0.02}
    _L0_tok_all = _L0_tok_setup()
    _L0_tok_in = {k: v for k, v in _L0_tok_all.items() if k in ('W', 'b', 'cls', 'pos_embed')}
    del _L0_tok_all

    def _L0_txt_setup():
        import jax, jax.numpy as jnp
        import numpy as np
        import math
        VOCAB = 32000
        BASIN_DIM = 64
        D_MODEL = 192
        EPS = 1e-08
        key = jax.random.key(seed)
        k1, k2, k3, k4 = jax.random.split(key, 4)
        token_ids = jax.random.randint(k1, (8, 1024), 0, VOCAB, dtype=jnp.int32)
        coords = jax.random.normal(k2, (VOCAB, BASIN_DIM), dtype=jnp.float32)
        coords = coords / jnp.linalg.norm(coords, axis=-1, keepdims=True)
        coords = coords * (math.sqrt(BASIN_DIM) / 5.0)
        coords = coords + jax.random.normal(k3, coords.shape, dtype=jnp.float32) * 0.01
        w = jax.random.normal(k4, (D_MODEL, BASIN_DIM), dtype=jnp.float32)
        q, _ = jnp.linalg.qr(w)
        proj_w = q * 0.1
        norm_w = jnp.ones((D_MODEL,), dtype=jnp.float32)
        return {'token_ids': token_ids, 'basin_coords': coords, 'proj_w': proj_w, 'norm_w': norm_w}
    _L0_txt_all = _L0_txt_setup()
    _L0_txt_in = {k: v for k, v in _L0_txt_all.items() if k in ('basin_coords', 'proj_w', 'norm_w')}
    del _L0_txt_all

    def _L0_attn_setup():
        import jax, jax.numpy as jnp
        import numpy as np
        NH, DK, DV, D = (8, 64, 64, 192)
        DECAY = 0.95
        WRITE_STRENGTH = 0.1
        key = jax.random.key(seed)
        ks = jax.random.split(key, 6)
        s = 0.02
        return {'x': jax.random.normal(ks[0], (4, 1024, D), dtype=jnp.float32), 'w_key': jax.random.normal(ks[1], (NH * DK, D), dtype=jnp.float32) * s, 'w_value': jax.random.normal(ks[2], (NH * DV, D), dtype=jnp.float32) * s, 'w_query': jax.random.normal(ks[3], (NH * DK, D), dtype=jnp.float32) * s, 'w_gate': jax.random.normal(ks[4], (NH, D), dtype=jnp.float32) * s, 'w_out': jax.random.normal(ks[5], (D, NH * DV), dtype=jnp.float32) * s}
    _L0_attn_all = _L0_attn_setup()
    _L0_attn_in = {k: v for k, v in _L0_attn_all.items() if k in ('w_key', 'w_value', 'w_query', 'w_gate', 'w_out')}
    del _L0_attn_all

    def _L0_ffn_setup():
        import jax, jax.numpy as jnp
        import numpy as np
        B, S, D = (4, 256, 192)
        E = 8
        H = 192
        HS = 768
        TOPK_ROUTED = 2
        key = jax.random.key(seed)
        ks = jax.random.split(key, 10)
        w = lambda k, shape: jax.random.normal(k, shape, dtype=jnp.float32) * 0.02
        return {'x': jax.random.normal(ks[0], (B, S, D), dtype=jnp.float32), 'router_w': w(ks[1], (D, E)), 'w_gate': w(ks[2], (E, D, H)), 'w_up': w(ks[3], (E, D, H)), 'w_down': w(ks[4], (E, H, D)), 'ws_gate': w(ks[5], (D, HS)), 'ws_up': w(ks[6], (D, HS)), 'ws_down': w(ks[7], (HS, D)), 'sg_w': w(ks[8], (D, 1)), 'sg_b': jnp.zeros((1,), jnp.float32)}
    _L0_ffn_all = _L0_ffn_setup()
    _L0_ffn_in = {k: v for k, v in _L0_ffn_all.items() if k in ('router_w', 'w_gate', 'w_up', 'w_down', 'ws_gate', 'ws_up', 'ws_down', 'sg_w', 'sg_b')}
    del _L0_ffn_all
    return {'x': x, 'x_txt': x_txt, 'L0_tok_W': _L0_tok_in['W'], 'L0_tok_b': _L0_tok_in['b'], 'L0_tok_cls': _L0_tok_in['cls'], 'L0_tok_pos_embed': _L0_tok_in['pos_embed'], 'L0_txt_basin_coords': _L0_txt_in['basin_coords'], 'L0_txt_proj_w': _L0_txt_in['proj_w'], 'L0_txt_norm_w': _L0_txt_in['norm_w'], 'L0_attn_w_key': _L0_attn_in['w_key'], 'L0_attn_w_value': _L0_attn_in['w_value'], 'L0_attn_w_query': _L0_attn_in['w_query'], 'L0_attn_w_gate': _L0_attn_in['w_gate'], 'L0_attn_w_out': _L0_attn_in['w_out'], 'L0_ffn_router_w': _L0_ffn_in['router_w'], 'L0_ffn_w_gate': _L0_ffn_in['w_gate'], 'L0_ffn_w_up': _L0_ffn_in['w_up'], 'L0_ffn_w_down': _L0_ffn_in['w_down'], 'L0_ffn_ws_gate': _L0_ffn_in['ws_gate'], 'L0_ffn_ws_up': _L0_ffn_in['ws_up'], 'L0_ffn_ws_down': _L0_ffn_in['ws_down'], 'L0_ffn_sg_w': _L0_ffn_in['sg_w'], 'L0_ffn_sg_b': _L0_ffn_in['sg_b']}

def reference(x, x_txt, L0_tok_W, L0_tok_b, L0_tok_cls, L0_tok_pos_embed, L0_txt_basin_coords, L0_txt_proj_w, L0_txt_norm_w, L0_attn_w_key, L0_attn_w_value, L0_attn_w_query, L0_attn_w_gate, L0_attn_w_out, L0_ffn_router_w, L0_ffn_w_gate, L0_ffn_w_up, L0_ffn_w_down, L0_ffn_ws_gate, L0_ffn_ws_up, L0_ffn_ws_down, L0_ffn_sg_w, L0_ffn_sg_b):
    import jax
    import jax.numpy as jnp

    def _L0_tok_ref(x, W, b, cls, pos_embed):
        import jax, jax.numpy as jnp
        import numpy as np
        PH = PW = 16

        def _patchify(x):
            B, C, H, Wd = x.shape
            nh, nw = (H // PH, Wd // PW)
            x = x.reshape(B, C, nh, PH, nw, PW)
            x = x.transpose(0, 2, 4, 3, 5, 1)
            return x.reshape(B, nh * nw, PH * PW * C)
        B = x.shape[0]
        patches = _patchify(x)
        out = jnp.einsum('bnp,pd->bnd', patches, W) + b
        cls_tok = jnp.broadcast_to(cls[None], (B, 1, cls.shape[-1]))
        out = jnp.concatenate([cls_tok, out], axis=1)
        out = out + pos_embed
        return out

    def _L0_txt_ref(token_ids, basin_coords, proj_w, norm_w):
        import jax, jax.numpy as jnp
        import numpy as np
        import math
        VOCAB = 32000
        BASIN_DIM = 64
        D_MODEL = 192
        EPS = 1e-08
        basin = basin_coords[token_ids]
        emb = jnp.einsum('bsk,dk->bsd', basin, proj_w)
        x_f = emb.astype(jnp.float32)
        rms = jnp.sqrt(jnp.mean(x_f * x_f, axis=-1, keepdims=True) + EPS)
        y = (x_f / rms).astype(emb.dtype)
        return y * norm_w

    def _L0_attn_ref(x, w_key, w_value, w_query, w_gate, w_out):
        import jax, jax.numpy as jnp
        import numpy as np
        NH, DK, DV, D = (8, 64, 64, 192)
        DECAY = 0.95
        WRITE_STRENGTH = 0.1
        B, S, _ = x.shape
        k = (x @ w_key.T).reshape(B, S, NH, DK)
        v = (x @ w_value.T).reshape(B, S, NH, DV)
        q = (x @ w_query.T).reshape(B, S, NH, DK)
        gate = jax.nn.sigmoid(x @ w_gate.T)
        k0 = k[0]
        v0 = v[0]
        g0 = gate[0]

        def step(fw, inp):
            q_t, k0_t, v0_t, g0_t = inp
            retrieved = jnp.einsum('bhk,hkv->bhv', q_t, fw)
            write = (WRITE_STRENGTH * g0_t)[:, None, None] * (k0_t[:, :, None] * v0_t[:, None, :])
            fw_new = DECAY * fw + jax.lax.stop_gradient(write)
            return (fw_new, retrieved)
        fw0 = jnp.zeros((NH, DK, DV), dtype=x.dtype)
        inputs = (q.transpose(1, 0, 2, 3), k0, v0, g0)
        _, retrieved = jax.lax.scan(step, fw0, inputs)
        retrieved = retrieved.transpose(1, 0, 2, 3).reshape(B, S, NH * DV)
        return x + retrieved @ w_out.T

    def _L0_ffn_ref(x, router_w, w_gate, w_up, w_down, ws_gate, ws_up, ws_down, sg_w, sg_b):
        import jax, jax.numpy as jnp
        import numpy as np
        B, S, D = (4, 256, 192)
        E = 8
        H = 192
        HS = 768
        TOPK_ROUTED = 2
        probs = jax.nn.softmax(x @ router_w, axis=-1)
        gates, idx = jax.lax.top_k(probs, TOPK_ROUTED)
        gates = gates / jnp.sum(gates, axis=-1, keepdims=True)
        n_exp = router_w.shape[1]
        dense_g = jnp.sum(jax.nn.one_hot(idx, n_exp, dtype=x.dtype) * gates[..., None], axis=-2)
        g = jax.nn.silu(jnp.einsum('bsd,edh->bseh', x, w_gate))
        u = jnp.einsum('bsd,edh->bseh', x, w_up)
        expert_out = jnp.einsum('bseh,ehd->bsed', g * u, w_down)
        routed = jnp.einsum('bse,bsed->bsd', dense_g, expert_out)
        shared = jax.nn.silu(x @ ws_gate) * (x @ ws_up) @ ws_down
        alpha = jax.nn.sigmoid(x @ sg_w + sg_b)
        return alpha * shared + (1.0 - alpha) * routed
    h = _L0_tok_ref(x, L0_tok_W, L0_tok_b, L0_tok_cls, L0_tok_pos_embed)
    h = jnp.concatenate([h, _L0_txt_ref(x_txt, L0_txt_basin_coords, L0_txt_proj_w, L0_txt_norm_w)], axis=1)
    h = h + _L0_attn_ref(_layernorm(h, axis=-1), L0_attn_w_key, L0_attn_w_value, L0_attn_w_query, L0_attn_w_gate, L0_attn_w_out)
    h = h + _L0_ffn_ref(_layernorm(h, axis=-1), L0_ffn_router_w, L0_ffn_w_gate, L0_ffn_w_up, L0_ffn_w_down, L0_ffn_ws_gate, L0_ffn_ws_up, L0_ffn_ws_down, L0_ffn_sg_w, L0_ffn_sg_b)
    return h

_drawn_inputs = setup_inputs


def setup_inputs(seed=0):
    import zlib

    import numpy as np

    out = dict(_drawn_inputs(seed))
    spreads = {'L0_txt_norm_w': (1.0, 0.2)}
    factors = {'L0_tok_b': 3.62,
     'L0_tok_pos_embed': 3.653,
     'L0_attn_w_gate': 8.0,
     'L0_ffn_router_w': 8.0,
     'L0_ffn_w_gate': 8.0,
     'L0_ffn_w_up': 8.0,
     'L0_ffn_w_down': 8.0,
     'L0_ffn_ws_gate': 8.0,
     'L0_ffn_ws_up': 8.0,
     'L0_ffn_ws_down': 8.0,
     'L0_ffn_sg_w': 8.0}
    for name, (base, spread) in spreads.items():
        noise = np.random.default_rng([zlib.crc32(name.encode()), seed]).standard_normal(out[name].shape)
        drawn = base * np.exp(spread * noise) if base else spread * noise
        out[name] = jnp.asarray(drawn.astype(out[name].dtype))
    for name, factor in factors.items():
        out[name] = (out[name] * factor).astype(out[name].dtype)
    return out
```

```python
import concourse.bass as bass
from concourse import mybir
from contextlib import ExitStack

F32 = mybir.dt.float32
F32R = mybir.dt.float32r
BF16 = mybir.dt.bfloat16
I32 = mybir.dt.int32
U32 = mybir.dt.uint32
ACT = mybir.ActivationFunctionType
ALU = mybir.AluOpType
AX = mybir.AxisListType

P = 128
B, T, D = 16, 709, 192
DA, DB = 128, D - 128
NPATCH, SIDE, PX = 196, 14, 16
NTXT, BASIN, VOCAB = 512, 64, 32000
NH, DK = 8, 64
STEP = 16
NCH = -(-T // STEP)
TPAD = NCH * STEP
HB = B // 2
NE, HE, HS = 8, 192, 768
CAP = B * TPAD + P
NTILE = -(-((2 * B * TPAD + NE * (P - 1)) // P) // 4) * 4
DUMMY = NE * CAP
NDUMMY = NTILE - 2 * B * TPAD // P
ROWS = DUMMY + NDUMMY * P
DECAY, WRITE = 0.95, 0.1
LN_EPS, RMS_EPS = 1e-5, 1e-8


def mm(nc, out, pairs, start=True, stop=True):
    for n, (lhsT, rhs) in enumerate(pairs):
        last = nc.tensor.matmul(out, lhsT, rhs, start=start and n == 0, stop=stop and n == len(pairs) - 1)
    return last


def prepare(nc, I, scratch, W, C):
    hbuf = scratch["hbuf"]
    ctx = ExitStack()
    sems = []
    with ctx:
        def sb(name, shape, dt=F32):
            return ctx.enter_context(nc.sbuf_tensor(name, shape, dt))

        def pb(name, shape, dt=F32):
            return ctx.enter_context(nc.psum_tensor(name, shape, dt))

        def sem(name):
            sems.append(nc.alloc_semaphore(name))
            return sems[-1]

        raw = [sb(f"raw{n}", [P, 1536]) for n in range(2)]
        img = [sb(f"img{n}", [96, SIDE, SIDE * PX]) for n in range(2)]
        tokw = sb("tokw", [96, 8, D])
        posb = sb("posb", [98, 2, D])
        bias_bc = sb("bias_bc", [98, D])
        pstage = [sb(f"pstage{n}", [98, 2, D]) for n in range(2)]
        cls_row = sb("cls_row", [B, D])
        pos0_row = sb("pos0_row", [B, D])
        cls_out = sb("cls_out", [B, D])
        zeros = sb("zeros", [P, D])
        projn = sb("projn", [P, 2, 2, BASIN])
        projT = sb("projT", [P, D])
        normw = sb("normw", [P, D])
        ids = sb("ids", [P, B, 4], I32)
        idsf = sb("idsf", [P, B, 4])
        idneg = sb("idneg", [P, B, 4])
        ids_ok = sb("ids_ok", [P, B, 4], U32)
        idc = [sb(f"idc{n}", [P, 4], U32) for n in range(2)]
        basin = [sb(f"basin{n}", [P, 4, BASIN]) for n in range(2)]
        basinT = [sb(f"basinT{n}", [P, 2, P]) for n in range(2)]
        sq = [sb(f"sq{n}", [P, 4, D]) for n in range(2)]
        ssq = [sb(f"ssq{n}", [P, 4]) for n in range(2)]
        msq = [sb(f"msq{n}", [P, 4]) for n in range(2)]
        rinv = [sb(f"rinv{n}", [P, 4]) for n in range(2)]
        tstage = [sb(f"tstage{n}", [P, 4, D]) for n in range(2)]
        tmp_i = sb("tmp_i", [P, 1], I32)
        part_i = sb("part_i", [P, 1], I32)
        s_f = sb("s_f", [P, 1])
        drow = sb("drow", [1, 2, P])
        one1 = sb("one1", [1, 1])

        ps_img = [pb(f"ps_img{n}", [P, 512]) for n in range(2)]
        ps_tT = [pb(f"ps_tT{n}", [P, 512]) for n in range(2)]
        ps_emb = [pb(f"ps_emb{n}", [P, 2, 512]) for n in range(2)]

        s_raw = [sem(f"raw_in{n}") for n in range(2)]
        s_hi = sem("hi_done")
        s_lo = sem("lo_done")
        s_tokw = sem("tokw_in")
        s_small = sem("small_in")
        s_ids = sem("ids_in")
        s_img = [sem(f"img_in{n}") for n in range(2)]
        s_posb = sem("posb_done")
        s_pmm = sem("patch_product")
        s_pst = sem("patch_staged")
        s_pout = [sem(f"patch_stored{n}") for n in range(2)]
        s_cls = sem("cls_done")
        s_clsout = sem("cls_stored")
        s_zero = sem("zeros_done")
        s_zout = sem("pads_stored")
        s_iota = sem("iota_done")
        s_const = sem("const_step")
        s_ident = sem("ident_done")
        s_drow = sem("decay_row")
        s_dcol = sem("decay_column")
        s_projT = sem("projT_product")
        s_projTc = sem("projT_done")
        s_idok = sem("ids_ok")
        s_idc = sem("ids_copied")
        s_apart = sem("apart")
        s_bas = [sem(f"basin_in{n}") for n in range(2)]
        s_bT = sem("basinT_product")
        s_bTc = sem("basinT_done")
        s_emb = sem("emb_product")
        s_ssq = sem("squares_summed")
        s_msq = sem("mean_square")
        s_rinv = sem("rms_inverse")
        s_tst = sem("text_staged")
        s_tout = [sem(f"text_stored{n}") for n in range(2)]
        block = ctx.enter_context(nc.Block())

        wg, wu, wd = (I[k].rearrange("e d h -> d e h") for k in ("L0_ffn_w_gate", "L0_ffn_w_up", "L0_ffn_w_down"))
        sg, su = I["L0_ffn_ws_gate"], I["L0_ffn_ws_up"]
        sd = I["L0_ffn_ws_down"].rearrange("(m p) d -> p m d", p=P)

        def pairs4(r):
            return r[:, :].rearrange("p (e n) -> p e n", e=4)

        pieces = []
        for e0 in (0, 4):
            pieces.append(([(lambda r: pairs4(r)[:, :, 0:HE], wg[0:DA, e0:e0 + 4, :]),
                            (lambda r: pairs4(r)[:, :, HE:2 * HE], wu[0:DA, e0:e0 + 4, :])],
                           W["gu_a"], slice(e0 * 2 * HE, (e0 + 4) * 2 * HE)))
            pieces.append(([(lambda r, q=q: pairs4(r)[q:q + DB, :, 0:HE], wg[DA:D, e0:e0 + 4, :]) for q in (0, 64)]
                           + [(lambda r, q=q: pairs4(r)[q:q + DB, :, HE:2 * HE], wu[DA:D, e0:e0 + 4, :]) for q in (0, 64)],
                           W["gu_b"], slice(e0 * 2 * HE, (e0 + 4) * 2 * HE)))
        pieces.append(([(lambda r: r[:, :].rearrange("p (e n) -> p e n", e=NE), wd[0:DA, :, :])],
                       W["dn_a"], slice(0, NE * D)))
        pieces.append(([(lambda r, q=q: r[q:q + DB, :].rearrange("p (e n) -> p e n", e=NE), wd[DA:D, :, :]) for q in (0, 64)],
                       W["dn_b"], slice(0, NE * D)))
        pieces.append(([(lambda r: r[:, 0:HS], sg[0:DA, :]), (lambda r: r[:, HS:2 * HS], su[0:DA, :])],
                       W["sgu_a"], slice(0, 2 * HS)))
        pieces.append(([(lambda r, q=q: r[q:q + DB, 0:HS], sg[DA:D, :]) for q in (0, 64)]
                       + [(lambda r, q=q: r[q:q + DB, HS:2 * HS], su[DA:D, :]) for q in (0, 64)],
                       W["sgu_b"], slice(0, 2 * HS)))
        pieces.append(([(lambda r: r[:, 0:6 * D].rearrange("p (m d) -> p m d", m=6), sd)],
                       W["sdn"], slice(0, 6 * D)))
        raw_count = [[0, 0]]
        for n, (dmas, _, _) in enumerate(pieces):
            c = list(raw_count[-1])
            c[n % 2] += 16 * len(dmas)
            raw_count.append(c)

        tokw_v = I["L0_tok_W"].rearrange("(i s j c) d -> s c i j d", i=PX, s=2, c=3)
        pos = I["L0_tok_pos_embed"]

        @block.sync
        def _(sp):
            for s in range(2):
                for c in range(3):
                    q = (3 * s + c) * PX
                    sp.dma_start(tokw[q:q + PX, :, :], tokw_v[s, c]).then_inc(s_tokw, 16)
            sp.dma_start(bias_bc[:, :], I["L0_tok_b"].partition_broadcast(98)).then_inc(s_small, 16)
            sp.dma_start(posb[:, :, :], pos[0, 1:NPATCH + 1, :].rearrange("(g p) d -> p g d", p=98)).then_inc(s_small, 16)
            sp.dma_start(cls_row[:, :], I["L0_tok_cls"][0, :].partition_broadcast(B)).then_inc(s_small, 16)
            sp.dma_start(pos0_row[:, :], pos[0, 0, :].partition_broadcast(B)).then_inc(s_small, 16)
            sp.dma_start(normw[:, :], I["L0_txt_norm_w"].partition_broadcast(P)).then_inc(s_small, 16)
            for q in range(2):
                sp.dma_start(projn[:, 0, q, :], I["L0_txt_proj_w"][0:P, :]).then_inc(s_small, 16)
                sp.dma_start(projn[0:DB, 1, q, :], I["L0_txt_proj_w"][P:D, :]).then_inc(s_small, 16)
            sp.dma_start(W["rw_a"][:, 0:NE], I["L0_ffn_router_w"][0:DA, :]).then_inc(s_small, 16)
            sp.dma_start(W["rw_b"][:, 0:NE], I["L0_ffn_router_w"][DA:D, :]).then_inc(s_small, 16)
            sp.dma_start(W["rw_a"][:, NE:NE + 1], I["L0_ffn_sg_w"][0:DA, :]).then_inc(s_small, 16)
            sp.dma_start(W["rw_b"][:, NE:NE + 1], I["L0_ffn_sg_w"][DA:D, :]).then_inc(s_small, 16)
            sp.dma_start(C["sgb"][:, :], I["L0_ffn_sg_b"].partition_broadcast(P)).then_inc(s_small, 16)
            with sp.Fori(0, HB) as pair:
                for u in range(2):
                    sp.wait_ge(s_pmm, 2 * pair + 1 + u)
                    for s in range(2):
                        for c in range(3):
                            q = (3 * s + c) * PX
                            src = I["x"][bass.ds(2 * pair + u, 1), c, :, :].rearrange("b (n i) w -> (b i) n w", i=PX)
                            n = SIDE * PX - 8 * s
                            sp.dma_start(img[u][q:q + PX, :, 0:n], src[:, :, 8 * s:8 * s + n]).then_inc(s_img[u], 16)
            for u in range(2):
                sp.wait_ge(s_pout[u], 16 * HB + 16)
                sp.wait_ge(s_tout[u], 16 * HB + 16)
            sp.wait_ge(s_clsout, 16)
            sp.wait_ge(s_zout, 32)

        @block.gpsimd
        def _(pool):
            nc.gpsimd.memset(zeros[:, :], 0.0).then_inc(s_zero, 1)
            nc.gpsimd.memset(C["ident"][:, :], 0.0).then_inc(s_zero, 1)
            nc.gpsimd.memset(C["tri"][:, :], 0.0).then_inc(s_zero, 1)
            nc.gpsimd.memset(C["ones"][:, :], 1.0).then_inc(s_zero, 1)
            nc.gpsimd.memset(C["neghalf"][:, :], -0.5).then_inc(s_zero, 1)
            nc.gpsimd.iota(C["iota8"][:, :], pattern=[[1, NE]], base=0, channel_multiplier=0,
                           allow_small_or_imprecise_dtypes=True).then_inc(s_iota, 1)
            nc.gpsimd.iota(C["ebase"][:, :], pattern=[[CAP, NE]], base=0, channel_multiplier=0,
                           allow_small_or_imprecise_dtypes=True).then_inc(s_iota, 1)
            nc.gpsimd.iota(part_i[:, :], pattern=[[0, 1]], base=0, channel_multiplier=1).then_inc(s_iota, 1)
            nc.gpsimd.iota(C["partf"][:, :], pattern=[[0, 1]], base=0, channel_multiplier=1,
                           allow_small_or_imprecise_dtypes=True).then_inc(s_iota, 1)
            nc.gpsimd.iota(C["maskf"][:, :, :], pattern=[[0, 2 * HB], [1, STEP]], base=0, channel_multiplier=0,
                           allow_small_or_imprecise_dtypes=True).then_inc(s_iota, 1)
            pool.wait_ge(s_zero, 5)
            nc.gpsimd.affine_select(out=C["ident"][:, :], in_=C["ident"][:, :], compare_op=ALU.not_equal, fill=1.0,
                                    base=0, pattern=[[-1, P]], channel_multiplier=1).then_inc(s_ident, 1)
            nc.gpsimd.affine_select(out=C["tri"][:, :], in_=C["tri"][:, :], compare_op=ALU.is_ge, fill=1.0,
                                    base=0, pattern=[[-1, P]], channel_multiplier=1).then_inc(s_ident, 1)
            pool.wait_ge(s_idok, 1)
            with pool.Fori(0, HB) as pair:
                for u in range(2):
                    pool.wait_ge(s_bT, 2 * pair + 1 + u)
                    nc.gpsimd.tensor_copy(idc[u][:, :], ids_ok[:, bass.ds(2 * pair + u, 1), :].rearrange("p a j -> p (a j)")).then_inc(s_idc, 1)
                    pool.wait_ge(s_idc, 2 * pair + 1 + u)
                    pool.sem_inc(s_apart, 1)
                    for j in range(4):
                        nc.gpsimd.indirect_dma_start(basin[u][:, j, :], None, I["L0_txt_basin_coords"],
                                                     bass.IndirectOffsetOnAxis(ap=idc[u][:, j:j + 1], axis=0)).then_inc(s_bas[u], 16)
                    if u == 1:
                        for v in range(2):
                            pool.wait_ge(s_msq, 2 * pair + 1 + v)
                            nc.gpsimd.tensor_tensor(rinv[v][:, :], msq[v][:, :], C["neghalf"][:, 0:4], ALU.pow).then_inc(s_rinv, 1)

        @block.scalar
        def _(act):
            act.dma_start(ids[:, :, :], I["x_txt"].rearrange("b (p j) -> p b j", j=4)).then_inc(s_ids, 16)

            def load(n):
                for dst, src in pieces[n][0]:
                    act.dma_start(dst(raw[n % 2]), src).then_inc(s_raw[n % 2], 16)
            load(0)
            load(1)
            act.wait_ge(s_zero, 1)
            act.dma_start(hbuf[:, T:TPAD, :], zeros[:, :].unsqueeze(1)[0:B, :, :].to_broadcast([B, TPAD - T, D])).then_inc(s_zout, 16)
            act.dma_start(scratch["xs"][DUMMY:ROWS, :].rearrange("(k p) d -> p k d", p=P),
                          zeros[:, :].unsqueeze(1).to_broadcast([P, NDUMMY, D])).then_inc(s_zout, 16)
            act.wait_ge(s_cls, 1)
            act.dma_start(hbuf[:, 0, :], cls_out[:, :]).then_inc(s_clsout, 16)
            for n, (_, (hi, lo), cols) in enumerate(pieces):
                act.wait_ge(s_raw[n % 2], raw_count[n + 1][n % 2])
                k = cols.stop - cols.start
                nc.scalar.activation(hi[:, cols], raw[n % 2][:, 0:k], ACT.Copy).then_inc(s_hi, 1)
                if n + 2 < len(pieces):
                    act.wait_ge(s_lo, n + 1)
                    load(n + 2)
            with act.Fori(0, HB) as pair:
                for u in range(2):
                    act.wait_ge(s_pst, 2 * pair + 3 + u)
                    dst = hbuf[bass.ds(2 * pair + u, 1), 1:1 + NPATCH, :].rearrange("b (g p) d -> p (b g) d", p=98)
                    act.dma_start(dst, pstage[u][:, :, :]).then_inc(s_pout[u], 16)
            with act.Fori(0, HB) as pair:
                for u in range(2):
                    act.wait_ge(s_bT, 2 * pair + 3 + u)
                    nc.scalar.activation(basinT[u][:, :, :], ps_tT[u][:, 0:2 * P].rearrange("p (j n) -> p j n", j=2), ACT.Copy).then_inc(s_bTc, 1)
                for u in range(2):
                    act.wait_ge(s_emb, 2 * pair + 1 + u)
                    for j in range(4):
                        last = nc.scalar.activation(sq[u][:, j, :], ps_emb[u][:, j % 2, j // 2 * D:(j // 2 + 1) * D],
                                                    ACT.Square, accum_out=ssq[u][:, j:j + 1])
                    last.then_inc(s_ssq, 1)
                for u in range(2):
                    act.wait_ge(s_tst, 2 * pair + 3 + u)
                    dst = hbuf[bass.ds(2 * pair + u, 1), 1 + NPATCH:T, :].rearrange("b (p j) d -> (b p) (j d)", j=4)
                    act.dma_start(dst, tstage[u][:, :, :].rearrange("p j d -> p (j d)")).then_inc(s_tout[u], 16)

        @block.vector
        def _(dve):
            dve.wait_ge(s_iota, 5)
            nc.vector.tensor_scalar(tmp_i[:, :], part_i[:, :], 3, None, ALU.arith_shift_right).then_inc(s_const, 1)
            dve.wait_ge(s_const, 1)
            nc.vector.tensor_copy(s_f[:, :], tmp_i[:, :]).then_inc(s_const, 1)
            dve.wait_ge(s_const, 2)
            nc.vector.tensor_scalar(C["maskf"][:, :, :], C["maskf"][:, :, :], s_f[:, 0:1], None, ALU.is_gt).then_inc(s_const, 1)
            for s in range(STEP):
                nc.vector.memset(drow[0:1, 0, :].rearrange("p (a s) -> p a s", s=STEP)[:, :, s:s + 1], DECAY ** s)
                last = nc.vector.memset(drow[0:1, 1, :].rearrange("p (a s) -> p a s", s=STEP)[:, :, s:s + 1],
                                        0.5 * WRITE * DECAY ** -(s + 1))
            nc.vector.memset(one1[:, :], 1.0).then_inc(s_drow, 1)
            dve.wait_ge(s_dcol, 1)
            nc.vector.tensor_copy(C["decay"][:, :], ps_tT[0][:, 0:2]).then_inc(s_const, 1)
            dve.wait_ge(s_ids, 16)
            nc.vector.tensor_copy(idsf[:, :, :], ids[:, :, :]).then_inc(s_const, 1)
            dve.wait_ge(s_const, 5)
            nc.vector.tensor_scalar(idneg[:, :, :], idsf[:, :, :], 0.0, float(VOCAB), ALU.is_lt, ALU.mult).then_inc(s_const, 1)
            dve.wait_ge(s_const, 6)
            nc.vector.tensor_tensor(idsf[:, :, :], idsf[:, :, :], idneg[:, :, :], ALU.add).then_inc(s_const, 1)
            dve.wait_ge(s_const, 7)
            nc.vector.tensor_scalar(ids_ok[:, :, :], idsf[:, :, :], 0.0, float(VOCAB - 1), ALU.max, ALU.min).then_inc(s_idok, 1)
            dve.wait_ge(s_small, 16 * 14)
            nc.vector.tensor_tensor(posb[:, :, :], posb[:, :, :], bias_bc[:, :].unsqueeze(1).to_broadcast([98, 2, D]), ALU.add).then_inc(s_posb, 1)
            nc.vector.tensor_tensor(cls_out[:, :], cls_row[:, :], pos0_row[:, :], ALU.add).then_inc(s_cls, 1)
            dve.wait_ge(s_projT, 1)
            nc.vector.tensor_copy(projT[:, :], ps_tT[1][:, 0:D]).then_inc(s_projTc, 1)
            for n, (_, (hi, lo), cols) in enumerate(pieces):
                dve.wait_ge(s_hi, n + 1)
                k = cols.stop - cols.start
                nc.vector.tensor_tensor(lo[:, cols], raw[n % 2][:, 0:k], hi[:, cols].bitcast(F32), ALU.subtract).then_inc(s_lo, 1)
            dve.wait_ge(s_posb, 1)
            for u in range(2):
                dve.sem_inc(s_pout[u], 16)
                dve.sem_inc(s_tout[u], 16)
            dve.sem_inc(s_pst, 2)
            dve.sem_inc(s_tst, 2)
            with dve.Fori(0, HB) as pair:
                for u in range(2):
                    dve.wait_ge(s_pmm, 2 * pair + 3 + u)
                    dve.wait_ge(s_pout[u], 16 * pair + 16)
                    nc.vector.tensor_tensor(pstage[u][:, :, :], ps_img[u][0:98, 0:2 * D].rearrange("p (g d) -> p g d", g=2),
                                            posb[:, :, :], ALU.add).then_inc(s_pst, 1)
            with dve.Fori(0, HB) as pair:
                for u in range(2):
                    dve.wait_ge(s_ssq, 2 * pair + 1 + u)
                    nc.vector.tensor_scalar(msq[u][:, :], ssq[u][:, :], 1.0 / D, RMS_EPS, ALU.mult, ALU.add).then_inc(s_msq, 1)
                for u in range(2):
                    dve.wait_ge(s_rinv, 2 * pair + 1 + u)
                    dve.wait_ge(s_tout[u], 16 * pair + 16)
                    for j in range(4):
                        last = nc.vector.scalar_tensor_tensor(
                            out=tstage[u][:, j, :], in0=ps_emb[u][:, j % 2, j // 2 * D:(j // 2 + 1) * D],
                            scalar=rinv[u][:, j:j + 1], in1=normw[:, :], op0=ALU.mult, op1=ALU.mult)
                    last.then_inc(s_tst, 1)

        @block.tensor
        def _(pe):
            pe.wait_ge(s_drow, 1)
            for k in range(2):
                last = nc.tensor.matmul(ps_tT[0][:, k:k + 1], drow[0:1, k, :], one1[:, :], start=True, stop=True)
            last.then_inc(s_dcol, 1)
            pe.wait_ge(s_small, 16 * 14)
            pe.wait_ge(s_ident, 2)
            nc.tensor.transpose(ps_tT[1][:, 0:P], projn[:, 0, :, :].rearrange("p q k -> p (q k)"), C["ident"][:, :])
            nc.tensor.transpose(ps_tT[1][:, P:D], projn[0:DB, 1, :, :].rearrange("p q k -> p (q k)"), C["ident"][0:DB, 0:DB]).then_inc(s_projT, 1)
            pe.sem_inc(s_pmm, 2)
            pe.wait_ge(s_tokw, 96)
            with pe.Fori(0, HB) as pair:
                for u in range(2):
                    pe.wait_ge(s_img[u], 96 * pair + 96)
                    pe.wait_ge(s_pst, 2 * pair + 1 + u)
                    for g in range(2):
                        for j in range(8):
                            px = img[u][:, 7 * g:7 * g + 7, :].rearrange("p n (w j) -> p n w j", j=PX)[:, :, :, j]
                            last = nc.tensor.matmul(ps_img[u][0:98, g * D:(g + 1) * D], px, tokw[:, j, :],
                                                    start=j == 0, stop=j == 7)
                    last.then_inc(s_pmm, 1)
            pe.wait_ge(s_const, 4)
            pe.wait_ge(s_projTc, 1)
            pe.sem_inc(s_bT, 2)
            with pe.Fori(0, HB) as pair:
                for u in range(2):
                    pe.wait_ge(s_bas[u], 64 * pair + 64)
                    for j in range(2):
                        last = nc.tensor.transpose(ps_tT[u][:, j * P:(j + 1) * P],
                                                   basin[u][:, 2 * j:2 * j + 2, :].rearrange("p j k -> p (j k)"), C["ident"][:, :])
                    last.then_inc(s_bT, 1)
                for u in range(2):
                    pe.wait_ge(s_bTc, 2 * pair + 1 + u)
                    pe.wait_ge(s_tst, 2 * pair + 1 + u)
                    for j in range(4):
                        last = nc.tensor.matmul(ps_emb[u][:, j % 2, j // 2 * D:(j // 2 + 1) * D], basinT[u][j % 2 * BASIN:(j % 2 + 1) * BASIN, j // 2, :],
                                                projT[j % 2 * BASIN:(j % 2 + 1) * BASIN, :],
                                                start=True, stop=True)
                    last.then_inc(s_emb, 1)
    nc.clear_and_free_semaphores(sems)
    nc.all_engine_barrier()


def attention_tables(nc, I, scratch, C):
    ctx = ExitStack()
    sems = []
    NF = TPAD // P
    TAIL = TPAD - NF * P
    BLK = [P] * NF + [TAIL]
    NB = NF + 1
    SPLIT = [(0, 368), (368, TPAD)]
    PER = 4 + NB
    with ctx:
        def sb(name, shape, dt=F32):
            return ctx.enter_context(nc.sbuf_tensor(name, shape, dt))

        def pb(name, shape, dt=F32):
            return ctx.enter_context(nc.psum_tensor(name, shape, dt))

        def sem(name):
            sems.append(nc.alloc_semaphore(name))
            return sems[-1]

        h0 = sb("h0", [P, NB, D])
        stats = sb("stats0", [P, NB, 6])
        mv = sb("mv0", [P, NB, 2])
        vare = sb("vare0", [P, NB])
        rstd = sb("rstd0", [P, NB])
        wk = sb("wk", [P, 4, D])
        wv = sb("wv", [P, 4, D])
        wq = sb("wq", [P, 4, D])
        wo = sb("wo", [P, 2, NH * DK])
        wgt = sb("wgt", [NH, D])
        wkT = [sb("wkT_a", [DA, 4, P]), sb("wkT_b", [DB, 4, P])]
        wvT = [sb("wvT_a", [DA, 4, P]), sb("wvT_b", [DB, 4, P])]
        woT = sb("woT", [P, 4, D])
        wgT = [sb("wgT_a", [DA, NH]), sb("wgT_b", [DB, NH])]
        x0T = [sb("x0T_a", [DA, TPAD]), sb("x0T_b", [DB, TPAD])]
        kvT = sb("kvT", [P, 2, TPAD])
        kqT_a = sb("kqT_a", [DA, TPAD, NH])
        kqT_b = sb("kqT_b", [P, 368, NH])
        rows = sb("rows", [P, NB, 2, D])
        gsc = sb("gsc", [P, NB, NH])
        gscale = sb("gscale", [P, NB, NH])
        ps = [pb(f"ps{n}", [P, 512]) for n in range(8)]

        s_w = sem("attn_weights_in")
        s_h = sem("h0_in")
        s_stat = sem("stats0_done")
        s_aggr = sem("aggr0_done")
        s_var = sem("var0_done")
        s_rstd = sem("rstd0_done")
        s_x0 = sem("x0_done")
        s_wTp = sem("weight_transposed")
        s_wT = sem("weightT_copied")
        s_x0Tp = sem("x0_transposed")
        s_x0T = sem("x0T_copied")
        s_gl = sem("gate_logits")
        s_gt = sem("gate_tanh")
        s_gs = sem("gate_scale")
        s_kv = sem("kv_product")
        s_kvc = sem("kv_copied")
        s_bank = sem("head_bank_filled")
        s_evA = sem("bank_copied_act")
        s_evD = sem("bank_copied_dve")
        s_row = sem("rows_stored")
        s_tab = sem("kqT_stored")
        block = ctx.enter_context(nc.Block())
        ident = C["ident"]
        hb = scratch["hbuf"]

        @block.sync
        def _(sp):
            sp.dma_start(h0[:, 0:NF, :], hb[0, 0:NF * P, :].rearrange("(k p) d -> p k d", p=P)).then_inc(s_h, 16)
            sp.dma_start(h0[0:TAIL, NF, :], hb[0, NF * P:TPAD, :]).then_inc(s_h, 16)
            for w, name in ((wk, "L0_attn_w_key"), (wv, "L0_attn_w_value"), (wq, "L0_attn_w_query")):
                sp.dma_start(w[:, :, :], I[name].rearrange("(m p) d -> p m d", p=P)).then_inc(s_w, 16)
            sp.dma_start(wo[:, 0, :], I["L0_attn_w_out"][0:P, :]).then_inc(s_w, 16)
            sp.dma_start(wo[0:DB, 1, :], I["L0_attn_w_out"][P:D, :]).then_inc(s_w, 16)
            sp.dma_start(wgt[:, :], I["L0_attn_w_gate"]).then_inc(s_w, 16)
            for h in range(NH):
                sp.wait_ge(s_evA, PER // 2 * (h + 1))
                sp.wait_ge(s_evD, PER // 2 * (h + 1))
                for t, name in enumerate(("kq", "vo")):
                    dst = scratch[name][:, h * D:(h + 1) * D]
                    sp.dma_start(dst[0:NF * P, :].rearrange("(k p) d -> p k d", p=P), rows[:, 0:NF, t, :]).then_inc(s_row, 16)
                    sp.dma_start(dst[NF * P:TPAD, :], rows[0:TAIL, NF, t, :]).then_inc(s_row, 16)
            c0 = SPLIT[0][1] // STEP
            dst = scratch["kqT"].rearrange("c d x -> d c x")
            sp.dma_start(dst[0:DA, :, :], kqT_a[:, :, :].rearrange("d (c s) h -> d c (s h)", s=STEP)).then_inc(s_tab, 16)
            sp.dma_start(dst[DA:D, 0:c0, :], kqT_b[0:DB, :, :].rearrange("d (c s) h -> d c (s h)", s=STEP)).then_inc(s_tab, 16)
            sp.dma_start(dst[DA:D, c0:NCH, :], kqT_b[DB:P, 0:TPAD - c0 * STEP, :].rearrange("d (c s) h -> d c (s h)", s=STEP)).then_inc(s_tab, 16)
            sp.wait_ge(s_tab, 48)
            sp.wait_ge(s_row, 64 * NH)

        @block.gpsimd
        def _(pool):
            pool.wait_ge(s_var, 1)
            nc.gpsimd.tensor_tensor(rstd[:, :], vare[:, :], C["neghalf"][:, 0:NB], ALU.pow).then_inc(s_rstd, 1)

        @block.scalar
        def _(act):
            act.wait_ge(s_wTp, 1)
            for n, wT in enumerate((wkT[0], wkT[1], wvT[0], wvT[1])):
                r = DA if n % 2 == 0 else DB
                nc.scalar.activation(wT[:, :, :], ps[n][0:r, :].rearrange("p (m n) -> p m n", m=4), ACT.Copy).then_inc(s_wT, 1)
            for n in range(2):
                nc.scalar.activation(woT[:, 2 * n:2 * n + 2, :], ps[4 + n][:, 0:2 * D].rearrange("p (m n) -> p m n", m=2), ACT.Copy).then_inc(s_wT, 1)
            nc.scalar.activation(wgT[0][:, :], ps[6][0:DA, 0:NH], ACT.Copy).then_inc(s_wT, 1)
            nc.scalar.activation(wgT[1][:, :], ps[6][0:DB, NH:2 * NH], ACT.Copy).then_inc(s_wT, 1)
            act.wait_ge(s_gl, 1)
            nc.scalar.activation(gsc[:, 0:NF, :], ps[4][:, 0:NF * NH].rearrange("p (k h) -> p k h", h=NH), ACT.Tanh, scale=0.5).then_inc(s_gt, 1)
            nc.scalar.activation(gsc[0:TAIL, NF, :], ps[4][0:TAIL, NF * NH:NB * NH], ACT.Tanh, scale=0.5).then_inc(s_gt, 1)
            act.wait_ge(s_gs, 2)
            for m in range(4):
                for t in range(2):
                    for n, (a, b) in enumerate(SPLIT):
                        act.wait_ge(s_kv, 4 * m + 2 * t + n + 1)
                        if m:
                            act.wait_ge(s_bank, 2 * PER * m)
                        nc.scalar.activation(kvT[:, t, a:b], ps[2 * t + n][:, 0:b - a], ACT.Copy).then_inc(s_kvc, 1)
                for h in (2 * m, 2 * m + 1):
                    for j in range(0, PER, 2):
                        bank = ps[4 + (PER * h + j) % 4]
                        act.wait_ge(s_bank, PER * h + j + 1)
                        if j < 4:
                            a, b = SPLIT[j // 2]
                            nc.scalar.activation(kqT_a[:, a:b, h], bank[:, 0:b - a], ACT.Copy).then_inc(s_evA, 1)
                        else:
                            k, n = j - 4, BLK[j - 4]
                            if h:
                                act.wait_ge(s_row, 64 * h)
                            nc.scalar.activation(rows[0:n, k, 0, :], bank[0:n, 0:D], ACT.Copy)
                            nc.scalar.activation(rows[0:n, k, 1, :], bank[0:n, D:2 * D], ACT.Copy, scale=gscale[0:n, k, h:h + 1]).then_inc(s_evA, 1)

        @block.vector
        def _(dve):
            dve.wait_ge(s_h, 32)
            for k, n in enumerate(BLK):
                last = nc.vector.bn_stats(stats[0:n, k, :], h0[0:n, k, :])
            last.then_inc(s_stat, 1)
            dve.wait_ge(s_stat, 1)
            nc.vector.memset(mv[:, :, :], 1.0).then_inc(s_aggr, 1)
            dve.wait_ge(s_aggr, 1)
            for k, n in enumerate(BLK):
                last = nc.vector.bn_aggr(mv[0:n, k, :], stats[0:n, k, :])
            last.then_inc(s_aggr, 1)
            dve.wait_ge(s_aggr, 2)
            nc.vector.tensor_scalar(vare[:, :], mv[:, :, 1], LN_EPS, None, ALU.add).then_inc(s_var, 1)
            dve.wait_ge(s_rstd, 1)
            for k, n in enumerate(BLK):
                last = nc.vector.tensor_scalar(h0[0:n, k, :], h0[0:n, k, :], mv[0:n, k, 0:1], rstd[0:n, k:k + 1],
                                               ALU.subtract, ALU.mult)
            last.then_inc(s_x0, 1)
            dve.wait_ge(s_x0Tp, 1)
            for half, r in enumerate((DA, DB)):
                nc.vector.tensor_copy(x0T[half][:, 0:512], ps[2 * half][0:r, 0:512])
                last = nc.vector.tensor_copy(x0T[half][:, 512:TPAD], ps[2 * half + 1][0:r, 0:TPAD - 512])
            last.then_inc(s_x0T, 1)
            dve.wait_ge(s_gt, 2)
            nc.vector.tensor_scalar(gscale[:, 0:NF, :], gsc[:, 0:NF, :], 1.0, C["decay"][:, 1:2], ALU.add, ALU.mult).then_inc(s_gs, 1)
            nc.vector.tensor_scalar(gscale[0:TAIL, NF, :], gsc[0:TAIL, NF, :], 1.0, C["decay"][0:TAIL, 1:2], ALU.add, ALU.mult).then_inc(s_gs, 1)
            dve.wait_ge(s_gs, 2)
            for h in range(NH):
                for j in range(1, PER, 2):
                    bank = ps[4 + (PER * h + j) % 4]
                    dve.wait_ge(s_bank, PER * h + j + 1)
                    if j < 4:
                        a, b = SPLIT[j // 2]
                        r0 = DB * (j // 2)
                        nc.vector.tensor_copy(kqT_b[r0:r0 + DB, 0:b - a, h], bank[r0:r0 + DB, 0:b - a]).then_inc(s_evD, 1)
                    else:
                        k, n = j - 4, BLK[j - 4]
                        if h:
                            dve.wait_ge(s_row, 64 * h)
                        nc.vector.tensor_copy(rows[0:n, k, 0, :], bank[0:n, 0:D])
                        nc.vector.tensor_scalar(rows[0:n, k, 1, :], bank[0:n, D:2 * D], gscale[0:n, k, h:h + 1], None, ALU.mult).then_inc(s_evD, 1)

        @block.tensor
        def _(pe):
            pe.wait_ge(s_w, 96)
            for n, w in enumerate((wk, wv)):
                for m in range(4):
                    nc.tensor.transpose(ps[2 * n][:, m * P:(m + 1) * P], w[:, m, 0:DA], ident[:, :])
                    nc.tensor.transpose(ps[2 * n + 1][0:DB, m * P:(m + 1) * P], w[:, m, DA:D], ident[:, :])
            for m in range(4):
                bank, c = ps[4 + m // 2], m % 2 * D
                nc.tensor.transpose(bank[:, c:c + DA], wo[:, 0, m * P:(m + 1) * P], ident[:, :])
                nc.tensor.transpose(bank[:, c + DA:c + D], wo[0:DB, 1, m * P:(m + 1) * P], ident[0:DB, 0:DB])
            nc.tensor.transpose(ps[6][0:DA, 0:NH], wgt[:, 0:DA], ident[0:NH, 0:NH])
            nc.tensor.transpose(ps[6][0:DB, NH:2 * NH], wgt[:, DA:D], ident[0:NH, 0:NH]).then_inc(s_wTp, 1)
            pe.wait_ge(s_x0, 1)
            pe.wait_ge(s_wT, 8)
            for half, (a, b) in enumerate(((0, DA), (DA, D))):
                for k, n in enumerate(BLK):
                    bank, c = ps[2 * half + k // 4], k % 4 * P
                    last = nc.tensor.transpose(bank[0:b - a, c:c + n], h0[0:n, k, a:b], ident[0:n, 0:n])
            last.then_inc(s_x0Tp, 1)
            pe.wait_ge(s_x0T, 1)
            for k, n in enumerate(BLK):
                last = mm(nc, ps[4][0:n, k * NH:(k + 1) * NH], [(x0T[q][:, k * P:k * P + n], wgT[q][:, :]) for q in range(2)])
            last.then_inc(s_gl, 1)
            pe.wait_ge(s_gt, 2)
            for m in range(4):
                for t, wT in enumerate((wkT, wvT)):
                    for n, (a, b) in enumerate(SPLIT):
                        if m:
                            pe.wait_ge(s_kvc, 4 * m - 3 + 2 * t + n)
                        mm(nc, ps[2 * t + n][:, 0:b - a], [(wT[q][:, m, :], x0T[q][:, a:b]) for q in range(2)]).then_inc(s_kv, 1)
                pe.wait_ge(s_kvc, 4 * m + 4)
                for h in (2 * m, 2 * m + 1):
                    r = slice(h % 2 * DK, (h % 2 + 1) * DK)
                    for j in range(PER):
                        n = PER * h + j
                        bank = ps[4 + n % 4]
                        if n >= 4:
                            pe.wait_ge(s_evA if j % 2 == 0 else s_evD, (n - 4) // 2 + 1)
                        if j < 4:
                            a, b = SPLIT[j // 2]
                            if j % 2 == 0:
                                out, wcols = bank[:, 0:b - a], slice(0, DA)
                            else:
                                out, wcols = bank[DB * (j // 2):DB * (j // 2) + DB, 0:b - a], slice(DA, D)
                            last = nc.tensor.matmul(out, wq[r, m, wcols], kvT[r, 0, a:b], start=True, stop=True)
                        else:
                            k, s = j - 4, BLK[j - 4]
                            nc.tensor.matmul(bank[0:s, 0:D], kvT[r, 0, k * P:k * P + s], wq[r, m, :], start=True, stop=True)
                            last = nc.tensor.matmul(bank[0:s, D:2 * D], kvT[r, 1, k * P:k * P + s], woT[r, m, :], start=True, stop=True)
                        last.then_inc(s_bank, 1)
    nc.clear_and_free_semaphores(sems)
    nc.all_engine_barrier()


RING = 3


def done(c):
    return c + 1 + RING


def free(c):
    return c + 1


def pipeline(eng, n, ring, stages, peel=1):
    for s in range(ring * peel):
        for lag, body in stages:
            if s >= lag:
                body(s - lag, (s - lag) % ring, (s - lag) // ring)
    with eng.Fori(peel, n // ring) as i:
        for u in range(ring):
            for lag, body in stages:
                body(ring * i + u - lag, (u - lag) % ring, i + (u - lag) // ring)
    for s in range(n, n + max(lag for lag, _ in stages)):
        for lag, body in stages:
            if s - lag < n:
                body(s - lag, (s - lag) % ring, (s - lag) // ring)


def tokens(nc, I, scratch, C, W):
    ctx = ExitStack()
    sems = []
    with ctx:
        def sb(name, shape, dt=F32):
            return ctx.enter_context(nc.sbuf_tensor(name, shape, dt))

        def ring(name, shape, dt=F32):
            return [sb(f"{name}_{n}", shape, dt) for n in range(RING)]

        def pb(name, shape, dt=F32):
            return ctx.enter_context(nc.psum_tensor(name, shape, dt))

        def sem(name):
            sems.append(nc.alloc_semaphore(name))
            return sems[-1]

        h = ring("h", [P, 2, D])
        x1 = ring("x1", [P, 2, D])
        hx = ring("hx", [P, 2, D])
        h2 = ring("h2s", [P, 2, D])
        x2 = ring("x2", [P, 2, D])
        st1 = ring("st1", [P, 2, 6])
        mv1 = ring("mv1", [P, 2, 2])
        ve1 = ring("ve1", [P, 2])
        rs1 = ring("rs1", [P, 2])
        st2 = ring("st2", [P, 2, 6])
        mv2 = ring("mv2", [P, 2, 2])
        ve2 = ring("ve2", [P, 2])
        rs2 = ring("rs2", [P, 2])
        x1a = ring("x1a", [DA, 2 * P])
        x1b = ring("x1b", [DB, 2 * P])
        x2a = ring("x2a", [DA, 2 * P])
        x2b = ring("x2b", [DB, 2 * P])
        kqa = ring("kqa", [DA, P])
        kqb = ring("kqb", [DB, P])
        kq = ring("kqr", [P, D])
        vo = ring("vor", [P, D])
        sc = ring("sc", [P, 2 * P])
        Ma = ring("Ma", [DA, D])
        Mb = ring("Mb", [DB, D])
        Msa = ring("Msa", [DA, D])
        Msb = ring("Msb", [DB, D])
        lg = ring("lg", [P, 2, NE + 1])
        mx = ring("mx", [P, 2, 8])
        ix = ring("ix", [P, 2, 8], U32)
        ixf = ring("ixf", [P, 2, 2])
        oh = ring("oh", [P, 4, NE])
        ohs = ring("ohs", [P, 2, NE], BF16)
        ld = ring("ld", [P, NE], BF16)
        pb8 = ring("pb8", [P, 2, NE])
        prod = ring("prod", [P, 4, NE])
        slf = ring("slf", [P, 4])
        slu = ring("slu", [P, 4], U32)

        ps_x1, ps_sc, ps_o, ps_m, ps_x2, ps_lg, ps_pos = [pb(n, [P, 512]) for n in
                                                          ("ps_x1", "ps_sc", "ps_o", "ps_m", "ps_x2", "ps_lg", "ps_pos")]

        s_h_in = [sem(f"h_in{n}") for n in range(RING)]
        s_k_in = [sem(f"k_in{n}") for n in range(RING)]
        s_h2_out = [sem(f"h2_out{n}") for n in range(RING)]
        s_x2T_out = [sem(f"x2T_out{n}") for n in range(RING)]
        s_scat = [sem(f"scattered{n}") for n in range(RING)]
        s_init = sem("init")
        s_apart_dve, s_apart_pool = sem("apart_dve"), sem("apart_pool")
        s_st1, s_ag1, s_ve1, s_rs1 = sem("stats1"), sem("aggr1"), sem("var1"), sem("rstd1")
        s_x1, s_hx = sem("x1"), sem("hx")
        s_x1Tp, s_x1T = sem("x1T_product"), sem("x1T")
        s_scp, s_sc = sem("score_product"), sem("scores")
        s_om = sem("attention_product")
        s_Ms, s_M = sem("M_scaled"), sem("M")
        s_h2 = sem("h2_done")
        s_st2, s_ag2, s_ve2, s_rs2 = sem("stats2"), sem("aggr2"), sem("var2"), sem("rstd2")
        s_x2 = sem("x2_done")
        s_x2Tp, s_x2T = sem("x2T_product"), sem("x2T_copied")
        s_lgp, s_lg = sem("logit_product"), sem("logits")
        s_mx, s_ix, s_ixf = sem("top8"), sem("top8_index"), sem("index_float")
        s_oh, s_ohs = sem("onehot"), sem("onehot_sum")
        s_ld = sem("load_done")
        s_posp, s_pb8, s_prod, s_slf, s_slot = sem("pos_product"), sem("pos_base"), sem("pos_chosen"), sem("slot_float"), sem("slot")
        block = ctx.enter_context(nc.Block())
        ident = C["ident"]
        c16 = DECAY ** STEP
        hb = scratch["hbuf"]

        def at(dram, c):
            return dram[bass.ds(c, 1)].rearrange("c a b -> (c a) b")

        @block.sync
        def _(sp):
            def loads(c, b, r):
                sp.wait_ge(s_hx, free(c))
                for half in range(2):
                    src = hb[half * HB:(half + 1) * HB, bass.ds(c * STEP, STEP), :]
                    sp.dma_start(h[b][:, half, :], src).then_inc(s_h_in[b], 16)
                sp.wait_ge(s_om, free(c))
                sp.dma_start(kqa[b][:, :], at(scratch["kqT"], c)[0:DA, :]).then_inc(s_k_in[b], 16)
                sp.dma_start(kqb[b][:, :], at(scratch["kqT"], c)[DA:D, :]).then_inc(s_k_in[b], 16)
                for dst, name in ((kq, "kq"), (vo, "vo")):
                    src = scratch[name][bass.ds(c * STEP, STEP), :].rearrange("s (h d) -> (s h) d", h=NH)
                    sp.dma_start(dst[b][:, :], src).then_inc(s_k_in[b], 16)
            pipeline(sp, NCH, RING, [(0, loads)])

        @block.gpsimd
        def _(pool):
            for s in (s_rs1, s_rs2, s_Ms):
                pool.sem_inc(s, RING)
            pool.wait_ge(s_init, 1)

            def norm1(c, b, r):
                pool.wait_ge(s_ve1, done(c))
                nc.gpsimd.tensor_tensor(rs1[b][:, :], ve1[b][:, :], C["neghalf"][:, 0:2], ALU.pow).then_inc(s_rs1, 1)

            def decay_state(c, b, r):
                pool.wait_ge(s_M, done(c - 1))
                pool.sem_inc(s_apart_pool, 1)
                nc.gpsimd.tensor_scalar(Msa[b][:, :], Ma[b][:, :], c16, 0.0, ALU.mult, ALU.add)
                nc.gpsimd.tensor_scalar(Msb[b][:, :], Mb[b][:, :], c16, 0.0, ALU.mult, ALU.add).then_inc(s_Ms, 1)

            def norm2(c, b, r):
                pool.wait_ge(s_ve2, done(c))
                nc.gpsimd.tensor_tensor(rs2[b][:, :], ve2[b][:, :], C["neghalf"][:, 0:2], ALU.pow).then_inc(s_rs2, 1)

            def scatter(c, b, r):
                pool.wait_ge(s_slot, done(c))
                pool.sem_inc(s_apart_pool, 1)
                for j in range(4):
                    nc.gpsimd.indirect_dma_start(scratch["xs"], bass.IndirectOffsetOnAxis(ap=slu[b][:, j:j + 1], axis=0),
                                                 x2[b][:, j // 2, :], None).then_inc(s_scat[b], 16)
            pipeline(pool, NCH, RING, [(1, decay_state), (0, norm1), (1, norm2), (2, scatter)])
            for b in range(RING):
                pool.wait_ge(s_scat[b], 64 * (NCH // RING))

        @block.scalar
        def _(act):
            for s in (s_x1T, s_x2T):
                act.sem_inc(s, RING)
            for b in range(RING):
                act.sem_inc(s_h2_out[b], 16)
                act.sem_inc(s_x2T_out[b], 32)

            def store_h2(c, b, r):
                act.wait_ge(s_h2, done(c))
                act.dma_start(at(scratch["h2"], c), h2[b][:, :, :].rearrange("p a d -> p (a d)")).then_inc(s_h2_out[b], 16)

            def x2_columns(c, b, r):
                act.wait_ge(s_x2Tp, done(c))
                act.wait_ge(s_x2T_out[b], 32 * r + 32)
                nc.scalar.activation(x2a[b][:, :], ps_x2[:, 0:2 * P], ACT.Copy)
                nc.scalar.activation(x2b[b][:, :], ps_x2[0:DB, 2 * P:4 * P], ACT.Copy).then_inc(s_x2T, 1)
                act.wait_ge(s_x2T, done(c))
                act.dma_start(at(scratch["x2T"], c)[0:DA, :], x2a[b][:, :]).then_inc(s_x2T_out[b], 16)
                act.dma_start(at(scratch["x2T"], c)[DA:D, :], x2b[b][:, :]).then_inc(s_x2T_out[b], 16)

            def x1_columns(c, b, r):
                act.wait_ge(s_x1Tp, done(c))
                act.wait_ge(s_om, free(c))
                nc.scalar.activation(x1a[b][:, :], ps_x1[:, 0:2 * P], ACT.Copy)
                nc.scalar.activation(x1b[b][:, :], ps_x1[0:DB, 2 * P:4 * P], ACT.Copy).then_inc(s_x1T, 1)
            pipeline(act, NCH, RING, [(2, x2_columns), (2, store_h2), (0, x1_columns)])
            for b in range(RING):
                act.wait_ge(s_h2_out[b], 16 * (NCH // RING) + 16)
                act.wait_ge(s_x2T_out[b], 32 * (NCH // RING) + 32)

        @block.vector
        def _(dve):
            nc.vector.memset(Ma[0][:, :], 0.0)
            nc.vector.memset(Mb[0][:, :], 0.0)
            nc.vector.memset(ld[0][:, :], 0.0).then_inc(s_init, 1)
            dve.wait_ge(s_init, 1)
            for s in (s_st1, s_ag1, s_ve1, s_x1, s_hx, s_sc, s_M, s_h2, s_st2, s_ag2, s_ve2, s_x2, s_lg, s_mx, s_ix,
                      s_ixf, s_oh, s_ohs, s_ld, s_pb8, s_prod, s_slf, s_slot):
                dve.sem_inc(s, RING)

            def stats1(c, b, r):
                dve.wait_ge(s_h_in[b], 32 * r + 32)
                nc.vector.bn_stats(st1[b][:, 0, :], h[b][:, 0, :])
                nc.vector.bn_stats(st1[b][:, 1, :], h[b][:, 1, :]).then_inc(s_st1, 1)
                dve.wait_ge(s_st1, done(c))
                dve.sem_inc(s_apart_dve, 1)
                nc.vector.bn_aggr(mv1[b][:, 0, :], st1[b][:, 0, :])
                nc.vector.bn_aggr(mv1[b][:, 1, :], st1[b][:, 1, :]).then_inc(s_ag1, 1)
                dve.wait_ge(s_ag1, done(c))
                nc.vector.tensor_scalar(ve1[b][:, :], mv1[b][:, :, 1], LN_EPS, None, ALU.add).then_inc(s_ve1, 1)

            def normed1(c, b, r):
                dve.wait_ge(s_rs1, done(c))
                for half in range(2):
                    last = nc.vector.tensor_scalar(x1[b][:, half, :], h[b][:, half, :], mv1[b][:, half, 0:1],
                                                   rs1[b][:, half:half + 1], ALU.subtract, ALU.mult)
                last.then_inc(s_x1, 1)
                dve.wait_ge(s_x1, done(c))
                nc.vector.tensor_tensor(hx[b][:, :, :], h[b][:, :, :], x1[b][:, :, :], ALU.add).then_inc(s_hx, 1)

            def masked(c, b, r):
                dve.wait_ge(s_scp, done(c))
                nc.vector.tensor_tensor(sc[b][:, :], ps_sc[:, 0:2 * P], C["maskf"][:, :, :].rearrange("p b s -> p (b s)"),
                                        ALU.mult).then_inc(s_sc, 1)

            def residual(c, b, r):
                dve.wait_ge(s_om, done(c))
                dve.wait_ge(s_Ms, done(c))
                n = (b + 1) % RING
                nc.vector.scalar_tensor_tensor(out=Ma[n][:, :], in0=ps_m[:, 0:D], scalar=c16, in1=Msa[b][:, :],
                                               op0=ALU.mult, op1=ALU.add)
                nc.vector.scalar_tensor_tensor(out=Mb[n][:, :], in0=ps_m[0:DB, D:2 * D], scalar=c16, in1=Msb[b][:, :],
                                               op0=ALU.mult, op1=ALU.add).then_inc(s_M, 1)
                dve.wait_ge(s_h2_out[b], 16 * r + 16)
                nc.vector.scalar_tensor_tensor(out=h2[b][:, :, :], in0=ps_o[:, 0:2 * D].rearrange("p (a d) -> p a d", a=2),
                                               scalar=C["decay"][:, 0:1], in1=hx[b][:, :, :],
                                               op0=ALU.mult, op1=ALU.add).then_inc(s_h2, 1)
                dve.wait_ge(s_h2, done(c))
                nc.vector.bn_stats(st2[b][:, 0, :], h2[b][:, 0, :])
                nc.vector.bn_stats(st2[b][:, 1, :], h2[b][:, 1, :]).then_inc(s_st2, 1)
                dve.wait_ge(s_st2, done(c))
                dve.sem_inc(s_apart_dve, 1)
                nc.vector.bn_aggr(mv2[b][:, 0, :], st2[b][:, 0, :])
                nc.vector.bn_aggr(mv2[b][:, 1, :], st2[b][:, 1, :]).then_inc(s_ag2, 1)
                dve.wait_ge(s_ag2, done(c))
                nc.vector.tensor_scalar(ve2[b][:, :], mv2[b][:, :, 1], LN_EPS, None, ALU.add).then_inc(s_ve2, 1)

            def choose(c, b, r):
                dve.wait_ge(s_lgp, done(c))
                nc.vector.tensor_copy(lg[b][:, :, :], ps_lg[:, 0:2 * (NE + 1)].rearrange("p (a e) -> p a e", a=2)).then_inc(s_lg, 1)
                dve.wait_ge(s_lg, done(c))
                dve.sem_inc(s_apart_dve, 1)
                nc.vector.max(mx[b][:, 0, :], lg[b][:, 0, 0:NE])
                nc.vector.max(mx[b][:, 1, :], lg[b][:, 1, 0:NE]).then_inc(s_mx, 1)
                dve.wait_ge(s_mx, done(c))
                dve.sem_inc(s_apart_dve, 1)
                nc.vector.max_index(ix[b][:, 0, :], mx[b][:, 0, :], lg[b][:, 0, 0:NE])
                nc.vector.max_index(ix[b][:, 1, :], mx[b][:, 1, :], lg[b][:, 1, 0:NE]).then_inc(s_ix, 1)
                nc.vector.tensor_tensor(C["pre"][:, bass.ds(2 * c, 2), 0:1], mx[b][:, :, 0:1], mx[b][:, :, 1:2], ALU.subtract)
                nc.vector.tensor_scalar(C["pre"][:, bass.ds(2 * c, 2), 1:2], lg[b][:, :, NE:NE + 1], C["sgb"][:, 0:1], None, ALU.add)
                dve.wait_ge(s_ix, done(c))
                nc.vector.tensor_copy(ixf[b][:, :, :], ix[b][:, :, 0:2]).then_inc(s_ixf, 1)
                dve.wait_ge(s_ixf, done(c))
                nc.vector.tensor_tensor(oh[b][:, :, :], C["iota8"][:, :].unsqueeze(1).to_broadcast([P, 4, NE]),
                                        ixf[b][:, :, :].rearrange("p a (k o) -> p (a k) o", o=1).to_broadcast([P, 4, NE]),
                                        ALU.is_equal).then_inc(s_oh, 1)
                dve.wait_ge(s_oh, done(c))
                pair = oh[b][:, :, :].rearrange("p (a k) e -> p a k e", k=2)
                nc.vector.tensor_tensor(ohs[b][:, :, :], pair[:, :, 0, :], pair[:, :, 1, :], ALU.add).then_inc(s_ohs, 1)

            def normed2(c, b, r):
                dve.wait_ge(s_rs2, done(c))
                if not (isinstance(r, int) and r == 0):
                    dve.wait_ge(s_scat[b], 64 * r)
                for half in range(2):
                    last = nc.vector.tensor_scalar(x2[b][:, half, :], h2[b][:, half, :], mv2[b][:, half, 0:1],
                                                   rs2[b][:, half:half + 1], ALU.subtract, ALU.mult)
                last.then_inc(s_x2, 1)

            def slots(c, b, r):
                n = (b + 1) % RING
                dve.wait_ge(s_ohs, done(c))
                nc.vector.tensor_tensor(pb8[b][:, 0, :], ohs[b][:, 0, :], ohs[b][:, 1, :], ALU.add).then_inc(s_ld, 1)
                dve.wait_ge(s_ld, 2 * c + RING + 1)
                nc.vector.tensor_tensor(ld[n][:, :], ld[b][:, :], pb8[b][:, 0, :], ALU.add).then_inc(s_ld, 1)
                dve.wait_ge(s_ld, 2 * c + RING + 2)
                dve.wait_ge(s_posp, done(c))
                nc.vector.tensor_tensor(pb8[b][:, :, :], ps_pos[:, 0:2 * NE].rearrange("p (a e) -> p a e", a=2),
                                        C["ebase"][:, :].unsqueeze(1).to_broadcast([P, 2, NE]), ALU.add).then_inc(s_pb8, 1)
                dve.wait_ge(s_pb8, done(c))
                nc.vector.tensor_tensor(prod[b][:, :, :].rearrange("p (a k) e -> p a k e", k=2),
                                        oh[b][:, :, :].rearrange("p (a k) e -> p a k e", k=2),
                                        pb8[b][:, :, :].unsqueeze(2).to_broadcast([P, 2, 2, NE]), ALU.mult).then_inc(s_prod, 1)
                dve.wait_ge(s_prod, done(c))
                nc.vector.reduce_sum(slf[b][:, :], prod[b][:, :, :], AX.X).then_inc(s_slf, 1)
                dve.wait_ge(s_slf, done(c))
                nc.vector.tensor_copy(C["slots"][:, bass.ds(c, 1), :].rearrange("p c k -> p (c k)"), slf[b][:, :])
                nc.vector.tensor_copy(slu[b][:, :], slf[b][:, :]).then_inc(s_slot, 1)
            pipeline(dve, NCH, RING, [(0, stats1), (1, masked), (0, normed1), (1, residual), (2, choose), (1, normed2), (2, slots)], peel=2)
            dve.wait_ge(s_ld, 2 * NCH + RING)
            nc.vector.tensor_copy(C["load"][:, :], ld[NCH % RING][:, :])

        @block.tensor
        def _(pe):
            for s in (s_x1Tp, s_scp, s_om, s_x2Tp, s_lgp, s_posp):
                pe.sem_inc(s, RING)
            pe.wait_ge(s_init, 1)

            def columns(out, x, s):
                for half in range(2):
                    nc.tensor.transpose(out[:, half * P:(half + 1) * P], x[:, half, 0:DA], ident[:, :])
                    last = nc.tensor.transpose(out[0:DB, (2 + half) * P:(3 + half) * P], x[:, half, DA:D], ident[:, :])
                last.then_inc(s, 1)

            def x1_transposes(c, b, r):
                pe.wait_ge(s_x1, done(c))
                pe.wait_ge(s_x1T, done(c - 1))
                columns(ps_x1, x1[b], s_x1Tp)

            def scores(c, b, r):
                pe.wait_ge(s_x1T, done(c))
                pe.wait_ge(s_k_in[b], 64 * r + 64)
                pe.wait_ge(s_sc, done(c - 1))
                mm(nc, ps_sc[:, 0:2 * P], [(kqa[b][:, :], x1a[b][:, :]), (kqb[b][:, :], x1b[b][:, :])]).then_inc(s_scp, 1)

            def attend(c, b, r):
                pe.wait_ge(s_sc, done(c))
                pe.wait_ge(s_M, done(c - 1))
                pe.wait_ge(s_h2, done(c - 1))
                for half in range(2):
                    t = slice(half * P, (half + 1) * P)
                    mm(nc, ps_o[:, half * D:(half + 1) * D],
                       [(sc[b][:, t], vo[b][:, :]), (x1a[b][:, t], Ma[b][:, :]), (x1b[b][:, t], Mb[b][:, :])])
                mm(nc, ps_m[:, 0:D], [(kq[b][:, 0:DA], vo[b][:, :])])
                mm(nc, ps_m[0:DB, D:2 * D], [(kq[b][:, DA:D], vo[b][:, :])]).then_inc(s_om, 1)

            def x2_transposes(c, b, r):
                pe.wait_ge(s_x2, done(c))
                pe.wait_ge(s_x2T, done(c - 1))
                columns(ps_x2, x2[b], s_x2Tp)

            def logits(c, b, r):
                pe.wait_ge(s_x2T, done(c))
                pe.wait_ge(s_lg, done(c - 1))
                for half in range(2):
                    t = slice(half * P, (half + 1) * P)
                    last = mm(nc, ps_lg[:, half * (NE + 1):(half + 1) * (NE + 1)],
                              [(x2a[b][:, t], W["rw_a"][:, :]), (x2b[b][:, t], W["rw_b"][:, :])])
                last.then_inc(s_lgp, 1)

            def positions(c, b, r):
                pe.wait_ge(s_ohs, done(c))
                pe.wait_ge(s_ld, 2 * c + RING)
                pe.wait_ge(s_pb8, done(c - 1))
                mm(nc, ps_pos[:, 0:NE], [(C["tri"][:, :], ohs[b][:, 0, :]), (C["ones"][:, :], ld[b][:, :])])
                mm(nc, ps_pos[:, NE:2 * NE], [(C["tri"][:, :], ohs[b][:, 1, :]), (C["ones"][:, :], ohs[b][:, 0, :]),
                                              (C["ones"][:, :], ld[b][:, :])]).then_inc(s_posp, 1)
            pipeline(pe, NCH, RING, [(1, scores), (2, x2_transposes), (2, logits), (0, x1_transposes), (1, attend), (2, positions)])
    nc.clear_and_free_semaphores(sems)
    nc.all_engine_barrier()


TURN = 4


def tile_done(t):
    return t + 1 + TURN


def experts(nc, scratch, C, W):
    ctx = ExitStack()
    sems = []
    with ctx:
        def sb(name, shape, dt=F32):
            return ctx.enter_context(nc.sbuf_tensor(name, shape, dt))

        def pair(name, shape, dt=F32):
            return [sb(f"{name}_{n}", shape, dt) for n in range(2)]

        def pb(name, shape, dt=F32):
            return ctx.enter_context(nc.psum_tensor(name, shape, dt))

        def sem(name):
            sems.append(nc.alloc_semaphore(name))
            return sems[-1]

        zrow = sb("zrow", [P, D])
        cnt = sb("cnt", [P, NE])
        padf = sb("padf", [P, NE])
        padu = sb("padu", [P, NE], U32)
        nti = sb("nti", [P, NE], I32)
        ntf = sb("ntf", [P, NE])
        ends = sb("ends", [1, NE])
        tno = sb("tno", [1, NTILE])
        past = sb("past", [1, NE, NTILE])
        leap = sb("leap", [1, NE, NTILE])
        ef = sb("ef", [1, NTILE])
        rf = sb("rf", [1, NTILE])
        tile_e = sb("tile_e", [1, NTILE], I32)
        tile_row = sb("tile_row", [1, NTILE], I32)
        xt = [sb(f"xt_{n}", [P, 2 * P]) for n in range(TURN)]
        xh = pair("xh", [P, 2 * P], F32R)
        xl = pair("xl", [P, P], F32R)
        sg = pair("sg", [P, HE])
        hm = pair("hm", [P, 2 * P])
        hh = pair("hh", [P, 2 * P], F32R)
        hl = pair("hl", [P, P], F32R)
        y = [sb(f"y_{n}", [P, D]) for n in range(TURN)]
        ps_xT = [pb(f"ps_xT{n}", [P, 512]) for n in range(2)]
        ps_gu = [pb(f"ps_gu{n}", [P, 512]) for n in range(2)]
        ps_hT = [pb(f"ps_hT{n}", [P, 512]) for n in range(2)]
        ps_y = [pb(f"ps_y{n}", [P, 512]) for n in range(2)]

        s_cntp, s_step, s_iota, s_pad, s_padded, s_table = (sem(n) for n in
                                                            ("count_product", "table_step", "tile_numbers", "pad_rows", "padded", "table"))
        s_zrow = sem("zero_row")
        s_hm2, s_apart = sem("hidden_twice"), sem("apart_e")
        s_x_in = [sem(f"x_in{n}") for n in range(TURN)]
        s_y_out = [sem(f"y_out{n}") for n in range(TURN)]
        s_xT, s_xh, s_xl, s_gu, s_sg, s_hm = (sem(n) for n in ("xT", "x_lead", "x_rest", "gate_up", "silu", "hidden"))
        s_hT, s_hh, s_hl, s_yp, s_y = (sem(n) for n in ("hT", "h_lead", "h_rest", "down", "y_copied"))
        block = ctx.enter_context(nc.Block())
        ident = C["ident"]

        @block.gpsimd
        def _(pool):
            nc.gpsimd.iota(tno[:, :], pattern=[[1, NTILE]], base=0, channel_multiplier=0,
                           allow_small_or_imprecise_dtypes=True).then_inc(s_iota, 1)
            nc.gpsimd.memset(zrow[:, :], 0.0).then_inc(s_zrow, 1)
            pool.wait_ge(s_zrow, 1)
            pool.wait_ge(s_pad, 1)
            for e in range(NE):
                nc.gpsimd.indirect_dma_start(scratch["xs"], bass.IndirectOffsetOnAxis(ap=padu[:, e:e + 1], axis=0),
                                             zrow[:, :], None).then_inc(s_padded, 16)
            pool.wait_ge(s_padded, 16 * NE)
            pool.sem_inc(s_hm2, TURN)

            def twice(t, b, r):
                pool.wait_ge(s_hm, tile_done(t))
                pool.sem_inc(s_apart, 1)
                nc.gpsimd.tensor_copy(hm[b % 2][:, HE:2 * P], hm[b % 2][:, DA:HE]).then_inc(s_hm2, 1)
            pipeline(pool, NTILE, TURN, [(1, twice)])

        @block.sync
        def _(sp):
            for n in range(TURN):
                sp.sem_inc(s_y_out[n], 16)
            sp.wait_ge(s_padded, 16 * NE)
            sp.wait_ge(s_table, 1)

            def load(t, b, r):
                if not (isinstance(t, int) and t < TURN):
                    sp.wait_ge(s_xT, tile_done(t - TURN))
                row = sp.value_load(tile_row[0:1, bass.ds(t, 1)], min_val=0, max_val=ROWS - P)
                sp.dma_start(xt[b][:, 0:D], scratch["xs"][bass.ds(row, P), :]).then_inc(s_x_in[b], 16)
                sp.dma_start(xt[b][:, D:2 * P], scratch["xs"][bass.ds(row, P), DA:D]).then_inc(s_x_in[b], 16)

            def store(t, b, r):
                sp.wait_ge(s_y, tile_done(t))
                sp.dma_start(scratch["ys"][bass.ds(t * P, P), :], y[b][:, :]).then_inc(s_y_out[b], 16)
            pipeline(sp, NTILE, TURN, [(5, store), (0, load)], peel=2)
            for n in range(TURN):
                sp.wait_ge(s_y_out[n], 16 * (NTILE // TURN) + 16)

        @block.scalar
        def _(act):
            for s in (s_xh, s_sg, s_hh, s_y):
                act.sem_inc(s, TURN)

            def x_lead(t, b, r):
                act.wait_ge(s_xT, tile_done(t))
                act.wait_ge(s_gu, tile_done(t - 2))
                nc.scalar.activation(xh[b % 2][:, :], ps_xT[b % 2][:, 0:2 * P], ACT.Copy).then_inc(s_xh, 1)

            def silu(t, b, r):
                act.wait_ge(s_gu, tile_done(t))
                act.wait_ge(s_hm, tile_done(t - 2))
                nc.scalar.activation(sg[b % 2][:, :], ps_gu[b % 2][:, 0:HE], ACT.Silu).then_inc(s_sg, 1)

            def h_lead(t, b, r):
                act.wait_ge(s_hT, tile_done(t))
                act.wait_ge(s_yp, tile_done(t - 2))
                nc.scalar.activation(hh[b % 2][:, :], ps_hT[b % 2][:, 0:2 * P], ACT.Copy).then_inc(s_hh, 1)

            def y_copy(t, b, r):
                act.wait_ge(s_yp, tile_done(t))
                act.wait_ge(s_y_out[b], 16 * r + 16)
                nc.scalar.activation(y[b][:, :], ps_y[b % 2][:, 0:D], ACT.Copy).then_inc(s_y, 1)
            pipeline(act, NTILE, TURN, [(3, y_copy), (2, h_lead), (1, silu), (0, x_lead)])

        @block.vector
        def _(dve):
            n = [0]

            def step(ins):
                n[0] += 1
                ins.then_inc(s_step, 1)
                dve.wait_ge(s_step, n[0])
            dve.wait_ge(s_cntp, 1)
            step(nc.vector.tensor_copy(cnt[:, :], ps_xT[0][:, 0:NE]))
            step(nc.vector.tensor_tensor(padf[:, :], cnt[:, :], C["ebase"][:, :], ALU.add))
            nc.vector.tensor_scalar(padu[:, :], padf[:, :], C["partf"][:, 0:1], None, ALU.add).then_inc(s_pad, 1)
            step(nc.vector.tensor_scalar(nti[:, :], cnt[:, :], float(P - 1), None, ALU.add))
            step(nc.vector.tensor_scalar(nti[:, :], nti[:, :], P.bit_length() - 1, None, ALU.arith_shift_right))
            step(nc.vector.tensor_copy(ntf[:, :], nti[:, :]))
            step(nc.vector.tensor_copy(ends[:, :], ntf[0:1, :]))
            for e in range(1, NE):
                step(nc.vector.tensor_tensor(ends[:, e:e + 1], ends[:, e:e + 1], ends[:, e - 1:e], ALU.add))
            step(nc.vector.tensor_scalar(C["jump"][:, :], ntf[:, :], -float(P), float(CAP), ALU.mult, ALU.add))
            dve.wait_ge(s_iota, 1)
            step(nc.vector.tensor_tensor(past[:, :, :], tno[:, :].unsqueeze(1).to_broadcast([1, NE, NTILE]),
                                         ends[:, :].unsqueeze(2).to_broadcast([1, NE, NTILE]), ALU.is_ge))
            step(nc.vector.tensor_tensor(leap[:, :, :], past[:, :, :], C["jump"][0:1, :].unsqueeze(2).to_broadcast([1, NE, NTILE]), ALU.mult))
            step(nc.vector.reduce_sum(ef[:, :], past[:, :, :].rearrange("p e t -> p t e"), AX.X))
            step(nc.vector.reduce_sum(rf[:, :], leap[:, :, :].rearrange("p e t -> p t e"), AX.X))
            step(nc.vector.scalar_tensor_tensor(out=rf[:, :], in0=tno[:, :], scalar=float(P), in1=rf[:, :], op0=ALU.mult, op1=ALU.add))
            nc.vector.tensor_copy(tile_row[:, :], rf[:, :])
            nc.vector.tensor_scalar(tile_e[:, :], ef[:, :], float(NE - 1), None, ALU.min).then_inc(s_table, 1)
            for s in (s_xl, s_hm, s_hl):
                dve.sem_inc(s, TURN)

            def x_rest(t, b, r):
                dve.wait_ge(s_xh, tile_done(t))
                dve.wait_ge(s_gu, tile_done(t - 2))
                q = b % 2
                nc.vector.tensor_tensor(xl[q][:, :], ps_xT[q][:, 0:P], xh[q][:, 0:P].bitcast(F32), ALU.subtract)
                nc.vector.tensor_tensor(xh[q][DB:P, P:2 * P], ps_xT[q][DB:P, P:2 * P], xh[q][DB:P, P:2 * P].bitcast(F32),
                                        ALU.subtract).then_inc(s_xl, 1)

            def hidden(t, b, r):
                dve.wait_ge(s_sg, tile_done(t))
                dve.wait_ge(s_hT, tile_done(t - 2))
                nc.vector.tensor_tensor(hm[b % 2][:, 0:HE], sg[b % 2][:, :], ps_gu[b % 2][:, HE:2 * HE], ALU.mult).then_inc(s_hm, 1)

            def h_rest(t, b, r):
                dve.wait_ge(s_hh, tile_done(t))
                dve.wait_ge(s_yp, tile_done(t - 2))
                q = b % 2
                nc.vector.tensor_tensor(hl[q][:, :], ps_hT[q][:, 0:P], hh[q][:, 0:P].bitcast(F32), ALU.subtract)
                nc.vector.tensor_tensor(hh[q][DB:P, P:2 * P], ps_hT[q][DB:P, P:2 * P], hh[q][DB:P, P:2 * P].bitcast(F32),
                                        ALU.subtract).then_inc(s_hl, 1)
            pipeline(dve, NTILE, TURN, [(2, h_rest), (1, hidden), (0, x_rest)])

        @block.tensor
        def _(pe):
            mm(nc, ps_xT[0][:, 0:NE], [(C["ones"][:, :], C["load"][:, :])]).then_inc(s_cntp, 1)
            for s in (s_xT, s_gu, s_hT, s_yp):
                pe.sem_inc(s, TURN)
            pe.wait_ge(s_table, 1)

            def columns(out, x, s):
                nc.tensor.transpose(out[:, 0:P], x[:, 0:DA], ident[:, :])
                nc.tensor.transpose(out[:, P:2 * P], x[:, P:2 * P], ident[:, :]).then_inc(s, 1)

            def product(out, lead, rest, wa, wb, at, s):
                mm(nc, out, [(lead[:, 0:P], wa[0][:, at]), (rest[:, :], wa[0][:, at]), (lead[:, 0:P], wa[1][:, at]),
                             (lead[:, P:2 * P], wb[0][:, at]), (lead[:, P:2 * P], wb[1][:, at])]).then_inc(s, 1)

            def x_columns(t, b, r):
                pe.wait_ge(s_x_in[b], 32 * r + 32)
                pe.wait_ge(s_xl, tile_done(t - 2))
                columns(ps_xT[b % 2], xt[b], s_xT)

            def gate_up(t, b, r):
                e = pe.value_load(tile_e[0:1, bass.ds(t, 1)], min_val=0, max_val=NE - 1)
                pe.wait_ge(s_xl, tile_done(t))
                pe.wait_ge(s_hm, tile_done(t - 2))
                product(ps_gu[b % 2][:, 0:2 * HE], xh[b % 2], xl[b % 2], W["gu_a"], W["gu_b"], bass.ds(e * (2 * HE), 2 * HE), s_gu)

            def h_columns(t, b, r):
                pe.wait_ge(s_hm2, tile_done(t))
                pe.wait_ge(s_hl, tile_done(t - 2))
                columns(ps_hT[b % 2], hm[b % 2], s_hT)

            def down(t, b, r):
                e = pe.value_load(tile_e[0:1, bass.ds(t, 1)], min_val=0, max_val=NE - 1)
                pe.wait_ge(s_hl, tile_done(t))
                pe.wait_ge(s_y, tile_done(t - 2))
                product(ps_y[b % 2][:, 0:D], hh[b % 2], hl[b % 2], W["dn_a"], W["dn_b"], bass.ds(e * D, D), s_yp)
            pipeline(pe, NTILE, TURN, [(0, x_columns), (2, h_columns), (3, down), (1, gate_up)])
    nc.clear_and_free_semaphores(sems)
    nc.all_engine_barrier()


def combine(nc, scratch, C, W, out):
    ctx = ExitStack()
    sems = []
    MP = HS // (2 * P)
    with ctx:
        def sb(name, shape, dt=F32):
            return ctx.enter_context(nc.sbuf_tensor(name, shape, dt))

        def ring(name, shape, dt=F32):
            return [sb(f"{name}_{n}", shape, dt) for n in range(RING)]

        def pb(name, shape, dt=F32):
            return ctx.enter_context(nc.psum_tensor(name, shape, dt))

        def sem(name):
            sems.append(nc.alloc_semaphore(name))
            return sems[-1]

        th = sb("th", [P, 2 * NCH, 2])
        beta = sb("beta", [P, 2 * NCH])
        gg = sb("gg", [P, 2 * NCH, 2])
        xa = ring("xa", [P, 2 * P])
        xb = ring("xb", [P, 2 * P])
        h2 = ring("h2c", [P, 2, D])
        xah = ring("xah", [P, 2 * P], F32R)
        xal = ring("xal", [P, 2 * P], F32R)
        xbh = ring("xbh", [P, 2 * P], F32R)
        sg = [sb(f"sgs_{n}", [P, 4 * P]) for n in range(MP)]
        pm = [sb(f"pm_{n}", [P, 4 * P]) for n in range(MP)]
        ph = ring("ph", [P, MP, 4 * P], F32R)
        pl = ring("pl", [P, MP, 4 * P], F32R)
        over = sb("over", [P, NE, NCH * 4])
        gidx = sb("gidx", [P, NCH, 4], U32)
        slu = ring("sluc", [P, 4], U32)
        yy = ring("yy", [P, 4, D])
        oo = ring("oo", [P, 2, D])
        ps_g = [pb(f"ps_g{n}", [P, 512]) for n in range(MP)]
        ps_u = [pb(f"ps_u{n}", [P, 512]) for n in range(MP)]
        ps_d = pb("ps_d", [P, 512])

        s_th, s_gs, s_gates = sem("gate_tanhs"), sem("gate_step"), sem("gates_done")
        s_x_in = [sem(f"xc_in{n}") for n in range(RING)]
        s_h2_in = [sem(f"h2c_in{n}") for n in range(RING)]
        s_y_in = [sem(f"yc_in{n}") for n in range(RING)]
        s_o_out = [sem(f"o_out{n}") for n in range(RING)]
        s_over, s_gidx = sem("jumps_chosen"), sem("gather_rows")
        s_slu, s_apart = sem("slots_copied"), sem("apart_c")
        s_xh, s_xl = sem("xc_lead"), sem("xc_rest")
        s_g, s_sg, s_pm, s_ph, s_pl = (sem(n) for n in ("shared_gate_up", "shared_silu", "shared_hidden", "hidden_lead", "hidden_rest"))
        s_d, s_o1, s_o2, s_o = sem("shared_down"), sem("sum1"), sem("sum2"), sem("sum3")
        block = ctx.enter_context(nc.Block())

        def at(dram, c):
            return dram[bass.ds(c, 1)].rearrange("c a b -> (c a) b")

        def done3(c, m):
            return MP * c + m + 1 + MP

        @block.sync
        def _(sp):
            def loads(c, b, r):
                sp.wait_ge(s_xl, free(c))
                sp.dma_start(xa[b][:, :], at(scratch["x2T"], c)[0:DA, :]).then_inc(s_x_in[b], 16)
                for q in (0, DB):
                    sp.dma_start(xb[b][q:q + DB, :], at(scratch["x2T"], c)[DA:D, :]).then_inc(s_x_in[b], 16)
                sp.wait_ge(s_o1, free(c))
                sp.dma_start(h2[b][:, :, :].rearrange("p a d -> p (a d)"), at(scratch["h2"], c)).then_inc(s_h2_in[b], 16)
            pipeline(sp, NCH, RING, [(0, loads)])

        @block.gpsimd
        def _(pool):
            pool.sem_inc(s_slu, RING)
            pool.wait_ge(s_gidx, 1)

            def gather(c, b, r):
                pool.wait_ge(s_o, free(c))
                nc.gpsimd.tensor_copy(slu[b][:, :], gidx[:, bass.ds(c, 1), :].rearrange("p c k -> p (c k)")).then_inc(s_slu, 1)
                pool.wait_ge(s_slu, done(c))
                pool.sem_inc(s_apart, 1)
                for j in range(4):
                    nc.gpsimd.indirect_dma_start(yy[b][:, j, :], None, scratch["ys"],
                                                 bass.IndirectOffsetOnAxis(ap=slu[b][:, j:j + 1], axis=0)).then_inc(s_y_in[b], 16)
            pipeline(pool, NCH, RING, [(0, gather)])

        @block.scalar
        def _(act):
            nc.scalar.activation(th[:, :, :], C["pre"][:, :, :], ACT.Tanh, scale=0.5).then_inc(s_th, 1)
            act.sem_inc(s_xh, RING)
            for s in (s_sg, s_ph):
                act.sem_inc(s, MP)
            for b in range(RING):
                act.sem_inc(s_o_out[b], 32)

            def x_lead(c, b, r):
                act.wait_ge(s_x_in[b], 48 * r + 48)
                act.wait_ge(s_g, done3(c - RING, MP - 1) if not isinstance(c, int) or c >= RING else 1)
                nc.scalar.activation(xah[b][:, :], xa[b][:, :], ACT.Copy)
                nc.scalar.activation(xbh[b][:, :], xb[b][:, :], ACT.Copy).then_inc(s_xh, 1)

            def silus(c, b, r):
                for m in range(MP):
                    act.wait_ge(s_g, done3(c, m))
                    act.wait_ge(s_pm, done3(c - 1, m))
                    nc.scalar.activation(sg[m][:, :], ps_g[m][:, :], ACT.Silu).then_inc(s_sg, 1)
                    act.wait_ge(s_pm, done3(c, m))
                    if m == 0:
                        act.wait_ge(s_d, free(c))
                    nc.scalar.activation(ph[b][:, m, :], pm[m][:, :], ACT.Copy).then_inc(s_ph, 1)

            def store(c, b, r):
                act.wait_ge(s_o, done(c))
                for half in range(2):
                    if isinstance(c, int) and c == NCH - 1:
                        for k in range(HB):
                            act.dma_start(out[half * HB + k, c * STEP:T, :], oo[b][k * STEP:k * STEP + T - c * STEP, half, :]).then_inc(s_o_out[b], 16)
                    else:
                        act.dma_start(out[half * HB:(half + 1) * HB, bass.ds(c * STEP, STEP), :], oo[b][:, half, :]).then_inc(s_o_out[b], 16)
            pipeline(act, NCH, RING, [(2, store), (0, x_lead), (0, silus)])
            for b in range(RING):
                last = 16 * 2 * (HB - 1) if b == (NCH - 1) % RING else 0
                act.wait_ge(s_o_out[b], 32 * (NCH // RING) + 32 + last)

        @block.vector
        def _(dve):
            flat = C["slots"][:, :, :].rearrange("p c k -> p (c k)")
            for e in range(1, NE):
                last = nc.vector.tensor_scalar(over[:, e, :], flat, float(e * CAP), C["jump"][:, e - 1:e], ALU.is_ge, ALU.mult)
            last.then_inc(s_over, 1)
            dve.wait_ge(s_over, 1)
            nc.vector.reduce_sum(over[:, 0, :], over[:, 1:NE, :].rearrange("p e n -> p n e"), AX.X).then_inc(s_over, 1)
            dve.wait_ge(s_over, 2)
            nc.vector.tensor_tensor(gidx[:, :, :].rearrange("p c k -> p (c k)"), flat, over[:, 0, :], ALU.subtract).then_inc(s_gidx, 1)
            dve.wait_ge(s_th, 1)
            nc.vector.tensor_scalar(C["gates"][:, :, 2:3], th[:, :, 1:2], 0.5, 0.5, ALU.mult, ALU.add)
            nc.vector.tensor_scalar(beta[:, :].unsqueeze(2), th[:, :, 1:2], -0.5, 0.5, ALU.mult, ALU.add)
            nc.vector.tensor_scalar(gg[:, :, 0:1], th[:, :, 0:1], 0.5, 0.5, ALU.mult, ALU.add)
            nc.vector.tensor_scalar(gg[:, :, 1:2], th[:, :, 0:1], -0.5, 0.5, ALU.mult, ALU.add).then_inc(s_gs, 1)
            dve.wait_ge(s_gs, 1)
            nc.vector.tensor_tensor(C["gates"][:, :, 0:2], gg[:, :, :], beta[:, :].unsqueeze(2).to_broadcast([P, 2 * NCH, 2]),
                                    ALU.mult).then_inc(s_gates, 1)
            dve.wait_ge(s_gates, 1)
            for s in (s_xl, s_o1, s_o2, s_o):
                dve.sem_inc(s, RING)
            for s in (s_pm, s_pl):
                dve.sem_inc(s, MP)

            def x_rest(c, b, r):
                dve.wait_ge(s_xh, done(c))
                nc.vector.tensor_tensor(xal[b][:, :], xa[b][:, :], xah[b][:, :].bitcast(F32), ALU.subtract)
                nc.vector.tensor_tensor(xbh[b][DB:P, :], xb[b][DB:P, :], xbh[b][DB:P, :].bitcast(F32), ALU.subtract).then_inc(s_xl, 1)

            def hiddens(c, b, r):
                for m in range(MP):
                    dve.wait_ge(s_sg, done3(c, m))
                    dve.wait_ge(s_pl, done3(c - 1, m))
                    nc.vector.tensor_tensor(pm[m][:, :], sg[m][:, :], ps_u[m][:, :], ALU.mult).then_inc(s_pm, 1)
                    dve.wait_ge(s_ph, done3(c, m))
                    nc.vector.tensor_tensor(pl[b][:, m, :], pm[m][:, :], ph[b][:, m, :].bitcast(F32), ALU.subtract).then_inc(s_pl, 1)

            def sums(c, b, r):
                dve.wait_ge(s_h2_in[b], 16 * r + 16)
                dve.wait_ge(s_d, done(c))
                dve.wait_ge(s_o_out[b], 32 * r + 32)
                for half in range(2):
                    last = nc.vector.scalar_tensor_tensor(
                        out=oo[b][:, half, :], in0=ps_d[:, half * D:(half + 1) * D],
                        scalar=C["gates"][:, bass.ds(2 * c + half, 1), 2:3].rearrange("p a k -> p (a k)"), in1=h2[b][:, half, :],
                        op0=ALU.mult, op1=ALU.add)
                last.then_inc(s_o1, 1)
                dve.wait_ge(s_y_in[b], 64 * r + 64)
                for k, s_in, s_out in ((0, s_o1, s_o2), (1, s_o2, s_o)):
                    dve.wait_ge(s_in, done(c))
                    for half in range(2):
                        last = nc.vector.scalar_tensor_tensor(
                            out=oo[b][:, half, :], in0=yy[b][:, 2 * half + k, :],
                            scalar=C["gates"][:, bass.ds(2 * c + half, 1), k:k + 1].rearrange("p a k -> p (a k)"), in1=oo[b][:, half, :],
                            op0=ALU.mult, op1=ALU.add)
                    last.then_inc(s_out, 1)
            pipeline(dve, NCH, RING, [(0, x_rest), (0, hiddens), (1, sums)])

        @block.tensor
        def _(pe):
            pe.sem_inc(s_g, MP)
            pe.sem_inc(s_d, RING)

            def gate_up(c, b, r):
                pe.wait_ge(s_xl, done(c))
                (wah, wal), (wbh, wbl) = W["sgu_a"], W["sgu_b"]
                for m in range(MP):
                    pe.wait_ge(s_pm, done3(c - 1, m))
                    for bank, w0 in ((ps_g[m], 0), (ps_u[m], HS)):
                        for k in range(2):
                            f = slice(w0 + (2 * m + k) * P, w0 + (2 * m + k + 1) * P)
                            last = mm(nc, bank[:, k * 2 * P:(k + 1) * 2 * P],
                                      [(wah[:, f], xah[b][:, :]), (wah[:, f], xal[b][:, :]), (wal[:, f], xah[b][:, :]),
                                       (wbh[:, f], xbh[b][:, :]), (wbl[:, f], xbh[b][:, :])])
                    last.then_inc(s_g, 1)

            def down(c, b, r):
                pe.wait_ge(s_pl, done3(c, MP - 1))
                pe.wait_ge(s_o1, done(c - 1))
                wh, wl = W["sdn"]
                for half in range(2):
                    pairs = []
                    for m in range(2 * MP):
                        t = slice(m % 2 * 2 * P + half * P, m % 2 * 2 * P + (half + 1) * P)
                        hi, lo, w = ph[b][:, m // 2, t], pl[b][:, m // 2, t], slice(m * D, (m + 1) * D)
                        pairs += [(hi, wh[:, w]), (lo, wh[:, w]), (hi, wl[:, w])]
                    last = mm(nc, ps_d[:, half * D:(half + 1) * D], pairs)
                last.then_inc(s_d, 1)
            pipeline(pe, NCH, RING, [(0, gate_up), (1, down)])
    nc.clear_and_free_semaphores(sems)
    nc.all_engine_barrier()


def launch_program(nc, I, out):
    scratch = {
        "hbuf": nc.dram_tensor("hbuf", (B, TPAD, D), F32, kind="Internal").ap(),
        "kqT": nc.dram_tensor("kqT", (NCH, D, P), F32, kind="Internal").ap(),
        "kq": nc.dram_tensor("kq", (TPAD, NH * D), F32, kind="Internal").ap(),
        "vo": nc.dram_tensor("vo", (TPAD, NH * D), F32, kind="Internal").ap(),
        "x2T": nc.dram_tensor("x2T", (NCH, D, 2 * P), F32, kind="Internal").ap(),
        "h2": nc.dram_tensor("h2", (NCH, P, 2 * D), F32, kind="Internal").ap(),
        "xs": nc.dram_tensor("xs", (ROWS, D), F32, kind="Internal").ap(),
        "ys": nc.dram_tensor("ys", (NTILE * P, D), F32, kind="Internal").ap(),
    }
    ctx = ExitStack()
    with ctx:
        def sb(name, shape, dt=F32):
            return ctx.enter_context(nc.sbuf_tensor(name, shape, dt))

        W = {name: (sb(name + "_hi", [P, n], F32R), sb(name + "_lo", [P, n], F32R))
             for name, n in (("gu_a", NE * 2 * HE), ("gu_b", NE * 2 * HE), ("dn_a", NE * D), ("dn_b", NE * D),
                             ("sgu_a", 2 * HS), ("sgu_b", 2 * HS), ("sdn", HS // P * D))}
        W["rw_a"] = sb("rw_a", [DA, NE + 1])
        W["rw_b"] = sb("rw_b", [DB, NE + 1])
        C = {"ident": sb("ident", [P, P]), "tri": sb("tri", [P, P], BF16), "ones": sb("ones", [P, P], BF16),
             "neghalf": sb("neghalf", [P, 8]), "iota8": sb("iota8", [P, NE]), "ebase": sb("ebase", [P, NE]),
             "partf": sb("partf", [P, 1]), "maskf": sb("maskf", [P, 2 * HB, STEP]), "decay": sb("decay", [P, 2]),
             "sgb": sb("sgb", [P, 1]),
             "slots": sb("slots", [P, NCH, 4]), "jump": sb("jump", [P, NE]), "pre": sb("pre", [P, 2 * NCH, 2]), "gates": sb("gates", [P, 2 * NCH, 3]),
             "load": sb("load", [P, NE], BF16)}
        prepare(nc, I, scratch, W, C)
        attention_tables(nc, I, scratch, C)
        tokens(nc, I, scratch, C, W)
        experts(nc, scratch, C, W)
        combine(nc, scratch, C, W, out)


_INS = ['x', 'x_txt', 'L0_tok_W', 'L0_tok_b', 'L0_tok_cls', 'L0_tok_pos_embed', 'L0_txt_basin_coords', 'L0_txt_proj_w',
        'L0_txt_norm_w', 'L0_attn_w_key', 'L0_attn_w_value', 'L0_attn_w_query', 'L0_attn_w_gate', 'L0_attn_w_out',
        'L0_ffn_router_w', 'L0_ffn_w_gate', 'L0_ffn_w_up', 'L0_ffn_w_down', 'L0_ffn_ws_gate', 'L0_ffn_ws_up',
        'L0_ffn_ws_down', 'L0_ffn_sg_w', 'L0_ffn_sg_b']


def kernel(**inputs):
    import numpy as _np
    import concourse.bacc as _bacc
    from concourse import mybir as _mybir
    from concourse.bass_utils import run_bass_kernel_spmd as _run

    nc = _bacc.Bacc("TRN2", target_bir_lowering=False, num_devices=1)
    arrays, args = {}, {}
    for name in _INS:
        a = _np.ascontiguousarray(inputs[name])
        arrays[f"in_{name}"] = a
        args[name] = nc.dram_tensor(f"in_{name}", a.shape, _mybir.dt.from_np(a.dtype), kind="ExternalInput").ap()
    out = nc.dram_tensor("out_0", (B, T, D), _mybir.dt.float32, kind="ExternalOutput").ap()
    launch_program(nc, args, out)
    r = _run(nc, [arrays], core_ids=[0])
    return r.results[0]["out_0"]
```

```python
import concourse.bass as bass
from concourse import mybir
from contextlib import ExitStack

F32 = mybir.dt.float32
F32R = mybir.dt.float32r
BF16 = mybir.dt.bfloat16
I32 = mybir.dt.int32
U32 = mybir.dt.uint32
ACT = mybir.ActivationFunctionType
ALU = mybir.AluOpType
AX = mybir.AxisListType

P = 128
B, T, D = 16, 709, 192
DA, DB = 128, D - 128
NPATCH, SIDE, PX = 196, 14, 16
NTXT, BASIN, VOCAB = 512, 64, 32000
NH, DK = 8, 64
STEP = 16
NCH = -(-T // STEP)
TPAD = NCH * STEP
HB = B // 2
NE, HE, HS = 8, 192, 768
CAP = B * TPAD + P
NTILE = -(-((2 * B * TPAD + NE * (P - 1)) // P) // 4) * 4
DUMMY = NE * CAP
NDUMMY = NTILE - 2 * B * TPAD // P
ROWS = DUMMY + NDUMMY * P
DECAY, WRITE = 0.95, 0.1
LN_EPS, RMS_EPS = 1e-5, 1e-8


def mm(nc, out, pairs, start=True, stop=True):
    for n, (lhsT, rhs) in enumerate(pairs):
        last = nc.tensor.matmul(out, lhsT, rhs, start=start and n == 0, stop=stop and n == len(pairs) - 1)
    return last


def pipeline(eng, n, ring, stages, peel=1, turn=None):
    for s in range(ring * peel):
        for lag, body in stages:
            if s >= lag:
                body(s - lag, (s - lag) % ring, (s - lag) // ring)
    with eng.Fori(peel, n // ring) as i:
        if turn:
            turn(i)
        for u in range(ring):
            for lag, body in stages:
                body(ring * i + u - lag, (u - lag) % ring, i + (u - lag) // ring)
    for s in range(n, n + max(lag for lag, _ in stages)):
        for lag, body in stages:
            if s - lag < n:
                body(s - lag, (s - lag) % ring, (s - lag) // ring)


def done2(c):
    return c + 3


def free2(c):
    return c + 1


def prepare(nc, I, scratch, W, C):
    hbuf = scratch["hbuf"]
    ctx = ExitStack()
    sems = []
    with ctx:
        def sb(name, shape, dt=F32):
            return ctx.enter_context(nc.sbuf_tensor(name, shape, dt))

        def pb(name, shape, dt=F32):
            return ctx.enter_context(nc.psum_tensor(name, shape, dt))

        def sem(name):
            sems.append(nc.alloc_semaphore(name))
            return sems[-1]

        raw = [sb(f"raw{n}", [P, 1536]) for n in range(2)]
        img = [sb(f"img{n}", [96, SIDE, SIDE * PX]) for n in range(4)]
        tokw = sb("tokw", [96, 8, D])
        posb = sb("posb", [98, 2, D])
        bias_bc = sb("bias_bc", [98, D])
        pstage = [sb(f"pstage{n}", [98, 2, D]) for n in range(2)]
        cls_row = sb("cls_row", [B, D])
        pos0_row = sb("pos0_row", [B, D])
        cls_out = sb("cls_out", [B, D])
        zeros = sb("zeros", [P, D])
        projn = sb("projn", [P, 2, 2, BASIN])
        projT = sb("projT", [P, D])
        normw = sb("normw", [P, D])
        ids = sb("ids", [P, B, 4], I32)
        idsf = sb("idsf", [P, B, 4])
        idneg = sb("idneg", [P, B, 4])
        ids_ok = sb("ids_ok", [P, B, 4], U32)
        idc = [sb(f"idc{n}", [P, 4], U32) for n in range(2)]
        basin = [sb(f"basin{n}", [P, 4, BASIN]) for n in range(2)]
        basinT = [sb(f"basinT{n}", [P, 2, P]) for n in range(2)]
        sq = [sb(f"sq{n}", [P, 4, D]) for n in range(2)]
        ssq = [sb(f"ssq{n}", [P, 4]) for n in range(2)]
        msq = [sb(f"msq{n}", [P, 4]) for n in range(2)]
        rinv = [sb(f"rinv{n}", [P, 4]) for n in range(2)]
        tstage = [sb(f"tstage{n}", [P, 4, D]) for n in range(2)]
        tmp_i = sb("tmp_i", [P, 1], I32)
        part_i = sb("part_i", [P, 1], I32)
        s_f = sb("s_f", [P, 1])
        drow = sb("drow", [1, 2, P])
        one1 = sb("one1", [1, 1])

        ps_img = [pb(f"ps_img{n}", [P, 512]) for n in range(2)]
        ps_tT = [pb(f"ps_tT{n}", [P, 512]) for n in range(2)]
        ps_emb = [pb(f"ps_emb{n}", [P, 2, 512]) for n in range(2)]

        s_raw = [sem(f"raw_in{n}") for n in range(2)]
        s_hi = sem("hi_done")
        s_lo = sem("lo_done")
        s_tokw = sem("tokw_in")
        s_small = sem("small_in")
        s_ids = sem("ids_in")
        s_img = [sem(f"img_in{n}") for n in range(4)]
        s_posb = sem("posb_done")
        s_pmm = sem("patch_product")
        s_pst = sem("patch_staged")
        s_pout = [sem(f"patch_stored{n}") for n in range(2)]
        s_cls = sem("cls_done")
        s_clsout = sem("cls_stored")
        s_zero = sem("zeros_done")
        s_zout = sem("pads_stored")
        s_iota = sem("iota_done")
        s_const = sem("const_step")
        s_ident = sem("ident_done")
        s_drow = sem("decay_row")
        s_dcol = sem("decay_column")
        s_projT = sem("projT_product")
        s_projTc = sem("projT_done")
        s_idok = sem("ids_ok")
        s_idc = sem("ids_copied")
        s_apart = sem("apart")
        s_bas = [sem(f"basin_in{n}") for n in range(2)]
        s_bT = sem("basinT_product")
        s_bTc = sem("basinT_done")
        s_emb = sem("emb_product")
        s_ssq = sem("squares_summed")
        s_msq = sem("mean_square")
        s_rinv = sem("rms_inverse")
        s_tst = sem("text_staged")
        s_tout = [sem(f"text_stored{n}") for n in range(2)]
        block = ctx.enter_context(nc.Block())

        wg, wu, wd = (I[k].rearrange("e d h -> d e h") for k in ("L0_ffn_w_gate", "L0_ffn_w_up", "L0_ffn_w_down"))
        sg, su = I["L0_ffn_ws_gate"], I["L0_ffn_ws_up"]
        sd = I["L0_ffn_ws_down"].rearrange("(m p) d -> p m d", p=P)

        def pairs4(r):
            return r[:, :].rearrange("p (e n) -> p e n", e=4)

        pieces = []
        for e0 in (0, 4):
            pieces.append(([(lambda r: pairs4(r)[:, :, 0:HE], wg[0:DA, e0:e0 + 4, :]),
                            (lambda r: pairs4(r)[:, :, HE:2 * HE], wu[0:DA, e0:e0 + 4, :])],
                           W["gu_a"], slice(e0 * 2 * HE, (e0 + 4) * 2 * HE)))
            pieces.append(([(lambda r, q=q: pairs4(r)[q:q + DB, :, 0:HE], wg[DA:D, e0:e0 + 4, :]) for q in (0, 64)]
                           + [(lambda r, q=q: pairs4(r)[q:q + DB, :, HE:2 * HE], wu[DA:D, e0:e0 + 4, :]) for q in (0, 64)],
                           W["gu_b"], slice(e0 * 2 * HE, (e0 + 4) * 2 * HE)))
        pieces.append(([(lambda r: r[:, :].rearrange("p (e n) -> p e n", e=NE), wd[0:DA, :, :])],
                       W["dn_a"], slice(0, NE * D)))
        pieces.append(([(lambda r, q=q: r[q:q + DB, :].rearrange("p (e n) -> p e n", e=NE), wd[DA:D, :, :]) for q in (0, 64)],
                       W["dn_b"], slice(0, NE * D)))
        pieces.append(([(lambda r: r[:, 0:HS], sg[0:DA, :]), (lambda r: r[:, HS:2 * HS], su[0:DA, :])],
                       W["sgu_a"], slice(0, 2 * HS)))
        pieces.append(([(lambda r, q=q: r[q:q + DB, 0:HS], sg[DA:D, :]) for q in (0, 64)]
                       + [(lambda r, q=q: r[q:q + DB, HS:2 * HS], su[DA:D, :]) for q in (0, 64)],
                       W["sgu_b"], slice(0, 2 * HS)))
        pieces.append(([(lambda r: r[:, 0:6 * D].rearrange("p (m d) -> p m d", m=6), sd)],
                       W["sdn"], slice(0, 6 * D)))
        raw_count = [[0, 0]]
        for n, (dmas, _, _) in enumerate(pieces):
            c = list(raw_count[-1])
            c[n % 2] += 16 * len(dmas)
            raw_count.append(c)

        tokw_v = I["L0_tok_W"].rearrange("(i s j c) d -> s c i j d", i=PX, s=2, c=3)
        pos = I["L0_tok_pos_embed"]

        @block.sync
        def _(sp):
            for s in range(2):
                for c in range(3):
                    q = (3 * s + c) * PX
                    sp.dma_start(tokw[q:q + PX, :, :], tokw_v[s, c]).then_inc(s_tokw, 16)

            def small():
                sp.dma_start(bias_bc[:, :], I["L0_tok_b"].partition_broadcast(98)).then_inc(s_small, 16)
                sp.dma_start(posb[:, :, :], pos[0, 1:NPATCH + 1, :].rearrange("(g p) d -> p g d", p=98)).then_inc(s_small, 16)
                sp.dma_start(cls_row[:, :], I["L0_tok_cls"][0, :].partition_broadcast(B)).then_inc(s_small, 16)
                sp.dma_start(pos0_row[:, :], pos[0, 0, :].partition_broadcast(B)).then_inc(s_small, 16)
                sp.dma_start(normw[:, :], I["L0_txt_norm_w"].partition_broadcast(P)).then_inc(s_small, 16)
                for q in range(2):
                    sp.dma_start(projn[:, 0, q, :], I["L0_txt_proj_w"][0:P, :]).then_inc(s_small, 16)
                    sp.dma_start(projn[0:DB, 1, q, :], I["L0_txt_proj_w"][P:D, :]).then_inc(s_small, 16)
                sp.dma_start(W["rw_a"][:, 0:NE], I["L0_ffn_router_w"][0:DA, :]).then_inc(s_small, 16)
                sp.dma_start(W["rw_b"][:, 0:NE], I["L0_ffn_router_w"][DA:D, :]).then_inc(s_small, 16)
                sp.dma_start(W["rw_a"][:, NE:NE + 1], I["L0_ffn_sg_w"][0:DA, :]).then_inc(s_small, 16)
                sp.dma_start(W["rw_b"][:, NE:NE + 1], I["L0_ffn_sg_w"][DA:D, :]).then_inc(s_small, 16)
                sp.dma_start(C["sgb"][:, :], I["L0_ffn_sg_b"].partition_broadcast(P)).then_inc(s_small, 16)

            def images(c, b, r):
                if not (isinstance(c, int) and c < 4):
                    sp.wait_ge(s_pmm, done2(c - 4))
                for s in range(2):
                    for ch in range(3):
                        q = (3 * s + ch) * PX
                        src = I["x"][bass.ds(c, 1), ch, :, :].rearrange("b (n i) w -> (b i) n w", i=PX)
                        n = SIDE * PX - 8 * s
                        sp.dma_start(img[b][q:q + PX, :, 0:n], src[:, :, 8 * s:8 * s + n]).then_inc(s_img[b], 16)
            images(0, 0, 0)
            small()
            for c in range(1, 4):
                images(c, c, 0)
            with sp.Fori(1, B // 4) as i:
                for u in range(4):
                    images(4 * i + u, u, i)
            for u in range(2):
                sp.wait_ge(s_pout[u], 16 * HB + 16)
                sp.wait_ge(s_tout[u], 16 * HB + 16)
            sp.wait_ge(s_clsout, 16)
            sp.wait_ge(s_zout, 32)

        @block.gpsimd
        def _(pool):
            nc.gpsimd.memset(zeros[:, :], 0.0).then_inc(s_zero, 1)
            nc.gpsimd.memset(C["ident"][:, :], 0.0).then_inc(s_zero, 1)
            nc.gpsimd.memset(C["tri"][:, :], 0.0).then_inc(s_zero, 1)
            nc.gpsimd.memset(C["ones"][:, :], 1.0).then_inc(s_zero, 1)
            nc.gpsimd.memset(C["neghalf"][:, :], -0.5).then_inc(s_zero, 1)
            nc.gpsimd.iota(C["iota8"][:, :], pattern=[[1, NE]], base=0, channel_multiplier=0,
                           allow_small_or_imprecise_dtypes=True).then_inc(s_iota, 1)
            nc.gpsimd.iota(C["ebase"][:, :], pattern=[[CAP, NE]], base=0, channel_multiplier=0,
                           allow_small_or_imprecise_dtypes=True).then_inc(s_iota, 1)
            nc.gpsimd.iota(part_i[:, :], pattern=[[0, 1]], base=0, channel_multiplier=1).then_inc(s_iota, 1)
            nc.gpsimd.iota(C["partf"][:, :], pattern=[[0, 1]], base=0, channel_multiplier=1,
                           allow_small_or_imprecise_dtypes=True).then_inc(s_iota, 1)
            nc.gpsimd.iota(C["maskf"][:, :, :, :], pattern=[[0, 2], [1, STEP], [0, HB]], base=0, channel_multiplier=0,
                           allow_small_or_imprecise_dtypes=True).then_inc(s_iota, 1)
            pool.wait_ge(s_zero, 5)
            nc.gpsimd.affine_select(out=C["ident"][:, :], in_=C["ident"][:, :], compare_op=ALU.not_equal, fill=1.0,
                                    base=0, pattern=[[-1, P]], channel_multiplier=1).then_inc(s_ident, 1)
            nc.gpsimd.affine_select(out=C["tri"][:, :], in_=C["tri"][:, :], compare_op=ALU.is_ge, fill=1.0,
                                    base=0, pattern=[[-1, P]], channel_multiplier=1).then_inc(s_ident, 1)
            pool.wait_ge(s_idok, 1)
            pool.sem_inc(s_idc, 2)
            pool.sem_inc(s_rinv, 2)

            def gather(c, b, r):
                pool.wait_ge(s_bT, free2(c))
                nc.gpsimd.tensor_copy(idc[b][:, :], ids_ok[:, bass.ds(c, 1), :].rearrange("p a j -> p (a j)")).then_inc(s_idc, 1)
                pool.wait_ge(s_idc, done2(c))
                pool.sem_inc(s_apart, 1)
                for j in range(4):
                    nc.gpsimd.indirect_dma_start(basin[b][:, j, :], None, I["L0_txt_basin_coords"],
                                                 bass.IndirectOffsetOnAxis(ap=idc[b][:, j:j + 1], axis=0)).then_inc(s_bas[b], 16)

            def rms_inverse(c, b, r):
                pool.wait_ge(s_msq, done2(c))
                pool.wait_ge(s_tst, free2(c))
                nc.gpsimd.tensor_tensor(rinv[b][:, :], msq[b][:, :], C["neghalf"][:, 0:4], ALU.pow).then_inc(s_rinv, 1)
            pipeline(pool, B, 2, [(0, gather), (3, rms_inverse)], peel=2)

        @block.scalar
        def _(act):
            act.dma_start(ids[:, :, :], I["x_txt"].rearrange("b (p j) -> p b j", j=4)).then_inc(s_ids, 16)

            def load(n):
                for dst, src in pieces[n][0]:
                    act.dma_start(dst(raw[n % 2]), src).then_inc(s_raw[n % 2], 16)
            load(0)
            load(1)
            act.wait_ge(s_zero, 1)
            act.dma_start(hbuf[T:TPAD, :, :].rearrange("t b d -> b t d"), zeros[:, :].unsqueeze(1)[0:B, :, :].to_broadcast([B, TPAD - T, D])).then_inc(s_zout, 16)
            act.dma_start(scratch["xs"][DUMMY:ROWS, :].rearrange("(k p) d -> p k d", p=P),
                          zeros[:, :].unsqueeze(1).to_broadcast([P, NDUMMY, D])).then_inc(s_zout, 16)
            act.wait_ge(s_cls, 1)
            act.dma_start(hbuf[0, :, :], cls_out[:, :]).then_inc(s_clsout, 16)
            act.sem_inc(s_bTc, 2)
            act.sem_inc(s_ssq, 2)

            def lead(n):
                hi, cols = pieces[n][1][0], pieces[n][2]
                act.wait_ge(s_raw[n % 2], raw_count[n + 1][n % 2])
                nc.scalar.activation(hi[:, cols], raw[n % 2][:, 0:cols.stop - cols.start], ACT.Copy).then_inc(s_hi, 1)
                if n >= 1 and n + 1 < len(pieces):
                    act.wait_ge(s_lo, n)
                    load(n + 1)

            def leads(c, b, r):
                if isinstance(c, int) and c < len(pieces) - 1:
                    lead(c)

            def basin_columns(c, b, r):
                act.wait_ge(s_bT, done2(c))
                act.wait_ge(s_emb, free2(c))
                nc.scalar.activation(basinT[b][:, :, :], ps_tT[b][:, 0:2 * P].rearrange("p (j n) -> p j n", j=2), ACT.Copy).then_inc(s_bTc, 1)

            def squares(c, b, r):
                act.wait_ge(s_emb, done2(c))
                act.wait_ge(s_msq, free2(c))
                for j in range(4):
                    last = nc.scalar.activation(sq[b][:, j, :], ps_emb[b][:, j % 2, j // 2 * D:(j // 2 + 1) * D],
                                                ACT.Square, accum_out=ssq[b][:, j:j + 1])
                last.then_inc(s_ssq, 1)

            def store_patches(c, b, r):
                act.wait_ge(s_pst, done2(c))
                dst = hbuf[1:1 + NPATCH, bass.ds(c, 1), :].rearrange("(g p) b d -> p (g b) d", p=98)
                act.dma_start(dst, pstage[b][:, :, :]).then_inc(s_pout[b], 16)

            def store_text(c, b, r):
                act.wait_ge(s_tst, done2(c))
                dst = hbuf[1 + NPATCH:T, bass.ds(c, 1), :].rearrange("(p j) b d -> p (j b) d", j=4)
                act.dma_start(dst, tstage[b][:, :, :]).then_inc(s_tout[b], 16)
            pipeline(act, B, 2, [(4, store_text), (1, basin_columns), (1, store_patches), (2, squares), (0, leads)], peel=len(pieces) // 2)
            lead(len(pieces) - 1)

        @block.vector
        def _(dve):
            dve.wait_ge(s_iota, 5)
            nc.vector.tensor_scalar(tmp_i[:, :], part_i[:, :], 3, None, ALU.arith_shift_right).then_inc(s_const, 1)
            dve.wait_ge(s_const, 1)
            nc.vector.tensor_copy(s_f[:, :], tmp_i[:, :]).then_inc(s_const, 1)
            dve.wait_ge(s_const, 2)
            nc.vector.tensor_scalar(C["maskf"][:, :, :, :], C["maskf"][:, :, :, :], s_f[:, 0:1], None, ALU.is_gt).then_inc(s_const, 1)
            for s in range(STEP):
                nc.vector.memset(drow[0:1, 0, s * P // STEP:(s + 1) * P // STEP], DECAY ** s)
                last = nc.vector.memset(drow[0:1, 1, :].rearrange("p (a s) -> p a s", s=STEP)[:, :, s:s + 1],
                                        0.5 * WRITE * DECAY ** -(s + 1))
            nc.vector.memset(one1[:, :], 1.0).then_inc(s_drow, 1)
            dve.wait_ge(s_dcol, 1)
            nc.vector.tensor_copy(C["decay"][:, :], ps_tT[0][:, 0:2]).then_inc(s_const, 1)
            dve.wait_ge(s_ids, 16)
            nc.vector.tensor_copy(idsf[:, :, :], ids[:, :, :]).then_inc(s_const, 1)
            dve.wait_ge(s_const, 5)
            nc.vector.tensor_scalar(idneg[:, :, :], idsf[:, :, :], 0.0, float(VOCAB), ALU.is_lt, ALU.mult).then_inc(s_const, 1)
            dve.wait_ge(s_const, 6)
            nc.vector.tensor_tensor(idsf[:, :, :], idsf[:, :, :], idneg[:, :, :], ALU.add).then_inc(s_const, 1)
            dve.wait_ge(s_const, 7)
            nc.vector.tensor_scalar(ids_ok[:, :, :], idsf[:, :, :], 0.0, float(VOCAB - 1), ALU.max, ALU.min).then_inc(s_idok, 1)
            dve.wait_ge(s_small, 16 * 14)
            nc.vector.tensor_tensor(posb[:, :, :], posb[:, :, :], bias_bc[:, :].unsqueeze(1).to_broadcast([98, 2, D]), ALU.add).then_inc(s_posb, 1)
            nc.vector.tensor_tensor(cls_out[:, :], cls_row[:, :], pos0_row[:, :], ALU.add).then_inc(s_cls, 1)
            dve.wait_ge(s_projT, 1)
            nc.vector.tensor_copy(projT[:, :], ps_tT[1][:, 0:D]).then_inc(s_projTc, 1)
            for u in range(2):
                dve.sem_inc(s_pout[u], 16)
                dve.sem_inc(s_tout[u], 16)
            for s in (s_pst, s_tst, s_msq):
                dve.sem_inc(s, 2)
            dve.wait_ge(s_posb, 1)

            def rest(n):
                (hi, lo), cols = pieces[n][1:]
                dve.wait_ge(s_hi, n + 1)
                nc.vector.tensor_tensor(lo[:, cols], raw[n % 2][:, 0:cols.stop - cols.start], hi[:, cols].bitcast(F32),
                                        ALU.subtract).then_inc(s_lo, 1)

            def rests(c, b, r):
                if isinstance(c, int) and c < len(pieces) - 1:
                    rest(c)

            def stage_patches(c, b, r):
                dve.wait_ge(s_pmm, done2(c))
                dve.wait_ge(s_pout[b], 16 * r + 16)
                nc.vector.tensor_tensor(pstage[b][:, :, :], ps_img[b][0:98, 0:2 * D].rearrange("p (g d) -> p g d", g=2),
                                        posb[:, :, :], ALU.add).then_inc(s_pst, 1)

            def mean_square(c, b, r):
                dve.wait_ge(s_ssq, done2(c))
                dve.wait_ge(s_rinv, free2(c))
                nc.vector.tensor_scalar(msq[b][:, :], ssq[b][:, :], 1.0 / D, RMS_EPS, ALU.mult, ALU.add).then_inc(s_msq, 1)

            def stage_text(c, b, r):
                dve.wait_ge(s_rinv, done2(c))
                dve.wait_ge(s_tout[b], 16 * r + 16)
                for j in range(4):
                    last = nc.vector.scalar_tensor_tensor(
                        out=tstage[b][:, j, :], in0=ps_emb[b][:, j % 2, j // 2 * D:(j // 2 + 1) * D],
                        scalar=rinv[b][:, j:j + 1], in1=normw[:, :], op0=ALU.mult, op1=ALU.mult)
                last.then_inc(s_tst, 1)
            pipeline(dve, B, 2, [(3, stage_text), (0, stage_patches), (0, rests), (2, mean_square)], peel=len(pieces) // 2)
            rest(len(pieces) - 1)

        @block.tensor
        def _(pe):
            pe.wait_ge(s_drow, 1)
            for k in range(2):
                last = nc.tensor.matmul(ps_tT[0][:, k:k + 1], drow[0:1, k, :], one1[:, :], start=True, stop=True)
            last.then_inc(s_dcol, 1)
            pe.wait_ge(s_small, 16 * 14)
            pe.wait_ge(s_ident, 2)
            nc.tensor.transpose(ps_tT[1][:, 0:P], projn[:, 0, :, :].rearrange("p q k -> p (q k)"), C["ident"][:, :])
            nc.tensor.transpose(ps_tT[1][:, P:D], projn[0:DB, 1, :, :].rearrange("p q k -> p (q k)"), C["ident"][0:DB, 0:DB]).then_inc(s_projT, 1)
            pe.wait_ge(s_tokw, 96)
            pe.wait_ge(s_const, 4)
            pe.wait_ge(s_projTc, 1)
            for s in (s_pmm, s_bT, s_emb):
                pe.sem_inc(s, 2)

            def patches(c, b, r):
                pe.wait_ge(s_img[b], 96 * r + 96)
                pe.wait_ge(s_pst, free2(c))
                for g in range(2):
                    for j in range(8):
                        px = img[b][:, 7 * g:7 * g + 7, :].rearrange("p n (w j) -> p n w j", j=PX)[:, :, :, j]
                        last = nc.tensor.matmul(ps_img[b % 2][0:98, g * D:(g + 1) * D], px, tokw[:, j, :],
                                                start=j == 0, stop=j == 7)
                last.then_inc(s_pmm, 1)

            def basin_transposes(c, b, r):
                pe.wait_ge(s_bas[b % 2], 64 * (2 * r + b // 2) + 64)
                pe.wait_ge(s_bTc, free2(c))
                for j in range(2):
                    last = nc.tensor.transpose(ps_tT[b % 2][:, j * P:(j + 1) * P],
                                               basin[b % 2][:, 2 * j:2 * j + 2, :].rearrange("p j k -> p (j k)"), C["ident"][:, :])
                last.then_inc(s_bT, 1)

            def embed(c, b, r):
                pe.wait_ge(s_bTc, done2(c))
                pe.wait_ge(s_tst, free2(c))
                for j in range(4):
                    last = nc.tensor.matmul(ps_emb[b % 2][:, j % 2, j // 2 * D:(j // 2 + 1) * D],
                                            basinT[b % 2][j % 2 * BASIN:(j % 2 + 1) * BASIN, j // 2, :],
                                            projT[j % 2 * BASIN:(j % 2 + 1) * BASIN, :], start=True, stop=True)
                last.then_inc(s_emb, 1)
            pipeline(pe, B, 4, [(1, basin_transposes), (0, patches), (2, embed)])
    nc.clear_and_free_semaphores(sems)
    nc.all_engine_barrier()


def attention_tables(nc, I, scratch, C):
    ctx = ExitStack()
    sems = []
    NF = TPAD // P
    TAIL = TPAD - NF * P
    BLK = [P] * NF + [TAIL]
    NB = NF + 1
    SPLIT = [(0, 368), (368, TPAD)]
    PER = 4 + NB
    with ctx:
        def sb(name, shape, dt=F32):
            return ctx.enter_context(nc.sbuf_tensor(name, shape, dt))

        def pb(name, shape, dt=F32):
            return ctx.enter_context(nc.psum_tensor(name, shape, dt))

        def sem(name):
            sems.append(nc.alloc_semaphore(name))
            return sems[-1]

        h0 = sb("h0", [P, NB, D])
        stats = sb("stats0", [P, NB, 6])
        mv = sb("mv0", [P, NB, 2])
        vare = sb("vare0", [P, NB])
        rstd = sb("rstd0", [P, NB])
        wk = sb("wk", [P, 4, D])
        wv = sb("wv", [P, 4, D])
        wq = sb("wq", [P, 4, D])
        wo = sb("wo", [P, 2, NH * DK])
        wgt = sb("wgt", [NH, D])
        wkT = [sb("wkT_a", [DA, 4, P]), sb("wkT_b", [DB, 4, P])]
        wvT = [sb("wvT_a", [DA, 4, P]), sb("wvT_b", [DB, 4, P])]
        woT = sb("woT", [P, 4, D])
        wgT = [sb("wgT_a", [DA, NH]), sb("wgT_b", [DB, NH])]
        x0T = [sb("x0T_a", [DA, TPAD]), sb("x0T_b", [DB, TPAD])]
        kvT = sb("kvT", [P, 2, TPAD])
        kqT_a = sb("kqT_a", [DA, TPAD, NH])
        kqT_b = sb("kqT_b", [P, 368, NH])
        rows = sb("rows", [P, NB, 2 * D])
        gsc = sb("gsc", [P, NB, NH])
        gscale = sb("gscale", [P, NB, NH])
        ps = [pb(f"ps{n}", [P, 512]) for n in range(8)]

        s_w = sem("attn_weights_in")
        s_h = sem("h0_in")
        s_stat = sem("stats0_done")
        s_aggr = sem("aggr0_done")
        s_var = sem("var0_done")
        s_rstd = sem("rstd0_done")
        s_x0 = sem("x0_done")
        s_wTp = sem("weight_transposed")
        s_wT = sem("weightT_copied")
        s_x0Tp = sem("x0_transposed")
        s_x0T = sem("x0T_copied")
        s_gl = sem("gate_logits")
        s_gt = sem("gate_tanh")
        s_gs = sem("gate_scale")
        s_kv = sem("kv_product")
        s_kvc = sem("kv_copied")
        s_bank = sem("head_bank_filled")
        s_evA = sem("bank_copied_act")
        s_evD = sem("bank_copied_dve")
        s_row = sem("rows_stored")
        s_tab = sem("kqT_stored")
        block = ctx.enter_context(nc.Block())
        ident = C["ident"]
        hb = scratch["hbuf"]

        @block.sync
        def _(sp):
            sp.dma_start(h0[:, 0:NF, :], hb[0:NF * P, 0, :].rearrange("(k p) d -> p k d", p=P)).then_inc(s_h, 16)
            sp.dma_start(h0[0:TAIL, NF, :], hb[NF * P:TPAD, 0, :]).then_inc(s_h, 16)
            for w, name in ((wk, "L0_attn_w_key"), (wv, "L0_attn_w_value"), (wq, "L0_attn_w_query")):
                sp.dma_start(w[:, :, :], I[name].rearrange("(m p) d -> p m d", p=P)).then_inc(s_w, 16)
            sp.dma_start(wo[:, 0, :], I["L0_attn_w_out"][0:P, :]).then_inc(s_w, 16)
            sp.dma_start(wo[0:DB, 1, :], I["L0_attn_w_out"][P:D, :]).then_inc(s_w, 16)
            sp.dma_start(wgt[:, :], I["L0_attn_w_gate"]).then_inc(s_w, 16)
            for h in range(NH):
                sp.wait_ge(s_evA, PER // 2 * (h + 1))
                sp.wait_ge(s_evD, PER // 2 * (h + 1))
                dst = scratch["kqvo"][:, h, :]
                sp.dma_start(dst[0:NF * P, :].rearrange("(k p) d -> p k d", p=P), rows[:, 0:NF, :]).then_inc(s_row, 16)
                sp.dma_start(dst[NF * P:TPAD, :], rows[0:TAIL, NF, :]).then_inc(s_row, 16)
            c0 = SPLIT[0][1] // STEP
            dst = scratch["kqT"].rearrange("c d x -> d c x")
            sp.dma_start(dst[0:DA, :, :], kqT_a[:, :, :].rearrange("d (c s) h -> d c (s h)", s=STEP)).then_inc(s_tab, 16)
            sp.dma_start(dst[DA:D, 0:c0, :], kqT_b[0:DB, :, :].rearrange("d (c s) h -> d c (s h)", s=STEP)).then_inc(s_tab, 16)
            sp.dma_start(dst[DA:D, c0:NCH, :], kqT_b[DB:P, 0:TPAD - c0 * STEP, :].rearrange("d (c s) h -> d c (s h)", s=STEP)).then_inc(s_tab, 16)
            sp.wait_ge(s_tab, 48)
            sp.wait_ge(s_row, 32 * NH)

        @block.gpsimd
        def _(pool):
            pool.wait_ge(s_var, 1)
            nc.gpsimd.tensor_tensor(rstd[:, :], vare[:, :], C["neghalf"][:, 0:NB], ALU.pow).then_inc(s_rstd, 1)

        @block.scalar
        def _(act):
            act.wait_ge(s_wTp, 1)
            for n, wT in enumerate((wkT[0], wkT[1], wvT[0], wvT[1])):
                r = DA if n % 2 == 0 else DB
                nc.scalar.activation(wT[:, :, :], ps[n][0:r, :].rearrange("p (m n) -> p m n", m=4), ACT.Copy).then_inc(s_wT, 1)
            for n in range(2):
                nc.scalar.activation(woT[:, 2 * n:2 * n + 2, :], ps[4 + n][:, 0:2 * D].rearrange("p (m n) -> p m n", m=2), ACT.Copy).then_inc(s_wT, 1)
            nc.scalar.activation(wgT[0][:, :], ps[6][0:DA, 0:NH], ACT.Copy).then_inc(s_wT, 1)
            nc.scalar.activation(wgT[1][:, :], ps[6][0:DB, NH:2 * NH], ACT.Copy).then_inc(s_wT, 1)
            act.wait_ge(s_gl, 1)
            nc.scalar.activation(gsc[:, 0:NF, :], ps[4][:, 0:NF * NH].rearrange("p (k h) -> p k h", h=NH), ACT.Tanh, scale=0.5).then_inc(s_gt, 1)
            nc.scalar.activation(gsc[0:TAIL, NF, :], ps[4][0:TAIL, NF * NH:NB * NH], ACT.Tanh, scale=0.5).then_inc(s_gt, 1)
            act.wait_ge(s_gs, 2)
            for m in range(4):
                for t in range(2):
                    for n, (a, b) in enumerate(SPLIT):
                        act.wait_ge(s_kv, 4 * m + 2 * t + n + 1)
                        if m:
                            act.wait_ge(s_bank, 2 * PER * m)
                        nc.scalar.activation(kvT[:, t, a:b], ps[2 * t + n][:, 0:b - a], ACT.Copy).then_inc(s_kvc, 1)
                for h in (2 * m, 2 * m + 1):
                    for j in range(0, PER, 2):
                        bank = ps[4 + (PER * h + j) % 4]
                        act.wait_ge(s_bank, PER * h + j + 1)
                        if j < 4:
                            a, b = SPLIT[j // 2]
                            nc.scalar.activation(kqT_a[:, a:b, h], bank[:, 0:b - a], ACT.Copy).then_inc(s_evA, 1)
                        else:
                            k, n = j - 4, BLK[j - 4]
                            if h:
                                act.wait_ge(s_row, 32 * h)
                            nc.scalar.activation(rows[0:n, k, 0:D], bank[0:n, 0:D], ACT.Copy)
                            nc.scalar.activation(rows[0:n, k, D:2 * D], bank[0:n, D:2 * D], ACT.Copy, scale=gscale[0:n, k, h:h + 1]).then_inc(s_evA, 1)

        @block.vector
        def _(dve):
            dve.wait_ge(s_h, 32)
            for k, n in enumerate(BLK):
                last = nc.vector.bn_stats(stats[0:n, k, :], h0[0:n, k, :])
            last.then_inc(s_stat, 1)
            dve.wait_ge(s_stat, 1)
            nc.vector.memset(mv[:, :, :], 1.0).then_inc(s_aggr, 1)
            dve.wait_ge(s_aggr, 1)
            for k, n in enumerate(BLK):
                last = nc.vector.bn_aggr(mv[0:n, k, :], stats[0:n, k, :])
            last.then_inc(s_aggr, 1)
            dve.wait_ge(s_aggr, 2)
            nc.vector.tensor_scalar(vare[:, :], mv[:, :, 1], LN_EPS, None, ALU.add).then_inc(s_var, 1)
            dve.wait_ge(s_rstd, 1)
            for k, n in enumerate(BLK):
                last = nc.vector.tensor_scalar(h0[0:n, k, :], h0[0:n, k, :], mv[0:n, k, 0:1], rstd[0:n, k:k + 1],
                                               ALU.subtract, ALU.mult)
            last.then_inc(s_x0, 1)
            dve.wait_ge(s_x0Tp, 1)
            for half, r in enumerate((DA, DB)):
                nc.vector.tensor_copy(x0T[half][:, 0:512], ps[2 * half][0:r, 0:512])
                last = nc.vector.tensor_copy(x0T[half][:, 512:TPAD], ps[2 * half + 1][0:r, 0:TPAD - 512])
            last.then_inc(s_x0T, 1)
            dve.wait_ge(s_gt, 2)
            nc.vector.tensor_scalar(gscale[:, 0:NF, :], gsc[:, 0:NF, :], 1.0, C["decay"][:, 1:2], ALU.add, ALU.mult).then_inc(s_gs, 1)
            nc.vector.tensor_scalar(gscale[0:TAIL, NF, :], gsc[0:TAIL, NF, :], 1.0, C["decay"][0:TAIL, 1:2], ALU.add, ALU.mult).then_inc(s_gs, 1)
            dve.wait_ge(s_gs, 2)
            for h in range(NH):
                for j in range(1, PER, 2):
                    bank = ps[4 + (PER * h + j) % 4]
                    dve.wait_ge(s_bank, PER * h + j + 1)
                    if j < 4:
                        a, b = SPLIT[j // 2]
                        r0 = DB * (j // 2)
                        nc.vector.tensor_copy(kqT_b[r0:r0 + DB, 0:b - a, h], bank[r0:r0 + DB, 0:b - a]).then_inc(s_evD, 1)
                    else:
                        k, n = j - 4, BLK[j - 4]
                        if h:
                            dve.wait_ge(s_row, 32 * h)
                        nc.vector.tensor_copy(rows[0:n, k, 0:D], bank[0:n, 0:D])
                        nc.vector.tensor_scalar(rows[0:n, k, D:2 * D], bank[0:n, D:2 * D], gscale[0:n, k, h:h + 1], None, ALU.mult).then_inc(s_evD, 1)

        @block.tensor
        def _(pe):
            pe.wait_ge(s_w, 96)
            for n, w in enumerate((wk, wv)):
                for m in range(4):
                    nc.tensor.transpose(ps[2 * n][:, m * P:(m + 1) * P], w[:, m, 0:DA], ident[:, :])
                    nc.tensor.transpose(ps[2 * n + 1][0:DB, m * P:(m + 1) * P], w[:, m, DA:D], ident[:, :])
            for m in range(4):
                bank, c = ps[4 + m // 2], m % 2 * D
                nc.tensor.transpose(bank[:, c:c + DA], wo[:, 0, m * P:(m + 1) * P], ident[:, :])
                nc.tensor.transpose(bank[:, c + DA:c + D], wo[0:DB, 1, m * P:(m + 1) * P], ident[0:DB, 0:DB])
            nc.tensor.transpose(ps[6][0:DA, 0:NH], wgt[:, 0:DA], ident[0:NH, 0:NH])
            nc.tensor.transpose(ps[6][0:DB, NH:2 * NH], wgt[:, DA:D], ident[0:NH, 0:NH]).then_inc(s_wTp, 1)
            pe.wait_ge(s_x0, 1)
            pe.wait_ge(s_wT, 8)
            for half, (a, b) in enumerate(((0, DA), (DA, D))):
                for k, n in enumerate(BLK):
                    bank, c = ps[2 * half + k // 4], k % 4 * P
                    last = nc.tensor.transpose(bank[0:b - a, c:c + n], h0[0:n, k, a:b], ident[0:n, 0:n])
            last.then_inc(s_x0Tp, 1)
            pe.wait_ge(s_x0T, 1)
            for k, n in enumerate(BLK):
                last = mm(nc, ps[4][0:n, k * NH:(k + 1) * NH], [(x0T[q][:, k * P:k * P + n], wgT[q][:, :]) for q in range(2)])
            last.then_inc(s_gl, 1)
            pe.wait_ge(s_gt, 2)
            for m in range(4):
                for t, wT in enumerate((wkT, wvT)):
                    for n, (a, b) in enumerate(SPLIT):
                        if m:
                            pe.wait_ge(s_kvc, 4 * m - 3 + 2 * t + n)
                        mm(nc, ps[2 * t + n][:, 0:b - a], [(wT[q][:, m, :], x0T[q][:, a:b]) for q in range(2)]).then_inc(s_kv, 1)
                pe.wait_ge(s_kvc, 4 * m + 4)
                for h in (2 * m, 2 * m + 1):
                    r = slice(h % 2 * DK, (h % 2 + 1) * DK)
                    for j in range(PER):
                        n = PER * h + j
                        bank = ps[4 + n % 4]
                        if n >= 4:
                            pe.wait_ge(s_evA if j % 2 == 0 else s_evD, (n - 4) // 2 + 1)
                        if j < 4:
                            a, b = SPLIT[j // 2]
                            if j % 2 == 0:
                                out, wcols = bank[:, 0:b - a], slice(0, DA)
                            else:
                                out, wcols = bank[DB * (j // 2):DB * (j // 2) + DB, 0:b - a], slice(DA, D)
                            last = nc.tensor.matmul(out, wq[r, m, wcols], kvT[r, 0, a:b], start=True, stop=True)
                        else:
                            k, s = j - 4, BLK[j - 4]
                            nc.tensor.matmul(bank[0:s, 0:D], kvT[r, 0, k * P:k * P + s], wq[r, m, :], start=True, stop=True)
                            last = nc.tensor.matmul(bank[0:s, D:2 * D], kvT[r, 1, k * P:k * P + s], woT[r, m, :], start=True, stop=True)
                        last.then_inc(s_bank, 1)
    nc.clear_and_free_semaphores(sems)
    nc.all_engine_barrier()


RING = 3


def done(c):
    return c + 1 + RING


def free(c):
    return c + 1


def tokens(nc, I, scratch, C, W):
    ctx = ExitStack()
    sems = []
    with ctx:
        def sb(name, shape, dt=F32):
            return ctx.enter_context(nc.sbuf_tensor(name, shape, dt))

        def ring(name, shape, dt=F32):
            return [sb(f"{name}_{n}", shape, dt) for n in range(RING)]

        def pb(name, shape, dt=F32):
            return ctx.enter_context(nc.psum_tensor(name, shape, dt))

        def sem(name):
            sems.append(nc.alloc_semaphore(name))
            return sems[-1]

        h = ring("h", [P, 2, D])
        x1 = ring("x1", [P, 2, D])
        hx = ring("hx", [P, 2, D])
        h2 = ring("h2s", [P, 2, D])
        x2 = ring("x2", [P, 2, D])
        x2r = ring("x2r", [P, 2, D])
        st1 = ring("st1", [P, 2, 6])
        mv1 = ring("mv1", [P, 2, 2])
        ve1 = ring("ve1", [P, 2])
        nm1 = ring("nm1", [P, 2])
        nb1 = ring("nb1", [P, 2])
        rs1 = ring("rs1", [P, 2])
        st2 = ring("st2", [P, 2, 6])
        mv2 = ring("mv2", [P, 2, 2])
        ve2 = ring("ve2", [P, 2])
        nm2 = ring("nm2", [P, 2])
        nb2 = ring("nb2", [P, 2])
        rs2 = ring("rs2", [P, 2])
        x1a = ring("x1a", [DA, 2 * P])
        x1b = ring("x1b", [DB, 2 * P])
        x2a = ring("x2a", [DA, 2 * P])
        x2b = ring("x2b", [DB, 2 * P])
        kqa = ring("kqa", [DA, P])
        kqb = ring("kqb", [DB, P])
        kqvo = ring("kqvo", [P, 2 * D])
        sc = ring("sc", [P, 2 * P])
        Ma = ring("Ma", [DA, D])
        Mb = ring("Mb", [DB, D])
        Msa = ring("Msa", [DA, D])
        Msb = ring("Msb", [DB, D])
        lg = ring("lg", [P, 2, NE + 1])
        mx = ring("mx", [P, 2, 8])
        ix = ring("ix", [P, 2, 8], U32)
        ixf = ring("ixf", [P, 2, 2])
        oh = ring("oh", [P, 4, NE])
        ohs = ring("ohs", [P, 2, NE], BF16)
        ld = ring("ld", [P, NE], BF16)
        ldc = ring("ldc", [P, NE])
        pb8 = ring("pb8", [P, 2, NE])
        prod = ring("prod", [P, 4, NE])
        slf = ring("slf", [P, 4])
        slu = ring("slu", [P, 4], U32)

        ps_x1, ps_sc, ps_o, ps_m, ps_x2, ps_lg, ps_pos = [pb(n, [P, 512]) for n in
                                                          ("ps_x1", "ps_sc", "ps_o", "ps_m", "ps_x2", "ps_lg", "ps_pos")]

        s_h_in = [sem(f"h_in{n}") for n in range(RING)]
        s_k_in = [sem(f"k_in{n}") for n in range(RING)]
        s_h2_out = [sem(f"h2_out{n}") for n in range(RING)]
        s_x2T_out = [sem(f"x2T_out{n}") for n in range(RING)]
        s_scat = [sem(f"scattered{n}") for n in range(RING)]
        s_init = sem("init")
        s_apart_dve, s_apart_pool = sem("apart_dve"), sem("apart_pool")
        s_st1, s_ag1, s_ve1, s_rs1 = sem("stats1"), sem("aggr1"), sem("var1"), sem("rstd1")
        s_nb1, s_nb2 = sem("shift1"), sem("shift2")
        s_x1, s_hx = sem("x1"), sem("hx")
        s_x1Tp, s_x1T = sem("x1T_product"), sem("x1T")
        s_scp, s_sc = sem("score_product"), sem("scores")
        s_om, s_mp = sem("attention_product"), sem("write_product")
        s_Ms, s_M = sem("M_scaled"), sem("M")
        s_h2 = sem("h2_done")
        s_st2, s_ag2, s_ve2, s_rs2 = sem("stats2"), sem("aggr2"), sem("var2"), sem("rstd2")
        s_x2, s_x2r = sem("x2_done"), sem("x2_rows")
        s_x2Tp, s_x2T = sem("x2T_product"), sem("x2T_copied")
        s_lgp, s_lg = sem("logit_product"), sem("logits")
        s_mx, s_ix, s_ixf = sem("top8"), sem("top8_index"), sem("index_float")
        s_oh, s_ohs = sem("onehot"), sem("onehot_sum")
        s_ld = sem("load_done")
        s_posp, s_pb8, s_prod, s_slf, s_slot = sem("pos_product"), sem("pos_base"), sem("pos_chosen"), sem("slot_float"), sem("slot")
        block = ctx.enter_context(nc.Block())
        ident = C["ident"]
        c16 = DECAY ** STEP
        hb = scratch["hbuf"]

        def at(dram, c):
            return dram[bass.ds(c, 1)].rearrange("c a b -> (c a) b")

        @block.sync
        def _(sp):
            def loads(c, b, r):
                sp.wait_ge(s_x1, free(c))
                sp.wait_ge(s_hx, free(c))
                src = hb[bass.ds(c * STEP, STEP), :, :].rearrange("t (k a) d -> (t k) (a d)", a=2)
                sp.dma_start(h[b][:, :, :].rearrange("p a d -> p (a d)"), src).then_inc(s_h_in[b], 16)

            def tables(c, b, r):
                sp.wait_ge(s_om, free(c))
                sp.dma_start(kqa[b][:, :], at(scratch["kqT"], c)[0:DA, :]).then_inc(s_k_in[b], 16)
                sp.dma_start(kqb[b][:, :], at(scratch["kqT"], c)[DA:D, :]).then_inc(s_k_in[b], 16)
                src = scratch["kqvo"][bass.ds(c * STEP, STEP), :, :].rearrange("s h d -> (s h) d")
                sp.dma_start(kqvo[b][:, :], src).then_inc(s_k_in[b], 16)

            def stores(c, b, r):
                sp.wait_ge(s_h2, done(c))
                sp.dma_start(at(scratch["h2"], c), h2[b][:, :, :].rearrange("p a d -> p (a d)")).then_inc(s_h2_out[b], 16)
                sp.wait_ge(s_x2T, done(c))
                sp.dma_start(at(scratch["x2T"], c)[0:DA, :], x2a[b][:, :]).then_inc(s_x2T_out[b], 16)
                sp.dma_start(at(scratch["x2T"], c)[DA:D, :], x2b[b][:, :]).then_inc(s_x2T_out[b], 16)
            for b in range(RING):
                sp.sem_inc(s_h2_out[b], 16)
                sp.sem_inc(s_x2T_out[b], 32)
            pipeline(sp, NCH, RING, [(0, loads), (6, stores), (1, tables)], peel=2)
            for b in range(RING):
                sp.wait_ge(s_h2_out[b], 16 * (NCH // RING) + 16)
                sp.wait_ge(s_x2T_out[b], 32 * (NCH // RING) + 32)

        @block.gpsimd
        def _(pool):
            for s in (s_rs1, s_rs2, s_nb1, s_nb2):
                pool.sem_inc(s, RING)
            pool.wait_ge(s_init, 1)

            def norm1(c, b, r):
                pool.wait_ge(s_ve1, done(c))
                pool.wait_ge(s_x1, free(c))
                nc.gpsimd.tensor_tensor(rs1[b][:, :], ve1[b][:, :], C["neghalf"][:, 0:2], ALU.pow).then_inc(s_rs1, 1)
                pool.wait_ge(s_rs1, done(c))
                nc.gpsimd.tensor_tensor(nb1[b][:, :], nm1[b][:, :], rs1[b][:, :], ALU.mult).then_inc(s_nb1, 1)

            def norm2(c, b, r):
                pool.wait_ge(s_ve2, done(c))
                pool.wait_ge(s_x2, free(c))
                nc.gpsimd.tensor_tensor(rs2[b][:, :], ve2[b][:, :], C["neghalf"][:, 0:2], ALU.pow).then_inc(s_rs2, 1)
                pool.wait_ge(s_rs2, done(c))
                nc.gpsimd.tensor_tensor(nb2[b][:, :], nm2[b][:, :], rs2[b][:, :], ALU.mult).then_inc(s_nb2, 1)

            def scatter(c, b, r):
                pool.wait_ge(s_slot, done(c))
                pool.wait_ge(s_x2r, done(c))
                pool.sem_inc(s_apart_pool, 1)
                for j in range(4):
                    nc.gpsimd.indirect_dma_start(scratch["xs"], bass.IndirectOffsetOnAxis(ap=slu[b][:, j:j + 1], axis=0),
                                                 x2r[b][:, j // 2, :], None).then_inc(s_scat[b], 16)
            pipeline(pool, NCH, RING, [(4, norm2), (0, norm1), (7, scatter)], peel=3)
            for b in range(RING):
                pool.wait_ge(s_scat[b], 64 * (NCH // RING))

        @block.scalar
        def _(act):
            for s in (s_x1T, s_x2T, s_x2r, s_Ms, s_x1, s_x2):
                act.sem_inc(s, RING)
            act.wait_ge(s_init, 1)

            def decay_state(c, b, r):
                act.wait_ge(s_M, done(c - 1))
                nc.scalar.activation(Msa[b][:, :], Ma[b][:, :], ACT.Copy, scale=c16)
                nc.scalar.activation(Msb[b][:, :], Mb[b][:, :], ACT.Copy, scale=c16).then_inc(s_Ms, 1)

            def x2_columns(c, b, r):
                act.wait_ge(s_x2Tp, done(c))
                act.wait_ge(s_x2T_out[b], 32 * r + 32)
                nc.scalar.activation(x2a[b][:, :], ps_x2[:, 0:2 * P], ACT.Copy)
                nc.scalar.activation(x2b[b][:, :], ps_x2[0:DB, 2 * P:4 * P], ACT.Copy).then_inc(s_x2T, 1)

            def normed1(c, b, r):
                act.wait_ge(s_nb1, done(c))
                act.wait_ge(s_hx, free(c))
                act.wait_ge(s_x1Tp, free(c))
                for half in range(2):
                    last = nc.scalar.activation(x1[b][:, half, :], h[b][:, half, :], ACT.Identity,
                                                bias=nb1[b][:, half:half + 1], scale=rs1[b][:, half:half + 1])
                last.then_inc(s_x1, 1)

            def normed2(c, b, r):
                act.wait_ge(s_nb2, done(c))
                act.wait_ge(s_x2r, free(c))
                act.wait_ge(s_x2Tp, free(c))
                for half in range(2):
                    last = nc.scalar.activation(x2[b][:, half, :], h2[b][:, half, :], ACT.Identity,
                                                bias=nb2[b][:, half:half + 1], scale=rs2[b][:, half:half + 1])
                last.then_inc(s_x2, 1)

            def x2_rows(c, b, r):
                act.wait_ge(s_x2, done(c))
                if not (isinstance(r, int) and r == 0):
                    act.wait_ge(s_scat[b], 64 * r)
                nc.scalar.activation(x2r[b][:, :, :], x2[b][:, :, :], ACT.Copy).then_inc(s_x2r, 1)

            def x1_columns(c, b, r):
                act.wait_ge(s_x1Tp, done(c))
                act.wait_ge(s_om, free(c))
                nc.scalar.activation(x1a[b][:, :], ps_x1[:, 0:2 * P], ACT.Copy)
                nc.scalar.activation(x1b[b][:, :], ps_x1[0:DB, 2 * P:4 * P], ACT.Copy).then_inc(s_x1T, 1)
            pipeline(act, NCH, RING, [(1, normed1), (5, normed2), (2, decay_state), (6, x2_rows), (1, x1_columns), (5, x2_columns)], peel=3)

        @block.vector
        def _(dve):
            nc.vector.memset(Ma[0][:, :], 0.0)
            nc.vector.memset(Mb[0][:, :], 0.0)
            nc.vector.memset(ld[0][:, :], 0.0).then_inc(s_init, 1)
            dve.wait_ge(s_init, 1)
            for s in (s_st1, s_ag1, s_ve1, s_hx, s_sc, s_M, s_h2, s_st2, s_ag2, s_ve2, s_lg, s_mx, s_ix,
                      s_ixf, s_oh, s_ohs, s_ld, s_pb8, s_prod, s_slf, s_slot):
                dve.sem_inc(s, RING)

            def stats1(c, b, r):
                dve.wait_ge(s_h_in[b], 16 * r + 16)
                nc.vector.bn_stats(st1[b][:, 0, :], h[b][:, 0, :])
                nc.vector.bn_stats(st1[b][:, 1, :], h[b][:, 1, :]).then_inc(s_st1, 1)

            def moments1(c, b, r):
                dve.wait_ge(s_st1, done(c))
                dve.sem_inc(s_apart_dve, 1)
                nc.vector.bn_aggr(mv1[b][:, 0, :], st1[b][:, 0, :])
                nc.vector.bn_aggr(mv1[b][:, 1, :], st1[b][:, 1, :]).then_inc(s_ag1, 1)

            def variance1(c, b, r):
                dve.wait_ge(s_ag1, done(c))
                dve.wait_ge(s_nb1, free(c))
                nc.vector.tensor_scalar(nm1[b][:, :], mv1[b][:, :, 0], -1.0, None, ALU.mult)
                nc.vector.tensor_scalar(ve1[b][:, :], mv1[b][:, :, 1], LN_EPS, None, ALU.add).then_inc(s_ve1, 1)

            def residual_own(c, b, r):
                dve.wait_ge(s_x1, done(c))
                dve.wait_ge(s_h2, free(c))
                nc.vector.tensor_tensor(hx[b][:, :, :], h[b][:, :, :], x1[b][:, :, :], ALU.add).then_inc(s_hx, 1)

            def masked(c, b, r):
                dve.wait_ge(s_scp, done(c))
                nc.vector.tensor_tensor(sc[b][:, :], ps_sc[:, 0:2 * P], C["maskf"][:, :, :, :].rearrange("p a s b -> p (a s b)"),
                                        ALU.mult).then_inc(s_sc, 1)

            def state(c, b, r):
                dve.wait_ge(s_mp, done(c))
                dve.wait_ge(s_Ms, done(c))
                dve.wait_ge(s_om, done(c - 2))
                n = (b + 1) % RING
                nc.vector.scalar_tensor_tensor(out=Ma[n][:, :], in0=ps_m[:, 0:D], scalar=c16, in1=Msa[b][:, :],
                                               op0=ALU.mult, op1=ALU.add)
                nc.vector.scalar_tensor_tensor(out=Mb[n][:, :], in0=ps_m[0:DB, D:2 * D], scalar=c16, in1=Msb[b][:, :],
                                               op0=ALU.mult, op1=ALU.add).then_inc(s_M, 1)

            def residual(c, b, r):
                dve.wait_ge(s_om, done(c))
                dve.wait_ge(s_hx, done(c))
                dve.wait_ge(s_x2, free(c))
                dve.wait_ge(s_h2_out[b], 16 * r + 16)
                nc.vector.scalar_tensor_tensor(out=h2[b][:, :, :], in0=ps_o[:, 0:2 * D].rearrange("p (a d) -> p a d", a=2),
                                               scalar=C["decay"][:, 0:1], in1=hx[b][:, :, :],
                                               op0=ALU.mult, op1=ALU.add).then_inc(s_h2, 1)

            def stats2(c, b, r):
                dve.wait_ge(s_h2, done(c))
                nc.vector.bn_stats(st2[b][:, 0, :], h2[b][:, 0, :])
                nc.vector.bn_stats(st2[b][:, 1, :], h2[b][:, 1, :]).then_inc(s_st2, 1)

            def moments2(c, b, r):
                dve.wait_ge(s_st2, done(c))
                dve.sem_inc(s_apart_dve, 1)
                nc.vector.bn_aggr(mv2[b][:, 0, :], st2[b][:, 0, :])
                nc.vector.bn_aggr(mv2[b][:, 1, :], st2[b][:, 1, :]).then_inc(s_ag2, 1)

            def variance2(c, b, r):
                dve.wait_ge(s_ag2, done(c))
                dve.wait_ge(s_nb2, free(c))
                nc.vector.tensor_scalar(nm2[b][:, :], mv2[b][:, :, 0], -1.0, None, ALU.mult)
                nc.vector.tensor_scalar(ve2[b][:, :], mv2[b][:, :, 1], LN_EPS, None, ALU.add).then_inc(s_ve2, 1)

            def logits_out(c, b, r):
                dve.wait_ge(s_lgp, done(c))
                nc.vector.tensor_copy(lg[b][:, :, :], ps_lg[:, 0:2 * (NE + 1)].rearrange("p (a e) -> p a e", a=2)).then_inc(s_lg, 1)

            def highest(c, b, r):
                dve.wait_ge(s_lg, done(c))
                dve.sem_inc(s_apart_dve, 1)
                nc.vector.max(mx[b][:, 0, :], lg[b][:, 0, 0:NE])
                nc.vector.max(mx[b][:, 1, :], lg[b][:, 1, 0:NE]).then_inc(s_mx, 1)

            def chosen(c, b, r):
                dve.wait_ge(s_mx, done(c))
                dve.sem_inc(s_apart_dve, 1)
                nc.vector.max_index(ix[b][:, 0, :], mx[b][:, 0, :], lg[b][:, 0, 0:NE])
                nc.vector.max_index(ix[b][:, 1, :], mx[b][:, 1, :], lg[b][:, 1, 0:NE]).then_inc(s_ix, 1)
                nc.vector.tensor_tensor(C["pre"][:, bass.ds(2 * c, 2), 0:1], mx[b][:, :, 0:1], mx[b][:, :, 1:2], ALU.subtract)
                nc.vector.tensor_scalar(C["pre"][:, bass.ds(2 * c, 2), 1:2], lg[b][:, :, NE:NE + 1], C["sgb"][:, 0:1], None, ALU.add)

            def index(c, b, r):
                dve.wait_ge(s_ix, done(c))
                nc.vector.tensor_copy(ixf[b][:, :, :], ix[b][:, :, 0:2]).then_inc(s_ixf, 1)

            def onehot(c, b, r):
                dve.wait_ge(s_ixf, done(c))
                nc.vector.tensor_tensor(oh[b][:, :, :], C["iota8"][:, :].unsqueeze(1).to_broadcast([P, 4, NE]),
                                        ixf[b][:, :, :].rearrange("p a (k o) -> p (a k) o", o=1).to_broadcast([P, 4, NE]),
                                        ALU.is_equal).then_inc(s_oh, 1)

            def onehot_sum(c, b, r):
                dve.wait_ge(s_oh, done(c))
                pair = oh[b][:, :, :].rearrange("p (a k) e -> p a k e", k=2)
                nc.vector.tensor_tensor(ohs[b][:, :, :], pair[:, :, 0, :], pair[:, :, 1, :], ALU.add).then_inc(s_ohs, 1)

            def load_chunk(c, b, r):
                dve.wait_ge(s_ohs, done(c))
                nc.vector.tensor_tensor(ldc[b][:, :], ohs[b][:, 0, :], ohs[b][:, 1, :], ALU.add).then_inc(s_ld, 1)

            def load_sum(c, b, r):
                n = (b + 1) % RING
                dve.wait_ge(s_ld, 2 * c + RING + 1)
                nc.vector.tensor_tensor(ld[n][:, :], ld[b][:, :], ldc[b][:, :], ALU.add).then_inc(s_ld, 1)

            def bases(c, b, r):
                dve.wait_ge(s_posp, done(c))
                nc.vector.tensor_tensor(pb8[b][:, :, :], ps_pos[:, 0:2 * NE].rearrange("p (a e) -> p a e", a=2),
                                        C["ebase"][:, :].unsqueeze(1).to_broadcast([P, 2, NE]), ALU.add).then_inc(s_pb8, 1)

            def chosen_bases(c, b, r):
                dve.wait_ge(s_pb8, done(c))
                nc.vector.tensor_tensor(prod[b][:, :, :].rearrange("p (a k) e -> p a k e", k=2),
                                        oh[b][:, :, :].rearrange("p (a k) e -> p a k e", k=2),
                                        pb8[b][:, :, :].unsqueeze(2).to_broadcast([P, 2, 2, NE]), ALU.mult).then_inc(s_prod, 1)

            def slot_sums(c, b, r):
                dve.wait_ge(s_prod, done(c))
                nc.vector.reduce_sum(slf[b][:, :], prod[b][:, :, :], AX.X).then_inc(s_slf, 1)

            def slots(c, b, r):
                dve.wait_ge(s_slf, done(c))
                nc.vector.tensor_copy(C["slots"][:, bass.ds(c, 1), :].rearrange("p c k -> p (c k)"), slf[b][:, :])
                if not (isinstance(r, int) and r == 0):
                    dve.wait_ge(s_scat[b], 64 * r)
                nc.vector.tensor_copy(slu[b][:, :], slf[b][:, :]).then_inc(s_slot, 1)
            pipeline(dve, NCH, RING, [(7, load_chunk), (4, residual), (7, load_sum), (7, bases), (4, stats2),
                                      (6, logits_out), (7, chosen_bases), (4, moments2), (6, highest), (7, slot_sums),
                                      (4, variance2), (6, chosen), (7, slots), (2, residual_own), (2, masked), (6, index), (0, stats1),
                                      (6, onehot), (2, state), (6, onehot_sum), (0, moments1), (0, variance1)], peel=4)
            dve.wait_ge(s_ld, 2 * NCH + RING)
            nc.vector.tensor_copy(C["load"][:, :], ld[NCH % RING][:, :])

        @block.tensor
        def _(pe):
            for s in (s_x1Tp, s_scp, s_om, s_mp, s_x2Tp, s_lgp, s_posp):
                pe.sem_inc(s, RING)
            pe.wait_ge(s_init, 1)

            def columns(out, x, s):
                for half in range(2):
                    nc.tensor.transpose(out[:, half * P:(half + 1) * P], x[:, half, 0:DA], ident[:, :])
                    last = nc.tensor.transpose(out[0:DB, (2 + half) * P:(3 + half) * P], x[:, half, DA:D], ident[:, :])
                last.then_inc(s, 1)

            def x1_transposes(c, b, r):
                pe.wait_ge(s_x1, done(c))
                pe.wait_ge(s_x1T, done(c - 1))
                columns(ps_x1, x1[b], s_x1Tp)

            def scores(c, b, r):
                pe.wait_ge(s_x1T, done(c))
                pe.wait_ge(s_k_in[b], 48 * r + 48)
                pe.wait_ge(s_sc, done(c - 1))
                mm(nc, ps_sc[:, 0:2 * P], [(kqa[b][:, :], x1a[b][:, :]), (kqb[b][:, :], x1b[b][:, :])]).then_inc(s_scp, 1)

            def attend(c, b, r):
                pe.wait_ge(s_sc, done(c))
                pe.wait_ge(s_M, done(c - 1))
                pe.wait_ge(s_h2, done(c - 1))
                for half in range(2):
                    t = slice(half * P, (half + 1) * P)
                    last = mm(nc, ps_o[:, half * D:(half + 1) * D],
                       [(sc[b][:, t], kqvo[b][:, D:2 * D]), (x1a[b][:, t], Ma[b][:, :]), (x1b[b][:, t], Mb[b][:, :])])
                last.then_inc(s_om, 1)

            def writes(c, b, r):
                pe.wait_ge(s_k_in[b], 48 * r + 48)
                pe.wait_ge(s_M, done(c - 1))
                mm(nc, ps_m[:, 0:D], [(kqvo[b][:, 0:DA], kqvo[b][:, D:2 * D])])
                mm(nc, ps_m[0:DB, D:2 * D], [(kqvo[b][:, DA:D], kqvo[b][:, D:2 * D])]).then_inc(s_mp, 1)

            def x2_transposes(c, b, r):
                pe.wait_ge(s_x2, done(c))
                pe.wait_ge(s_x2T, done(c - 1))
                columns(ps_x2, x2[b], s_x2Tp)

            def logits(c, b, r):
                pe.wait_ge(s_x2T, done(c))
                pe.wait_ge(s_lg, done(c - 1))
                for half in range(2):
                    t = slice(half * P, (half + 1) * P)
                    last = mm(nc, ps_lg[:, half * (NE + 1):(half + 1) * (NE + 1)],
                              [(x2a[b][:, t], W["rw_a"][:, :]), (x2b[b][:, t], W["rw_b"][:, :])])
                last.then_inc(s_lgp, 1)

            def positions(c, b, r):
                pe.wait_ge(s_ohs, done(c))
                pe.wait_ge(s_ld, 2 * c + RING)
                pe.wait_ge(s_pb8, done(c - 1))
                mm(nc, ps_pos[:, 0:NE], [(C["tri"][:, :], ohs[b][:, 0, :]), (C["ones"][:, :], ld[b][:, :])])
                mm(nc, ps_pos[:, NE:2 * NE], [(C["tri"][:, :], ohs[b][:, 1, :]), (C["ones"][:, :], ohs[b][:, 0, :]),
                                              (C["ones"][:, :], ld[b][:, :])]).then_inc(s_posp, 1)
            pipeline(pe, NCH, RING, [(2, scores), (2, writes), (6, logits), (7, positions), (1, x1_transposes), (5, x2_transposes),
                                (3, attend)], peel=3)
    nc.clear_and_free_semaphores(sems)
    nc.all_engine_barrier()


GATE_UP, DOWN = 2, 5
FIELDS = 7
TURN = 4


def tile_done(t):
    return t + 1 + TURN


def experts(nc, scratch, C, W):
    ctx = ExitStack()
    sems = []
    with ctx:
        def sb(name, shape, dt=F32):
            return ctx.enter_context(nc.sbuf_tensor(name, shape, dt))

        def pair(name, shape, dt=F32):
            return [sb(f"{name}_{n}", shape, dt) for n in range(2)]

        def pb(name, shape, dt=F32):
            return ctx.enter_context(nc.psum_tensor(name, shape, dt))

        def sem(name):
            sems.append(nc.alloc_semaphore(name))
            return sems[-1]

        zrow = sb("zrow", [P, D])
        ident_r = sb("ident_r", [P, P], F32R)
        cnt = sb("cnt", [P, NE])
        padf = sb("padf", [P, NE])
        padu = sb("padu", [P, NE], U32)
        nti = sb("nti", [P, NE], I32)
        ntf = sb("ntf", [P, NE])
        ends = sb("ends", [1, NE])
        tno = sb("tno", [1, NTILE])
        past = sb("past", [1, NE, NTILE])
        leap = sb("leap", [1, NE, NTILE])
        ef = sb("ef", [1, NTILE])
        rf = sb("rf", [1, NTILE])
        tile_e = sb("tile_e", [1, NTILE], I32)
        efp = sb("efp", [1, 2 + NTILE // TURN, TURN])
        pack = sb("pack", [1, NTILE // TURN])
        turn_e = sb("turn_e", [1, NTILE // TURN], I32)
        tile_row = sb("tile_row", [1, NTILE], I32)
        xt = [sb(f"xt_{n}", [P, D]) for n in range(TURN)]
        xs2 = pair("xs2", [P, 2 * D], F32R)
        xc = pair("xc", [P, 3, P], F32R)
        sg = pair("sg", [P, HE])
        hm = pair("hm", [P, HE])
        hs2 = pair("hs2", [P, 2 * HE], F32R)
        hc = pair("hc", [P, 3, P], F32R)
        y = [sb(f"y_{n}", [P, D]) for n in range(TURN)]
        ps_xT = [pb(f"ps_xT{n}", [P, 512]) for n in range(2)]
        ps_gu = [pb(f"ps_gu{n}", [P, 512]) for n in range(2)]
        ps_hT = [pb(f"ps_hT{n}", [P, 512]) for n in range(2)]
        ps_y = [pb(f"ps_y{n}", [P, 512]) for n in range(2)]

        s_cntp, s_step, s_iota, s_pad, s_padded, s_table = (sem(n) for n in
                                                            ("count_product", "table_step", "tile_numbers", "pad_rows", "padded", "table"))
        s_zrow = sem("zero_row")
        s_x_in = [sem(f"x_in{n}") for n in range(TURN)]
        s_y_out = [sem(f"y_out{n}") for n in range(TURN)]
        s_xh, s_xl, s_xT, s_xc, s_gu, s_sg, s_hm = (sem(n) for n in
                                                    ("x_lead", "x_rest", "xT", "x_copied", "gate_up", "silu", "hidden"))
        s_hh, s_hl, s_hT, s_hc, s_yp, s_y = (sem(n) for n in ("h_lead", "h_rest", "hT", "h_copied", "down", "y_copied"))
        block = ctx.enter_context(nc.Block())

        def rest(eng, split, whole):
            lead = split[:, 0:D].bitcast(F32)
            eng.tensor_tensor(split[:, D:2 * P], whole[:, DA:D], lead[:, DA:D], ALU.subtract)
            return eng.tensor_tensor(split[:, 2 * P:2 * D], whole[:, 0:DA], lead[:, 0:DA], ALU.subtract)

        @block.gpsimd
        def _(pool):
            nc.gpsimd.iota(tno[:, :], pattern=[[1, NTILE]], base=0, channel_multiplier=0,
                           allow_small_or_imprecise_dtypes=True).then_inc(s_iota, 1)
            nc.gpsimd.memset(zrow[:, :], 0.0).then_inc(s_zrow, 1)
            pool.wait_ge(s_zrow, 1)
            pool.wait_ge(s_pad, 1)
            for e in range(NE):
                nc.gpsimd.indirect_dma_start(scratch["xs"], bass.IndirectOffsetOnAxis(ap=padu[:, e:e + 1], axis=0),
                                             zrow[:, :], None).then_inc(s_padded, 16)
            pool.wait_ge(s_padded, 16 * NE)
            pool.sem_inc(s_xl, TURN)

            def x_rest(t, b, r):
                pool.wait_ge(s_xh, tile_done(t))
                rest(nc.gpsimd, xs2[b % 2], xt[b]).then_inc(s_xl, 1)
            pipeline(pool, NTILE, TURN, [(0, x_rest)])

        @block.sync
        def _(sp):
            for n in range(TURN):
                sp.sem_inc(s_y_out[n], 16)
            sp.wait_ge(s_padded, 16 * NE)
            sp.wait_ge(s_table, 1)

            def load(t, b, r):
                if not (isinstance(t, int) and t < TURN):
                    sp.wait_ge(s_xl, tile_done(t - TURN))
                row = sp.value_load(tile_row[0:1, bass.ds(t, 1)], min_val=0, max_val=ROWS - P)
                sp.dma_start(xt[b][:, :], scratch["xs"][bass.ds(row, P), :]).then_inc(s_x_in[b], 16)

            def store(t, b, r):
                sp.wait_ge(s_y, tile_done(t))
                sp.dma_start(scratch["ys"][bass.ds(t * P, P), :], y[b][:, :]).then_inc(s_y_out[b], 16)
            pipeline(sp, NTILE, TURN, [(7, store), (0, load)], peel=2)
            for n in range(TURN):
                sp.wait_ge(s_y_out[n], 16 * (NTILE // TURN) + 16)

        @block.scalar
        def _(act):
            for s in (s_xh, s_sg, s_hh, s_hc, s_y):
                act.sem_inc(s, TURN)

            def x_lead(t, b, r):
                act.wait_ge(s_x_in[b], 16 * r + 16)
                act.wait_ge(s_xT, tile_done(t - 2))
                nc.scalar.activation(xs2[b % 2][:, 0:D], xt[b][:, :], ACT.Copy).then_inc(s_xh, 1)

            def silu(t, b, r):
                act.wait_ge(s_gu, tile_done(t))
                act.wait_ge(s_hm, tile_done(t - 2))
                nc.scalar.activation(sg[b % 2][:, :], ps_gu[b % 2][:, 0:HE], ACT.Silu).then_inc(s_sg, 1)

            def h_lead(t, b, r):
                act.wait_ge(s_hm, tile_done(t))
                act.wait_ge(s_hT, tile_done(t - 2))
                nc.scalar.activation(hs2[b % 2][:, 0:HE], hm[b % 2][:, :], ACT.Copy).then_inc(s_hh, 1)

            def h_copy(t, b, r):
                act.wait_ge(s_hT, tile_done(t))
                act.wait_ge(s_yp, tile_done(t - 2))
                nc.scalar.activation(hc[b % 2][:, :, :].rearrange("p a n -> p (a n)"), ps_hT[b % 2][:, 0:3 * P], ACT.Copy).then_inc(s_hc, 1)

            def y_copy(t, b, r):
                act.wait_ge(s_yp, tile_done(t))
                act.wait_ge(s_y_out[b], 16 * r + 16)
                nc.scalar.activation(y[b][:, :], ps_y[b % 2][:, 0:D], ACT.Copy).then_inc(s_y, 1)
            pipeline(act, NTILE, TURN, [(3, h_lead), (0, x_lead), (2, silu), (5, y_copy), (4, h_copy)], peel=2)

        @block.vector
        def _(dve):
            n = [0]

            def step(ins):
                n[0] += 1
                ins.then_inc(s_step, 1)
                dve.wait_ge(s_step, n[0])
            step(nc.vector.tensor_copy(ident_r[:, :], C["ident"][:, :]))
            dve.wait_ge(s_cntp, 1)
            step(nc.vector.tensor_copy(cnt[:, :], ps_xT[0][:, 0:NE]))
            step(nc.vector.tensor_tensor(padf[:, :], cnt[:, :], C["ebase"][:, :], ALU.add))
            nc.vector.tensor_scalar(padu[:, :], padf[:, :], C["partf"][:, 0:1], None, ALU.add).then_inc(s_pad, 1)
            step(nc.vector.tensor_scalar(nti[:, :], cnt[:, :], float(P - 1), None, ALU.add))
            step(nc.vector.tensor_scalar(nti[:, :], nti[:, :], P.bit_length() - 1, None, ALU.arith_shift_right))
            step(nc.vector.tensor_copy(ntf[:, :], nti[:, :]))
            step(nc.vector.tensor_copy(ends[:, :], ntf[0:1, :]))
            for e in range(1, NE):
                step(nc.vector.tensor_tensor(ends[:, e:e + 1], ends[:, e:e + 1], ends[:, e - 1:e], ALU.add))
            step(nc.vector.tensor_scalar(C["jump"][:, :], ntf[:, :], -float(P), float(CAP), ALU.mult, ALU.add))
            dve.wait_ge(s_iota, 1)
            step(nc.vector.tensor_tensor(past[:, :, :], tno[:, :].unsqueeze(1).to_broadcast([1, NE, NTILE]),
                                         ends[:, :].unsqueeze(2).to_broadcast([1, NE, NTILE]), ALU.is_ge))
            step(nc.vector.tensor_tensor(leap[:, :, :], past[:, :, :], C["jump"][0:1, :].unsqueeze(2).to_broadcast([1, NE, NTILE]), ALU.mult))
            step(nc.vector.reduce_sum(ef[:, :], past[:, :, :].rearrange("p e t -> p t e"), AX.X))
            step(nc.vector.reduce_sum(rf[:, :], leap[:, :, :].rearrange("p e t -> p t e"), AX.X))
            step(nc.vector.scalar_tensor_tensor(out=rf[:, :], in0=tno[:, :], scalar=float(P), in1=rf[:, :], op0=ALU.mult, op1=ALU.add))
            nc.vector.tensor_copy(tile_row[:, :], rf[:, :])
            nc.vector.memset(efp[:, :, :], 0.0)
            step(nc.vector.memset(pack[:, :], 0.0))
            step(nc.vector.tensor_scalar(efp[:, 2:2 + NTILE // TURN, :].rearrange("p q f -> p (q f)"), ef[:, :],
                                         float(NE - 1), None, ALU.min))
            for k in reversed(range(FIELDS)):
                q, f = divmod(2 * TURN - DOWN + k, TURN)
                step(nc.vector.scalar_tensor_tensor(out=pack[:, :].unsqueeze(2), in0=pack[:, :].unsqueeze(2), scalar=float(NE),
                                                    in1=efp[:, q:q + NTILE // TURN, f:f + 1], op0=ALU.mult, op1=ALU.add))
            step(nc.vector.tensor_copy(turn_e[:, :], pack[:, :]))
            nc.vector.tensor_scalar(tile_e[:, :], ef[:, :], float(NE - 1), None, ALU.min).then_inc(s_table, 1)
            for s in (s_xc, s_hm, s_hl):
                dve.sem_inc(s, TURN)

            def x_copy(t, b, r):
                dve.wait_ge(s_xT, tile_done(t))
                dve.wait_ge(s_gu, tile_done(t - 2))
                nc.vector.tensor_copy(xc[b % 2][:, :, :].rearrange("p a n -> p (a n)"), ps_xT[b % 2][:, 0:3 * P]).then_inc(s_xc, 1)

            def hidden(t, b, r):
                dve.wait_ge(s_sg, tile_done(t))
                dve.wait_ge(s_hl, tile_done(t - 2))
                nc.vector.tensor_tensor(hm[b % 2][:, :], sg[b % 2][:, :], ps_gu[b % 2][:, HE:2 * HE], ALU.mult).then_inc(s_hm, 1)

            def h_rest(t, b, r):
                dve.wait_ge(s_hh, tile_done(t))
                rest(nc.vector, hs2[b % 2], hm[b % 2]).then_inc(s_hl, 1)
            pipeline(dve, NTILE, TURN, [(3, h_rest), (1, x_copy), (2, hidden)])

        @block.tensor
        def _(pe):
            mm(nc, ps_xT[0][:, 0:NE], [(C["ones"][:, :], C["load"][:, :])]).then_inc(s_cntp, 1)
            for s in (s_xT, s_gu, s_hT, s_yp):
                pe.sem_inc(s, TURN)
            pe.wait_ge(s_table, 1)

            def columns(out, split, s):
                for k in range(3):
                    last = mm(nc, out[:, k * P:(k + 1) * P], [(split[:, k * P:(k + 1) * P], ident_r[:, :])])
                last.then_inc(s, 1)

            def product(out, x, wa, wb, at, s):
                mm(nc, out, [(x[:, 0, :], wa[0][:, at]), (x[:, 0, :], wa[1][:, at]), (x[:, 2, :], wa[0][:, at]),
                             (x[:, 1, :], wb[0][:, at]), (x[:, 1, :], wb[1][:, at])]).then_inc(s, 1)

            def x_columns(t, b, r):
                pe.wait_ge(s_xl, tile_done(t))
                pe.wait_ge(s_xc, tile_done(t - 2))
                columns(ps_xT[b % 2], xs2[b % 2], s_xT)

            held = []

            def load_experts(i):
                held[:] = [pe.value_load(turn_e[0:1, bass.ds(i, 1)], min_val=0, max_val=NE ** FIELDS - 1)]

            def expert(t, b, lag):
                if isinstance(t, int):
                    return pe.value_load(tile_e[0:1, bass.ds(t, 1)], min_val=0, max_val=NE - 1)
                field = (b + lag) % TURN + DOWN - lag
                return (held[0] >> (3 * field)) & (NE - 1)

            def gate_up(t, b, r):
                e = expert(t, b, GATE_UP)
                pe.wait_ge(s_xc, tile_done(t))
                pe.wait_ge(s_hm, tile_done(t - 2))
                product(ps_gu[b % 2][:, 0:2 * HE], xc[b % 2], W["gu_a"], W["gu_b"], bass.ds(e * (2 * HE), 2 * HE), s_gu)

            def h_columns(t, b, r):
                pe.wait_ge(s_hl, tile_done(t))
                pe.wait_ge(s_hc, tile_done(t - 2))
                columns(ps_hT[b % 2], hs2[b % 2], s_hT)

            def down(t, b, r):
                e = expert(t, b, DOWN)
                pe.wait_ge(s_hc, tile_done(t))
                pe.wait_ge(s_y, tile_done(t - 2))
                product(ps_y[b % 2][:, 0:D], hc[b % 2], W["dn_a"], W["dn_b"], bass.ds(e * D, D), s_yp)
            pipeline(pe, NTILE, TURN, [(GATE_UP, gate_up), (1, x_columns), (DOWN, down), (4, h_columns)], peel=2,
                     turn=load_experts)
    nc.clear_and_free_semaphores(sems)
    nc.all_engine_barrier()


def combine(nc, scratch, C, W, out):
    ctx = ExitStack()
    sems = []
    MP = HS // (2 * P)
    with ctx:
        def sb(name, shape, dt=F32):
            return ctx.enter_context(nc.sbuf_tensor(name, shape, dt))

        def ring(name, shape, dt=F32):
            return [sb(f"{name}_{n}", shape, dt) for n in range(RING)]

        def pb(name, shape, dt=F32):
            return ctx.enter_context(nc.psum_tensor(name, shape, dt))

        def sem(name):
            sems.append(nc.alloc_semaphore(name))
            return sems[-1]

        th = sb("th", [P, 2 * NCH, 2])
        beta = sb("beta", [P, 2 * NCH])
        gg = sb("gg", [P, 2 * NCH, 2])
        xa = ring("xa", [P, 2 * P])
        xb = ring("xb", [P, 2 * P])
        h2 = ring("h2c", [P, 2, D])
        xah = ring("xah", [P, 2 * P], F32R)
        xal = ring("xal", [P, 2 * P], F32R)
        xbh = ring("xbh", [P, 2 * P], F32R)
        sg = [sb(f"sgs_{n}", [P, 4 * P]) for n in range(MP)]
        pm = [sb(f"pm_{n}", [P, 4 * P]) for n in range(MP)]
        ph = ring("ph", [P, MP, 4 * P], F32R)
        pl = ring("pl", [P, MP, 4 * P], F32R)
        over = sb("over", [P, NE, NCH * 4])
        gidx = sb("gidx", [P, NCH, 4], U32)
        slu = ring("sluc", [P, 4], U32)
        yy = ring("yy", [P, 4, D])
        oo = ring("oo", [P, 2, D])
        ps_g = [pb(f"ps_g{n}", [P, 512]) for n in range(MP)]
        ps_u = [pb(f"ps_u{n}", [P, 512]) for n in range(MP)]
        ps_d = pb("ps_d", [P, 512])

        s_th, s_gs, s_gates = sem("gate_tanhs"), sem("gate_step"), sem("gates_done")
        s_x_in = [sem(f"xc_in{n}") for n in range(RING)]
        s_h2_in = [sem(f"h2c_in{n}") for n in range(RING)]
        s_y_in = [sem(f"yc_in{n}") for n in range(RING)]
        s_o_out = [sem(f"o_out{n}") for n in range(RING)]
        s_over, s_gidx = sem("jumps_chosen"), sem("gather_rows")
        s_slu, s_apart = sem("slots_copied"), sem("apart_c")
        s_xh, s_xl = sem("xc_lead"), sem("xc_rest")
        s_g, s_sg, s_pm, s_ph, s_pl = (sem(n) for n in ("shared_gate_up", "shared_silu", "shared_hidden", "hidden_lead", "hidden_rest"))
        s_d, s_o1, s_o2, s_o = sem("shared_down"), sem("sum1"), sem("sum2"), sem("sum3")
        block = ctx.enter_context(nc.Block())

        def at(dram, c):
            return dram[bass.ds(c, 1)].rearrange("c a b -> (c a) b")

        def done3(c, m):
            return MP * c + m + 1 + MP

        @block.sync
        def _(sp):
            def loads(c, b, r):
                sp.wait_ge(s_xl, free(c))
                sp.dma_start(xa[b][:, :], at(scratch["x2T"], c)[0:DA, :]).then_inc(s_x_in[b], 16)
                for q in (0, DB):
                    sp.dma_start(xb[b][q:q + DB, :], at(scratch["x2T"], c)[DA:D, :]).then_inc(s_x_in[b], 16)
                sp.wait_ge(s_o1, free(c))
                sp.dma_start(h2[b][:, :, :].rearrange("p a d -> p (a d)"), at(scratch["h2"], c)).then_inc(s_h2_in[b], 16)

            def store(c, b, r):
                sp.wait_ge(s_o, done(c))
                steps = T - c * STEP if isinstance(c, int) and c == NCH - 1 else STEP
                for half in range(2):
                    dst = out.rearrange("(k a) t d -> a t k d", a=2)[half, bass.ds(c * STEP, steps), :, :]
                    sp.dma_start(dst, oo[b][0:steps * HB, half, :]).then_inc(s_o_out[b], 16)
            for b in range(RING):
                sp.sem_inc(s_o_out[b], 32)
            pipeline(sp, NCH, RING, [(0, loads), (5, store)], peel=2)
            for b in range(RING):
                sp.wait_ge(s_o_out[b], 32 * (NCH // RING) + 32)

        @block.gpsimd
        def _(pool):
            pool.sem_inc(s_slu, RING)
            pool.wait_ge(s_gidx, 1)

            def gather(c, b, r):
                pool.wait_ge(s_o, free(c))
                nc.gpsimd.tensor_copy(slu[b][:, :], gidx[:, bass.ds(c, 1), :].rearrange("p c k -> p (c k)")).then_inc(s_slu, 1)
                pool.wait_ge(s_slu, done(c))
                pool.sem_inc(s_apart, 1)
                for j in range(4):
                    nc.gpsimd.indirect_dma_start(yy[b][:, j, :], None, scratch["ys"],
                                                 bass.IndirectOffsetOnAxis(ap=slu[b][:, j:j + 1], axis=0)).then_inc(s_y_in[b], 16)
            pipeline(pool, NCH, RING, [(0, gather)])

        @block.scalar
        def _(act):
            nc.scalar.activation(th[:, :, :], C["pre"][:, :, :], ACT.Tanh, scale=0.5).then_inc(s_th, 1)
            act.sem_inc(s_xh, RING)
            for s in (s_sg, s_ph):
                act.sem_inc(s, MP)

            def x_lead(c, b, r):
                act.wait_ge(s_x_in[b], 48 * r + 48)
                act.wait_ge(s_g, done3(c - RING, MP - 1) if not isinstance(c, int) or c >= RING else 1)
                nc.scalar.activation(xah[b][:, :], xa[b][:, :], ACT.Copy)
                nc.scalar.activation(xbh[b][:, :], xb[b][:, :], ACT.Copy).then_inc(s_xh, 1)

            def silus(c, b, r):
                for m in range(MP):
                    act.wait_ge(s_g, done3(c, m))
                    act.wait_ge(s_pm, done3(c - 1, m))
                    nc.scalar.activation(sg[m][:, :], ps_g[m][:, :], ACT.Silu).then_inc(s_sg, 1)
                    act.wait_ge(s_pm, done3(c, m))
                    if m == 0:
                        act.wait_ge(s_d, free(c))
                    nc.scalar.activation(ph[b][:, m, :], pm[m][:, :], ACT.Copy).then_inc(s_ph, 1)

            pipeline(act, NCH, RING, [(0, x_lead), (1, silus)])

        @block.vector
        def _(dve):
            flat = C["slots"][:, :, :].rearrange("p c k -> p (c k)")
            for e in range(1, NE):
                last = nc.vector.tensor_scalar(over[:, e, :], flat, float(e * CAP), C["jump"][:, e - 1:e], ALU.is_ge, ALU.mult)
            last.then_inc(s_over, 1)
            dve.wait_ge(s_over, 1)
            nc.vector.reduce_sum(over[:, 0, :], over[:, 1:NE, :].rearrange("p e n -> p n e"), AX.X).then_inc(s_over, 1)
            dve.wait_ge(s_over, 2)
            nc.vector.tensor_tensor(gidx[:, :, :].rearrange("p c k -> p (c k)"), flat, over[:, 0, :], ALU.subtract).then_inc(s_gidx, 1)
            dve.wait_ge(s_th, 1)
            nc.vector.tensor_scalar(C["gates"][:, :, 2:3], th[:, :, 1:2], 0.5, 0.5, ALU.mult, ALU.add)
            nc.vector.tensor_scalar(beta[:, :].unsqueeze(2), th[:, :, 1:2], -0.5, 0.5, ALU.mult, ALU.add)
            nc.vector.tensor_scalar(gg[:, :, 0:1], th[:, :, 0:1], 0.5, 0.5, ALU.mult, ALU.add)
            nc.vector.tensor_scalar(gg[:, :, 1:2], th[:, :, 0:1], -0.5, 0.5, ALU.mult, ALU.add).then_inc(s_gs, 1)
            dve.wait_ge(s_gs, 1)
            nc.vector.tensor_tensor(C["gates"][:, :, 0:2], gg[:, :, :], beta[:, :].unsqueeze(2).to_broadcast([P, 2 * NCH, 2]),
                                    ALU.mult).then_inc(s_gates, 1)
            dve.wait_ge(s_gates, 1)
            for s in (s_xl, s_o1, s_o2, s_o):
                dve.sem_inc(s, RING)
            for s in (s_pm, s_pl):
                dve.sem_inc(s, MP)

            def x_rest(c, b, r):
                dve.wait_ge(s_xh, done(c))
                nc.vector.tensor_tensor(xal[b][:, :], xa[b][:, :], xah[b][:, :].bitcast(F32), ALU.subtract)
                nc.vector.tensor_tensor(xbh[b][DB:P, :], xb[b][DB:P, :], xbh[b][DB:P, :].bitcast(F32), ALU.subtract).then_inc(s_xl, 1)

            def hiddens(c, b, r):
                for m in range(MP):
                    dve.wait_ge(s_sg, done3(c, m))
                    dve.wait_ge(s_pl, done3(c - 1, m))
                    nc.vector.tensor_tensor(pm[m][:, :], sg[m][:, :], ps_u[m][:, :], ALU.mult).then_inc(s_pm, 1)
                    dve.wait_ge(s_ph, done3(c, m))
                    nc.vector.tensor_tensor(pl[b][:, m, :], pm[m][:, :], ph[b][:, m, :].bitcast(F32), ALU.subtract).then_inc(s_pl, 1)

            def sums(c, b, r):
                dve.wait_ge(s_h2_in[b], 16 * r + 16)
                dve.wait_ge(s_d, done(c))
                dve.wait_ge(s_o_out[b], 32 * r + 32)
                for half in range(2):
                    last = nc.vector.scalar_tensor_tensor(
                        out=oo[b][:, half, :], in0=ps_d[:, half * D:(half + 1) * D],
                        scalar=C["gates"][:, bass.ds(2 * c + half, 1), 2:3].rearrange("p a k -> p (a k)"), in1=h2[b][:, half, :],
                        op0=ALU.mult, op1=ALU.add)
                last.then_inc(s_o1, 1)
                dve.wait_ge(s_y_in[b], 64 * r + 64)
                for k, s_in, s_out in ((0, s_o1, s_o2), (1, s_o2, s_o)):
                    dve.wait_ge(s_in, done(c))
                    for half in range(2):
                        last = nc.vector.scalar_tensor_tensor(
                            out=oo[b][:, half, :], in0=yy[b][:, 2 * half + k, :],
                            scalar=C["gates"][:, bass.ds(2 * c + half, 1), k:k + 1].rearrange("p a k -> p (a k)"), in1=oo[b][:, half, :],
                            op0=ALU.mult, op1=ALU.add)
                    last.then_inc(s_out, 1)
            pipeline(dve, NCH, RING, [(3, sums), (0, x_rest), (1, hiddens)])

        @block.tensor
        def _(pe):
            pe.sem_inc(s_g, MP)
            pe.sem_inc(s_d, RING)

            def gate_up(c, b, r):
                pe.wait_ge(s_xl, done(c))
                (wah, wal), (wbh, wbl) = W["sgu_a"], W["sgu_b"]
                for m in range(MP):
                    pe.wait_ge(s_pm, done3(c - 1, m))
                    for bank, w0 in ((ps_g[m], 0), (ps_u[m], HS)):
                        for k in range(2):
                            f = slice(w0 + (2 * m + k) * P, w0 + (2 * m + k + 1) * P)
                            last = mm(nc, bank[:, k * 2 * P:(k + 1) * 2 * P],
                                      [(wah[:, f], xah[b][:, :]), (wah[:, f], xal[b][:, :]), (wal[:, f], xah[b][:, :]),
                                       (wbh[:, f], xbh[b][:, :]), (wbl[:, f], xbh[b][:, :])])
                    last.then_inc(s_g, 1)

            def down(c, b, r):
                pe.wait_ge(s_pl, done3(c, MP - 1))
                pe.wait_ge(s_o1, done(c - 1))
                wh, wl = W["sdn"]
                for half in range(2):
                    pairs = []
                    for m in range(2 * MP):
                        t = slice(m % 2 * 2 * P + half * P, m % 2 * 2 * P + (half + 1) * P)
                        hi, lo, w = ph[b][:, m // 2, t], pl[b][:, m // 2, t], slice(m * D, (m + 1) * D)
                        pairs += [(hi, wh[:, w]), (lo, wh[:, w]), (hi, wl[:, w])]
                    last = mm(nc, ps_d[:, half * D:(half + 1) * D], pairs)
                last.then_inc(s_d, 1)
            pipeline(pe, NCH, RING, [(1, gate_up), (2, down)])
    nc.clear_and_free_semaphores(sems)
    nc.all_engine_barrier()


def launch_program(nc, I, out):
    scratch = {
        "hbuf": nc.dram_tensor("hbuf", (TPAD, B, D), F32, kind="Internal").ap(),
        "kqT": nc.dram_tensor("kqT", (NCH, D, P), F32, kind="Internal").ap(),
        "kqvo": nc.dram_tensor("kqvo", (TPAD, NH, 2 * D), F32, kind="Internal").ap(),
        "x2T": nc.dram_tensor("x2T", (NCH, D, 2 * P), F32, kind="Internal").ap(),
        "h2": nc.dram_tensor("h2", (NCH, P, 2 * D), F32, kind="Internal").ap(),
        "xs": nc.dram_tensor("xs", (ROWS, D), F32, kind="Internal").ap(),
        "ys": nc.dram_tensor("ys", (NTILE * P, D), F32, kind="Internal").ap(),
    }
    ctx = ExitStack()
    with ctx:
        def sb(name, shape, dt=F32):
            return ctx.enter_context(nc.sbuf_tensor(name, shape, dt))

        W = {name: (sb(name + "_hi", [P, n], F32R), sb(name + "_lo", [P, n], F32R))
             for name, n in (("gu_a", NE * 2 * HE), ("gu_b", NE * 2 * HE), ("dn_a", NE * D), ("dn_b", NE * D),
                             ("sgu_a", 2 * HS), ("sgu_b", 2 * HS), ("sdn", HS // P * D))}
        W["rw_a"] = sb("rw_a", [DA, NE + 1])
        W["rw_b"] = sb("rw_b", [DB, NE + 1])
        C = {"ident": sb("ident", [P, P]), "tri": sb("tri", [P, P], BF16), "ones": sb("ones", [P, P], BF16),
             "neghalf": sb("neghalf", [P, 8]), "iota8": sb("iota8", [P, NE]), "ebase": sb("ebase", [P, NE]),
             "partf": sb("partf", [P, 1]), "maskf": sb("maskf", [P, 2, STEP, HB]), "decay": sb("decay", [P, 2]),
             "sgb": sb("sgb", [P, 1]),
             "slots": sb("slots", [P, NCH, 4]), "jump": sb("jump", [P, NE]), "pre": sb("pre", [P, 2 * NCH, 2]), "gates": sb("gates", [P, 2 * NCH, 3]),
             "load": sb("load", [P, NE], BF16)}
        prepare(nc, I, scratch, W, C)
        attention_tables(nc, I, scratch, C)
        tokens(nc, I, scratch, C, W)
        experts(nc, scratch, C, W)
        combine(nc, scratch, C, W, out)


_INS = ['x', 'x_txt', 'L0_tok_W', 'L0_tok_b', 'L0_tok_cls', 'L0_tok_pos_embed', 'L0_txt_basin_coords', 'L0_txt_proj_w',
        'L0_txt_norm_w', 'L0_attn_w_key', 'L0_attn_w_value', 'L0_attn_w_query', 'L0_attn_w_gate', 'L0_attn_w_out',
        'L0_ffn_router_w', 'L0_ffn_w_gate', 'L0_ffn_w_up', 'L0_ffn_w_down', 'L0_ffn_ws_gate', 'L0_ffn_ws_up',
        'L0_ffn_ws_down', 'L0_ffn_sg_w', 'L0_ffn_sg_b']


def kernel(**inputs):
    import numpy as _np
    import concourse.bacc as _bacc
    from concourse import mybir as _mybir
    from concourse.bass_utils import run_bass_kernel_spmd as _run

    nc = _bacc.Bacc("TRN2", target_bir_lowering=False, num_devices=1)
    arrays, args = {}, {}
    for name in _INS:
        a = _np.ascontiguousarray(inputs[name])
        arrays[f"in_{name}"] = a
        args[name] = nc.dram_tensor(f"in_{name}", a.shape, _mybir.dt.from_np(a.dtype), kind="ExternalInput").ap()
    out = nc.dram_tensor("out_0", (B, T, D), _mybir.dt.float32, kind="ExternalOutput").ap()
    launch_program(nc, args, out)
    r = _run(nc, [arrays], core_ids=[0])
    return r.results[0]["out_0"]
```

```python
import concourse.bass as bass
from concourse import mybir
from contextlib import ExitStack

F32 = mybir.dt.float32
F32R = mybir.dt.float32r
BF16 = mybir.dt.bfloat16
I32 = mybir.dt.int32
U32 = mybir.dt.uint32
ACT = mybir.ActivationFunctionType
ALU = mybir.AluOpType
AX = mybir.AxisListType

P = 128
B, T, D = 16, 709, 192
DA, DB = 128, D - 128
NPATCH, SIDE, PX = 196, 14, 16
NTXT, BASIN, VOCAB = 512, 64, 32000
NH, DK = 8, 64
STEP = 16
NCH = -(-T // STEP)
TPAD = NCH * STEP
HB = B // 2
NE, HE, HS = 8, 192, 768
CAP = B * TPAD + P
NTILE = -(-((2 * B * TPAD + NE * (P - 1)) // P) // 4) * 4
DUMMY = NE * CAP
NDUMMY = NTILE - 2 * B * TPAD // P
ROWS = DUMMY + NDUMMY * P
DECAY, WRITE = 0.95, 0.1
LN_EPS, RMS_EPS = 1e-5, 1e-8


def mm(nc, out, pairs, start=True, stop=True):
    for n, (lhsT, rhs) in enumerate(pairs):
        last = nc.tensor.matmul(out, lhsT, rhs, start=start and n == 0, stop=stop and n == len(pairs) - 1)
    return last


def pipeline(eng, n, ring, stages, peel=1, turn=None):
    for s in range(ring * peel):
        if turn and s % ring == 0:
            turn(s // ring)
        for lag, body in stages:
            if s >= lag:
                body(s - lag, (s - lag) % ring, (s - lag) // ring)
    with eng.Fori(peel, n // ring) as i:
        if turn:
            turn(i)
        for u in range(ring):
            for lag, body in stages:
                body(ring * i + u - lag, (u - lag) % ring, i + (u - lag) // ring)
    for s in range(n, n + max(lag for lag, _ in stages)):
        if turn and s % ring == 0:
            turn(s // ring)
        for lag, body in stages:
            if s - lag < n:
                body(s - lag, (s - lag) % ring, (s - lag) // ring)


def done2(c):
    return c + 3


def free2(c):
    return c + 1


def prepare(nc, I, scratch, W, C):
    hbuf = scratch["hbuf"]
    ctx = ExitStack()
    sems = []
    with ctx:
        def sb(name, shape, dt=F32):
            return ctx.enter_context(nc.sbuf_tensor(name, shape, dt))

        def pb(name, shape, dt=F32):
            return ctx.enter_context(nc.psum_tensor(name, shape, dt))

        def sem(name):
            sems.append(nc.alloc_semaphore(name))
            return sems[-1]

        raw = [sb(f"raw{n}", [P, 1536]) for n in range(2)]
        img = [sb(f"img{n}", [96, SIDE, SIDE * PX]) for n in range(4)]
        tokw = sb("tokw", [96, 8, D])
        posb = sb("posb", [98, 2, D])
        bias_bc = sb("bias_bc", [98, D])
        pstage = [sb(f"pstage{n}", [98, 2, D]) for n in range(2)]
        cls_row = sb("cls_row", [B, D])
        pos0_row = sb("pos0_row", [B, D])
        cls_out = sb("cls_out", [B, D])
        zeros = sb("zeros", [P, D])
        projn = sb("projn", [P, 2, 2, BASIN])
        projT = sb("projT", [P, D])
        normw = sb("normw", [P, D])
        ids = sb("ids", [P, B, 4], I32)
        idsf = sb("idsf", [P, B, 4])
        idneg = sb("idneg", [P, B, 4])
        ids_ok = sb("ids_ok", [P, B, 4], U32)
        idc = [sb(f"idc{n}", [P, 4], U32) for n in range(2)]
        basin = [sb(f"basin{n}", [P, 4, BASIN]) for n in range(2)]
        basinT = [sb(f"basinT{n}", [P, 2, P]) for n in range(2)]
        sq = [sb(f"sq{n}", [P, 4, D]) for n in range(2)]
        ssq = [sb(f"ssq{n}", [P, 4]) for n in range(2)]
        msq = [sb(f"msq{n}", [P, 4]) for n in range(2)]
        rinv = [sb(f"rinv{n}", [P, 4]) for n in range(2)]
        tstage = [sb(f"tstage{n}", [P, 4, D]) for n in range(2)]
        tmp_i = sb("tmp_i", [P, 1], I32)
        part_i = sb("part_i", [P, 1], I32)
        s_f = sb("s_f", [P, 1])
        drow = sb("drow", [1, 2, P])
        one1 = sb("one1", [1, 1])

        ps_img = [pb(f"ps_img{n}", [P, 512]) for n in range(2)]
        ps_tT = [pb(f"ps_tT{n}", [P, 512]) for n in range(2)]
        ps_emb = [pb(f"ps_emb{n}", [P, 2, 512]) for n in range(2)]

        s_raw = [sem(f"raw_in{n}") for n in range(2)]
        s_hi = sem("hi_done")
        s_lo = sem("lo_done")
        s_tokw = sem("tokw_in")
        s_small = sem("small_in")
        s_ids = sem("ids_in")
        s_img = [sem(f"img_in{n}") for n in range(4)]
        s_posb = sem("posb_done")
        s_pmm = sem("patch_product")
        s_pst = sem("patch_staged")
        s_pout = [sem(f"patch_stored{n}") for n in range(2)]
        s_cls = sem("cls_done")
        s_clsout = sem("cls_stored")
        s_zero = sem("zeros_done")
        s_zout = sem("pads_stored")
        s_iota = sem("iota_done")
        s_const = sem("const_step")
        s_ident = sem("ident_done")
        s_drow = sem("decay_row")
        s_dcol = sem("decay_column")
        s_projT = sem("projT_product")
        s_projTc = sem("projT_done")
        s_idok = sem("ids_ok")
        s_idc = sem("ids_copied")
        s_apart = sem("apart")
        s_bas = [sem(f"basin_in{n}") for n in range(2)]
        s_bT = sem("basinT_product")
        s_bTc = sem("basinT_done")
        s_emb = sem("emb_product")
        s_ssq = sem("squares_summed")
        s_msq = sem("mean_square")
        s_rinv = sem("rms_inverse")
        s_tst = sem("text_staged")
        s_tout = [sem(f"text_stored{n}") for n in range(2)]
        block = ctx.enter_context(nc.Block())

        wg, wu, wd = (I[k].rearrange("e d h -> d e h") for k in ("L0_ffn_w_gate", "L0_ffn_w_up", "L0_ffn_w_down"))
        sg, su = I["L0_ffn_ws_gate"], I["L0_ffn_ws_up"]
        sd = I["L0_ffn_ws_down"].rearrange("(m p) d -> p m d", p=P)

        def halves(name):
            blocks = W[name][:, :].rearrange("p (n k d) -> p n k d", k=2, d=D)
            return blocks[:, :, 0, :], blocks[:, :, 1, :]

        def split_views(n):
            (hi, lo), cols = pieces[n][1:]
            if cols is None:
                width = hi.shape[1] * D
                return raw[n % 2][:, 0:width].rearrange("p (n d) -> p n d", d=D), hi, lo
            return raw[n % 2][:, 0:cols.stop - cols.start], hi[:, cols], lo[:, cols]

        def pairs4(r):
            return r[:, :].rearrange("p (e n) -> p e n", e=4)

        pieces = []
        for e0 in (0, 4):
            pieces.append(([(lambda r: pairs4(r)[:, :, 0:HE], wg[0:DA, e0:e0 + 4, :]),
                            (lambda r: pairs4(r)[:, :, HE:2 * HE], wu[0:DA, e0:e0 + 4, :])],
                           W["gu_a"], slice(e0 * 2 * HE, (e0 + 4) * 2 * HE)))
            pieces.append(([(lambda r, q=q: pairs4(r)[q:q + DB, :, 0:HE], wg[DA:D, e0:e0 + 4, :]) for q in (0, 64)]
                           + [(lambda r, q=q: pairs4(r)[q:q + DB, :, HE:2 * HE], wu[DA:D, e0:e0 + 4, :]) for q in (0, 64)],
                           W["gu_b"], slice(e0 * 2 * HE, (e0 + 4) * 2 * HE)))
        pieces.append(([(lambda r: r[:, :].rearrange("p (e n) -> p e n", e=NE), wd[0:DA, :, :])],
                       halves("dn_a"), None))
        pieces.append(([(lambda r, q=q: r[q:q + DB, :].rearrange("p (e n) -> p e n", e=NE), wd[DA:D, :, :]) for q in (0, 64)],
                       halves("dn_b"), None))
        pieces.append(([(lambda r: r[:, 0:HS], sg[0:DA, :]), (lambda r: r[:, HS:2 * HS], su[0:DA, :])],
                       W["sgu_a"], slice(0, 2 * HS)))
        pieces.append(([(lambda r, q=q: r[q:q + DB, 0:HS], sg[DA:D, :]) for q in (0, 64)]
                       + [(lambda r, q=q: r[q:q + DB, HS:2 * HS], su[DA:D, :]) for q in (0, 64)],
                       W["sgu_b"], slice(0, 2 * HS)))
        pieces.append(([(lambda r: r[:, 0:6 * D].rearrange("p (m d) -> p m d", m=6), sd)],
                       halves("sdn"), None))
        raw_count = [[0, 0]]
        for n, (dmas, _, _) in enumerate(pieces):
            c = list(raw_count[-1])
            c[n % 2] += 16 * len(dmas)
            raw_count.append(c)

        tokw_v = I["L0_tok_W"].rearrange("(i s j c) d -> s c i j d", i=PX, s=2, c=3)
        pos = I["L0_tok_pos_embed"]

        @block.sync
        def _(sp):
            for s in range(2):
                for c in range(3):
                    q = (3 * s + c) * PX
                    sp.dma_start(tokw[q:q + PX, :, :], tokw_v[s, c]).then_inc(s_tokw, 16)

            def small():
                sp.dma_start(bias_bc[:, :], I["L0_tok_b"].partition_broadcast(98)).then_inc(s_small, 16)
                sp.dma_start(posb[:, :, :], pos[0, 1:NPATCH + 1, :].rearrange("(g p) d -> p g d", p=98)).then_inc(s_small, 16)
                sp.dma_start(cls_row[:, :], I["L0_tok_cls"][0, :].partition_broadcast(B)).then_inc(s_small, 16)
                sp.dma_start(pos0_row[:, :], pos[0, 0, :].partition_broadcast(B)).then_inc(s_small, 16)
                sp.dma_start(normw[:, :], I["L0_txt_norm_w"].partition_broadcast(P)).then_inc(s_small, 16)
                for q in range(2):
                    sp.dma_start(projn[:, 0, q, :], I["L0_txt_proj_w"][0:P, :]).then_inc(s_small, 16)
                    sp.dma_start(projn[0:DB, 1, q, :], I["L0_txt_proj_w"][P:D, :]).then_inc(s_small, 16)
                sp.dma_start(W["rw_a"][:, 0:NE], I["L0_ffn_router_w"][0:DA, :]).then_inc(s_small, 16)
                sp.dma_start(W["rw_b"][:, 0:NE], I["L0_ffn_router_w"][DA:D, :]).then_inc(s_small, 16)
                sp.dma_start(W["rw_a"][:, NE:NE + 1], I["L0_ffn_sg_w"][0:DA, :]).then_inc(s_small, 16)
                sp.dma_start(W["rw_b"][:, NE:NE + 1], I["L0_ffn_sg_w"][DA:D, :]).then_inc(s_small, 16)
                sp.dma_start(C["sgb"][:, :], I["L0_ffn_sg_b"].partition_broadcast(P)).then_inc(s_small, 16)

            def images(c, b, r):
                if not (isinstance(c, int) and c < 4):
                    sp.wait_ge(s_pmm, done2(c - 4))
                for s in range(2):
                    for ch in range(3):
                        q = (3 * s + ch) * PX
                        src = I["x"][bass.ds(c, 1), ch, :, :].rearrange("b (n i) w -> (b i) n w", i=PX)
                        n = SIDE * PX - 8 * s
                        sp.dma_start(img[b][q:q + PX, :, 0:n], src[:, :, 8 * s:8 * s + n]).then_inc(s_img[b], 16)
            images(0, 0, 0)
            small()
            for c in range(1, 4):
                images(c, c, 0)
            with sp.Fori(1, B // 4) as i:
                for u in range(4):
                    images(4 * i + u, u, i)
            for u in range(2):
                sp.wait_ge(s_pout[u], 16 * HB + 16)
                sp.wait_ge(s_tout[u], 16 * HB + 16)
            sp.wait_ge(s_clsout, 16)
            sp.wait_ge(s_zout, 32)

        @block.gpsimd
        def _(pool):
            nc.gpsimd.memset(zeros[:, :], 0.0).then_inc(s_zero, 1)
            nc.gpsimd.memset(C["ident"][:, :], 0.0).then_inc(s_zero, 1)
            nc.gpsimd.memset(C["tri"][:, :], 0.0).then_inc(s_zero, 1)
            nc.gpsimd.memset(C["ones"][:, :], 1.0).then_inc(s_zero, 1)
            nc.gpsimd.memset(C["neghalf"][:, :], -0.5).then_inc(s_zero, 1)
            nc.gpsimd.iota(C["iota8"][:, :], pattern=[[1, NE]], base=0, channel_multiplier=0,
                           allow_small_or_imprecise_dtypes=True).then_inc(s_iota, 1)
            nc.gpsimd.iota(C["ebase"][:, :], pattern=[[CAP, NE]], base=0, channel_multiplier=0,
                           allow_small_or_imprecise_dtypes=True).then_inc(s_iota, 1)
            nc.gpsimd.iota(part_i[:, :], pattern=[[0, 1]], base=0, channel_multiplier=1).then_inc(s_iota, 1)
            nc.gpsimd.iota(C["partf"][:, :], pattern=[[0, 1]], base=0, channel_multiplier=1,
                           allow_small_or_imprecise_dtypes=True).then_inc(s_iota, 1)
            nc.gpsimd.iota(C["maskf"][:, :, :, :], pattern=[[0, 2], [1, STEP], [0, HB]], base=0, channel_multiplier=0,
                           allow_small_or_imprecise_dtypes=True).then_inc(s_iota, 1)
            pool.wait_ge(s_zero, 5)
            nc.gpsimd.affine_select(out=C["ident"][:, :], in_=C["ident"][:, :], compare_op=ALU.not_equal, fill=1.0,
                                    base=0, pattern=[[-1, P]], channel_multiplier=1).then_inc(s_ident, 1)
            nc.gpsimd.affine_select(out=C["tri"][:, :], in_=C["tri"][:, :], compare_op=ALU.is_ge, fill=1.0,
                                    base=0, pattern=[[-1, P]], channel_multiplier=1).then_inc(s_ident, 1)
            pool.wait_ge(s_idok, 1)
            pool.sem_inc(s_idc, 2)
            pool.sem_inc(s_rinv, 2)

            def gather(c, b, r):
                pool.wait_ge(s_bT, free2(c))
                nc.gpsimd.tensor_copy(idc[b][:, :], ids_ok[:, bass.ds(c, 1), :].rearrange("p a j -> p (a j)")).then_inc(s_idc, 1)
                pool.wait_ge(s_idc, done2(c))
                pool.sem_inc(s_apart, 1)
                for j in range(4):
                    nc.gpsimd.indirect_dma_start(basin[b][:, j, :], None, I["L0_txt_basin_coords"],
                                                 bass.IndirectOffsetOnAxis(ap=idc[b][:, j:j + 1], axis=0)).then_inc(s_bas[b], 16)

            def rms_inverse(c, b, r):
                pool.wait_ge(s_msq, done2(c))
                pool.wait_ge(s_tst, free2(c))
                nc.gpsimd.tensor_tensor(rinv[b][:, :], msq[b][:, :], C["neghalf"][:, 0:4], ALU.pow).then_inc(s_rinv, 1)
            pipeline(pool, B, 2, [(0, gather), (3, rms_inverse)], peel=2)

        @block.scalar
        def _(act):
            act.dma_start(ids[:, :, :], I["x_txt"].rearrange("b (p j) -> p b j", j=4)).then_inc(s_ids, 16)

            def load(n):
                for dst, src in pieces[n][0]:
                    act.dma_start(dst(raw[n % 2]), src).then_inc(s_raw[n % 2], 16)
            load(0)
            load(1)
            act.wait_ge(s_zero, 1)
            act.dma_start(hbuf[T:TPAD, :, :].rearrange("t b d -> b t d"), zeros[:, :].unsqueeze(1)[0:B, :, :].to_broadcast([B, TPAD - T, D])).then_inc(s_zout, 16)
            act.dma_start(scratch["xs"][DUMMY:ROWS, :].rearrange("(k p) d -> p k d", p=P),
                          zeros[:, :].unsqueeze(1).to_broadcast([P, NDUMMY, D])).then_inc(s_zout, 16)
            act.wait_ge(s_cls, 1)
            act.dma_start(hbuf[0, :, :], cls_out[:, :]).then_inc(s_clsout, 16)
            act.sem_inc(s_bTc, 2)
            act.sem_inc(s_ssq, 2)

            def lead(n):
                whole, hi, _ = split_views(n)
                act.wait_ge(s_raw[n % 2], raw_count[n + 1][n % 2])
                nc.scalar.activation(hi, whole, ACT.Copy).then_inc(s_hi, 1)
                if n >= 1 and n + 1 < len(pieces):
                    act.wait_ge(s_lo, n)
                    load(n + 1)

            def leads(c, b, r):
                if isinstance(c, int) and c < len(pieces) - 1:
                    lead(c)

            def basin_columns(c, b, r):
                act.wait_ge(s_bT, done2(c))
                act.wait_ge(s_emb, free2(c))
                nc.scalar.activation(basinT[b][:, :, :], ps_tT[b][:, 0:2 * P].rearrange("p (j n) -> p j n", j=2), ACT.Copy).then_inc(s_bTc, 1)

            def squares(c, b, r):
                act.wait_ge(s_emb, done2(c))
                act.wait_ge(s_msq, free2(c))
                for j in range(4):
                    last = nc.scalar.activation(sq[b][:, j, :], ps_emb[b][:, j % 2, j // 2 * D:(j // 2 + 1) * D],
                                                ACT.Square, accum_out=ssq[b][:, j:j + 1])
                last.then_inc(s_ssq, 1)

            def store_patches(c, b, r):
                act.wait_ge(s_pst, done2(c))
                dst = hbuf[1:1 + NPATCH, bass.ds(c, 1), :].rearrange("(g p) b d -> p (g b) d", p=98)
                act.dma_start(dst, pstage[b][:, :, :]).then_inc(s_pout[b], 16)

            def store_text(c, b, r):
                act.wait_ge(s_tst, done2(c))
                dst = hbuf[1 + NPATCH:T, bass.ds(c, 1), :].rearrange("(p j) b d -> p (j b) d", j=4)
                act.dma_start(dst, tstage[b][:, :, :]).then_inc(s_tout[b], 16)
            pipeline(act, B, 2, [(4, store_text), (1, basin_columns), (1, store_patches), (2, squares), (0, leads)], peel=len(pieces) // 2)
            lead(len(pieces) - 1)

        @block.vector
        def _(dve):
            for u in range(2):
                dve.sem_inc(s_pout[u], 16)
                dve.sem_inc(s_tout[u], 16)
            for s in (s_pst, s_tst, s_msq):
                dve.sem_inc(s, 2)
            dve.wait_ge(s_iota, 5)
            nc.vector.tensor_scalar(tmp_i[:, :], part_i[:, :], 3, None, ALU.arith_shift_right).then_inc(s_const, 1)
            dve.wait_ge(s_const, 1)
            nc.vector.tensor_copy(s_f[:, :], tmp_i[:, :]).then_inc(s_const, 1)
            dve.wait_ge(s_const, 2)
            nc.vector.tensor_scalar(C["maskf"][:, :, :, :], C["maskf"][:, :, :, :], s_f[:, 0:1], None, ALU.is_gt).then_inc(s_const, 1)
            for s in range(STEP):
                nc.vector.memset(drow[0:1, 0, s * P // STEP:(s + 1) * P // STEP], DECAY ** s)
                last = nc.vector.memset(drow[0:1, 1, :].rearrange("p (a s) -> p a s", s=STEP)[:, :, s:s + 1],
                                        0.5 * WRITE * DECAY ** -(s + 1))
            nc.vector.memset(one1[:, :], 1.0).then_inc(s_drow, 1)
            dve.wait_ge(s_dcol, 1)
            nc.vector.tensor_copy(C["decay"][:, :], ps_tT[0][:, 0:2]).then_inc(s_const, 1)
            dve.wait_ge(s_ids, 16)
            nc.vector.tensor_copy(idsf[:, :, :], ids[:, :, :]).then_inc(s_const, 1)
            dve.wait_ge(s_const, 5)
            nc.vector.tensor_scalar(idneg[:, :, :], idsf[:, :, :], 0.0, float(VOCAB), ALU.is_lt, ALU.mult).then_inc(s_const, 1)
            dve.wait_ge(s_const, 6)
            nc.vector.tensor_tensor(idsf[:, :, :], idsf[:, :, :], idneg[:, :, :], ALU.add).then_inc(s_const, 1)
            dve.wait_ge(s_const, 7)
            nc.vector.tensor_scalar(ids_ok[:, :, :], idsf[:, :, :], 0.0, float(VOCAB - 1), ALU.max, ALU.min).then_inc(s_idok, 1)
            dve.wait_ge(s_small, 16 * 14)
            nc.vector.tensor_tensor(posb[:, :, :], posb[:, :, :], bias_bc[:, :].unsqueeze(1).to_broadcast([98, 2, D]), ALU.add).then_inc(s_posb, 1)
            nc.vector.tensor_tensor(cls_out[:, :], cls_row[:, :], pos0_row[:, :], ALU.add).then_inc(s_cls, 1)
            dve.wait_ge(s_projT, 1)
            nc.vector.tensor_copy(projT[:, :], ps_tT[1][:, 0:D]).then_inc(s_projTc, 1)
            dve.wait_ge(s_posb, 1)

            def rest(n):
                whole, hi, lo = split_views(n)
                dve.wait_ge(s_hi, n + 1)
                nc.vector.tensor_tensor(lo, whole, hi.bitcast(F32), ALU.subtract).then_inc(s_lo, 1)

            def rests(c, b, r):
                if isinstance(c, int) and c < len(pieces) - 1:
                    rest(c)

            def stage_patches(c, b, r):
                dve.wait_ge(s_pmm, done2(c))
                dve.wait_ge(s_pout[b], 16 * r + 16)
                nc.vector.tensor_tensor(pstage[b][:, :, :], ps_img[b][0:98, 0:2 * D].rearrange("p (g d) -> p g d", g=2),
                                        posb[:, :, :], ALU.add).then_inc(s_pst, 1)

            def mean_square(c, b, r):
                dve.wait_ge(s_ssq, done2(c))
                dve.wait_ge(s_rinv, free2(c))
                nc.vector.tensor_scalar(msq[b][:, :], ssq[b][:, :], 1.0 / D, RMS_EPS, ALU.mult, ALU.add).then_inc(s_msq, 1)

            def stage_text(c, b, r):
                dve.wait_ge(s_rinv, done2(c))
                dve.wait_ge(s_tout[b], 16 * r + 16)
                for j in range(4):
                    last = nc.vector.scalar_tensor_tensor(
                        out=tstage[b][:, j, :], in0=ps_emb[b][:, j % 2, j // 2 * D:(j // 2 + 1) * D],
                        scalar=rinv[b][:, j:j + 1], in1=normw[:, :], op0=ALU.mult, op1=ALU.mult)
                last.then_inc(s_tst, 1)
            pipeline(dve, B, 2, [(3, stage_text), (0, stage_patches), (0, rests), (2, mean_square)], peel=len(pieces) // 2)
            rest(len(pieces) - 1)

        @block.tensor
        def _(pe):
            pe.wait_ge(s_drow, 1)
            for k in range(2):
                last = nc.tensor.matmul(ps_tT[0][:, k:k + 1], drow[0:1, k, :], one1[:, :], start=True, stop=True)
            last.then_inc(s_dcol, 1)
            pe.wait_ge(s_tokw, 96)
            pe.wait_ge(s_const, 4)
            for s in (s_pmm, s_bT, s_emb):
                pe.sem_inc(s, 2)

            def patches(c, b, r):
                pe.wait_ge(s_img[b], 96 * r + 96)
                pe.wait_ge(s_pst, free2(c))
                for g in range(2):
                    for j in range(8):
                        px = img[b][:, 7 * g:7 * g + 7, :].rearrange("p n (w j) -> p n w j", j=PX)[:, :, :, j]
                        last = nc.tensor.matmul(ps_img[b % 2][0:98, g * D:(g + 1) * D], px, tokw[:, j, :],
                                                start=j == 0, stop=j == 7)
                last.then_inc(s_pmm, 1)

            def projection(c, b, r):
                if isinstance(c, int) and c == 0:
                    pe.wait_ge(s_small, 16 * 14)
                    pe.wait_ge(s_ident, 2)
                    nc.tensor.transpose(ps_tT[1][:, 0:P], projn[:, 0, :, :].rearrange("p q k -> p (q k)"), C["ident"][:, :])
                    nc.tensor.transpose(ps_tT[1][:, P:D], projn[0:DB, 1, :, :].rearrange("p q k -> p (q k)"),
                                        C["ident"][0:DB, 0:DB]).then_inc(s_projT, 1)

            def basin_transposes(c, b, r):
                if isinstance(c, int) and c == 1:
                    pe.wait_ge(s_projTc, 1)
                pe.wait_ge(s_bas[b % 2], 64 * (2 * r + b // 2) + 64)
                pe.wait_ge(s_bTc, free2(c))
                for j in range(2):
                    last = nc.tensor.transpose(ps_tT[b % 2][:, j * P:(j + 1) * P],
                                               basin[b % 2][:, 2 * j:2 * j + 2, :].rearrange("p j k -> p (j k)"), C["ident"][:, :])
                last.then_inc(s_bT, 1)

            def embed(c, b, r):
                pe.wait_ge(s_bTc, done2(c))
                pe.wait_ge(s_tst, free2(c))
                for j in range(4):
                    last = nc.tensor.matmul(ps_emb[b % 2][:, j % 2, j // 2 * D:(j // 2 + 1) * D],
                                            basinT[b % 2][j % 2 * BASIN:(j % 2 + 1) * BASIN, j // 2, :],
                                            projT[j % 2 * BASIN:(j % 2 + 1) * BASIN, :], start=True, stop=True)
                last.then_inc(s_emb, 1)
            pipeline(pe, B, 4, [(0, patches), (0, projection), (1, basin_transposes), (2, embed)])
    nc.clear_and_free_semaphores(sems)
    nc.all_engine_barrier()


def attention_tables(nc, I, scratch, C):
    ctx = ExitStack()
    sems = []
    NF = TPAD // P
    TAIL = TPAD - NF * P
    BLK = [P] * NF + [TAIL]
    NB = NF + 1
    SPLIT = [(0, 368), (368, TPAD)]
    with ctx:
        def sb(name, shape, dt=F32):
            return ctx.enter_context(nc.sbuf_tensor(name, shape, dt))

        def pb(name, shape, dt=F32):
            return ctx.enter_context(nc.psum_tensor(name, shape, dt))

        def sem(name):
            sems.append(nc.alloc_semaphore(name))
            return sems[-1]

        stats = sb("stats0", [P, NB, 6])
        mv = sb("mv0", [P, NB, 2])
        vare = sb("vare0", [P, NB])
        rstd = sb("rstd0", [P, NB])
        rows = [sb(f"rows{n}", [P, NB, 2 * D]) for n in range(2)]
        early = [r[:, :, :].rearrange("p k d -> p (k d)") for r in rows]
        h0 = early[0][:, 0:NB * D].rearrange("p (k d) -> p k d", d=D)
        wo = early[0][:, NB * D:NB * D + 2 * NH * DK].rearrange("p (k d) -> p k d", k=2)
        wk = early[1][:, 0:4 * D].rearrange("p (m d) -> p m d", m=4)
        wv = early[1][:, 4 * D:8 * D].rearrange("p (m d) -> p m d", m=4)
        wq = sb("wq", [P, 4, D])
        wgt = sb("wgt", [NH, D])
        wkT = [sb("wkT_a", [DA, 4, P]), sb("wkT_b", [DB, 4, P])]
        wvT = [sb("wvT_a", [DA, 4, P]), sb("wvT_b", [DB, 4, P])]
        woT = sb("woT", [P, 4, D])
        wgT = [sb("wgT_a", [DA, NH]), sb("wgT_b", [DB, NH])]
        x0T = [sb("x0T_a", [DA, TPAD]), sb("x0T_b", [DB, TPAD])]
        kvT = sb("kvT", [P, 4, 2, TPAD])
        kqT_a = sb("kqT_a", [DA, TPAD, NH])
        kqT_b = sb("kqT_b", [P, 368, NH])
        gsc = sb("gsc", [P, NB, NH])
        gscale = sb("gscale", [P, NB, NH])
        ps = [pb(f"ps{n}", [P, 512]) for n in range(8)]

        s_w = sem("attn_weights_in")
        s_h = sem("h0_in")
        s_stat = sem("stats0_done")
        s_aggr = sem("aggr0_done")
        s_var = sem("var0_done")
        s_rstd = sem("rstd0_done")
        s_x0 = sem("x0_done")
        s_wTp = sem("weight_transposed")
        s_wT = sem("weightT_copied")
        s_x0Tp = sem("x0_transposed")
        s_x0T = sem("x0T_copied")
        s_gl = sem("gate_logits")
        s_gt = sem("gate_tanh")
        s_gs = sem("gate_scale")
        s_kv = sem("kv_product")
        s_kvc = sem("kv_copied")
        s_bank = sem("head_bank_filled")
        s_evA = sem("bank_copied_act")
        s_evD = sem("bank_copied_dve")
        s_row = [sem(f"rows_stored{n}") for n in range(2)]
        s_tab = sem("kqT_stored")
        block = ctx.enter_context(nc.Block())
        ident = C["ident"]
        hb = scratch["hbuf"]

        @block.sync
        def _(sp):
            sp.dma_start(h0[:, 0:NF, :], hb[0:NF * P, 0, :].rearrange("(k p) d -> p k d", p=P)).then_inc(s_h, 16)
            sp.dma_start(h0[0:TAIL, NF, :], hb[NF * P:TPAD, 0, :]).then_inc(s_h, 16)
            for w, name in ((wk, "L0_attn_w_key"), (wv, "L0_attn_w_value"), (wq, "L0_attn_w_query")):
                sp.dma_start(w[:, :, :], I[name].rearrange("(m p) d -> p m d", p=P)).then_inc(s_w, 16)
            sp.dma_start(wo[:, 0, :], I["L0_attn_w_out"][0:P, :]).then_inc(s_w, 16)
            sp.dma_start(wo[0:DB, 1, :], I["L0_attn_w_out"][P:D, :]).then_inc(s_w, 16)
            sp.dma_start(wgt[:, :], I["L0_attn_w_gate"]).then_inc(s_w, 16)
            sp.wait_ge(s_evA, 2 * NH)
            sp.wait_ge(s_evD, 2 * NH)
            c0 = SPLIT[0][1] // STEP
            columns = scratch["kqT"].rearrange("c d x -> d c x")
            sp.dma_start(columns[0:DA, :, :], kqT_a[:, :, :].rearrange("d (c s) h -> d c (s h)", s=STEP)).then_inc(s_tab, 16)
            for h in range(NH):
                sp.wait_ge(s_evA, 2 * NH + NB // 2 * (h + 1))
                sp.wait_ge(s_evD, 2 * NH + NB // 2 * (h + 1))
                dst = scratch["kqvo"][:, h, :]
                sp.dma_start(dst[0:NF * P, :].rearrange("(k p) d -> p k d", p=P), rows[h % 2][:, 0:NF, :]).then_inc(s_row[h % 2], 16)
                sp.dma_start(dst[NF * P:TPAD, :], rows[h % 2][0:TAIL, NF, :]).then_inc(s_row[h % 2], 16)
                if h == 1:
                    sp.dma_start(columns[DA:D, 0:c0, :], kqT_b[0:DB, :, :].rearrange("d (c s) h -> d c (s h)", s=STEP)).then_inc(s_tab, 16)
                if h == 3:
                    sp.dma_start(columns[DA:D, c0:NCH, :], kqT_b[DB:P, 0:TPAD - c0 * STEP, :].rearrange("d (c s) h -> d c (s h)", s=STEP)).then_inc(s_tab, 16)
            sp.wait_ge(s_tab, 48)
            for n in range(2):
                sp.wait_ge(s_row[n], 32 * NH // 2)

        @block.gpsimd
        def _(pool):
            pool.wait_ge(s_var, 1)
            nc.gpsimd.tensor_tensor(rstd[:, :], vare[:, :], C["neghalf"][:, 0:NB], ALU.pow).then_inc(s_rstd, 1)

        @block.scalar
        def _(act):
            act.wait_ge(s_wTp, 1)
            for n, wT in enumerate((wkT[0], wkT[1], wvT[0], wvT[1])):
                r = DA if n % 2 == 0 else DB
                nc.scalar.activation(wT[:, :, :], ps[n][0:r, :].rearrange("p (m n) -> p m n", m=4), ACT.Copy).then_inc(s_wT, 1)
            for n in range(2):
                nc.scalar.activation(woT[:, 2 * n:2 * n + 2, :], ps[4 + n][:, 0:2 * D].rearrange("p (m n) -> p m n", m=2), ACT.Copy).then_inc(s_wT, 1)
            nc.scalar.activation(wgT[0][:, :], ps[6][0:DA, 0:NH], ACT.Copy).then_inc(s_wT, 1)
            nc.scalar.activation(wgT[1][:, :], ps[6][0:DB, NH:2 * NH], ACT.Copy).then_inc(s_wT, 1)
            act.wait_ge(s_gl, 1)
            nc.scalar.activation(gsc[:, 0:NF, :], ps[4][:, 0:NF * NH].rearrange("p (k h) -> p k h", h=NH), ACT.Tanh, scale=0.5).then_inc(s_gt, 1)
            nc.scalar.activation(gsc[0:TAIL, NF, :], ps[4][0:TAIL, NF * NH:NB * NH], ACT.Tanh, scale=0.5).then_inc(s_gt, 1)
            act.wait_ge(s_gs, 2)

            def keys_values(m):
                for t in range(2):
                    for n, (a, b) in enumerate(SPLIT):
                        act.wait_ge(s_kv, 4 * m + 2 * t + n + 1)
                        nc.scalar.activation(kvT[:, m, t, a:b], ps[2 * t + n][:, 0:b - a], ACT.Copy).then_inc(s_kvc, 1)
            keys_values(0)
            for m in range(4):
                if m < 3:
                    keys_values(m + 1)
                for h in (2 * m, 2 * m + 1):
                    for half, (a, b) in enumerate(SPLIT):
                        fill = 4 * h + 2 * half
                        act.wait_ge(s_bank, fill + 1)
                        nc.scalar.activation(kqT_a[:, a:b, h], ps[4 + fill % 4][:, 0:b - a], ACT.Copy).then_inc(s_evA, 1)
            for h in range(NH):
                r = rows[h % 2]
                if h >= 2:
                    act.wait_ge(s_row[h % 2], 32 * (h // 2))
                for k in range(0, NB, 2):
                    fill, n = 4 * NH + NB * h + k, BLK[k]
                    act.wait_ge(s_bank, fill + 1)
                    bank = ps[4 + fill % 4]
                    nc.scalar.activation(r[0:n, k, 0:D], bank[0:n, 0:D], ACT.Copy)
                    nc.scalar.activation(r[0:n, k, D:2 * D], bank[0:n, D:2 * D], ACT.Copy, scale=gscale[0:n, k, h:h + 1]).then_inc(s_evA, 1)

        @block.vector
        def _(dve):
            dve.wait_ge(s_h, 32)
            for k, n in enumerate(BLK):
                last = nc.vector.bn_stats(stats[0:n, k, :], h0[0:n, k, :])
            last.then_inc(s_stat, 1)
            dve.wait_ge(s_stat, 1)
            nc.vector.memset(mv[:, :, :], 1.0).then_inc(s_aggr, 1)
            dve.wait_ge(s_aggr, 1)
            for k, n in enumerate(BLK):
                last = nc.vector.bn_aggr(mv[0:n, k, :], stats[0:n, k, :])
            last.then_inc(s_aggr, 1)
            dve.wait_ge(s_aggr, 2)
            nc.vector.tensor_scalar(vare[:, :], mv[:, :, 1], LN_EPS, None, ALU.add).then_inc(s_var, 1)
            dve.wait_ge(s_rstd, 1)
            for k, n in enumerate(BLK):
                last = nc.vector.tensor_scalar(h0[0:n, k, :], h0[0:n, k, :], mv[0:n, k, 0:1], rstd[0:n, k:k + 1],
                                               ALU.subtract, ALU.mult)
            last.then_inc(s_x0, 1)
            dve.wait_ge(s_x0Tp, 1)
            for half, r in enumerate((DA, DB)):
                nc.vector.tensor_copy(x0T[half][:, 0:512], ps[2 * half][0:r, 0:512])
                last = nc.vector.tensor_copy(x0T[half][:, 512:TPAD], ps[2 * half + 1][0:r, 0:TPAD - 512])
            last.then_inc(s_x0T, 1)
            dve.wait_ge(s_gt, 2)
            nc.vector.tensor_scalar(gscale[:, 0:NF, :], gsc[:, 0:NF, :], 1.0, C["decay"][:, 1:2], ALU.add, ALU.mult).then_inc(s_gs, 1)
            nc.vector.tensor_scalar(gscale[0:TAIL, NF, :], gsc[0:TAIL, NF, :], 1.0, C["decay"][0:TAIL, 1:2], ALU.add, ALU.mult).then_inc(s_gs, 1)
            dve.wait_ge(s_gs, 2)
            for h in range(NH):
                for half, (a, b) in enumerate(SPLIT):
                    fill, r0 = 4 * h + 2 * half + 1, DB * half
                    dve.wait_ge(s_bank, fill + 1)
                    nc.vector.tensor_copy(kqT_b[r0:r0 + DB, 0:b - a, h], ps[4 + fill % 4][r0:r0 + DB, 0:b - a]).then_inc(s_evD, 1)
            for h in range(NH):
                r = rows[h % 2]
                if h >= 2:
                    dve.wait_ge(s_row[h % 2], 32 * (h // 2))
                for k in range(1, NB, 2):
                    fill, n = 4 * NH + NB * h + k, BLK[k]
                    dve.wait_ge(s_bank, fill + 1)
                    bank = ps[4 + fill % 4]
                    nc.vector.tensor_copy(r[0:n, k, 0:D], bank[0:n, 0:D])
                    nc.vector.tensor_scalar(r[0:n, k, D:2 * D], bank[0:n, D:2 * D], gscale[0:n, k, h:h + 1], None, ALU.mult).then_inc(s_evD, 1)

        @block.tensor
        def _(pe):
            pe.wait_ge(s_w, 96)
            for n, w in enumerate((wk, wv)):
                for m in range(4):
                    nc.tensor.transpose(ps[2 * n][:, m * P:(m + 1) * P], w[:, m, 0:DA], ident[:, :])
                    nc.tensor.transpose(ps[2 * n + 1][0:DB, m * P:(m + 1) * P], w[:, m, DA:D], ident[:, :])
            for m in range(4):
                bank, c = ps[4 + m // 2], m % 2 * D
                nc.tensor.transpose(bank[:, c:c + DA], wo[:, 0, m * P:(m + 1) * P], ident[:, :])
                nc.tensor.transpose(bank[:, c + DA:c + D], wo[0:DB, 1, m * P:(m + 1) * P], ident[0:DB, 0:DB])
            nc.tensor.transpose(ps[6][0:DA, 0:NH], wgt[:, 0:DA], ident[0:NH, 0:NH])
            nc.tensor.transpose(ps[6][0:DB, NH:2 * NH], wgt[:, DA:D], ident[0:NH, 0:NH]).then_inc(s_wTp, 1)
            pe.wait_ge(s_x0, 1)
            pe.wait_ge(s_wT, 8)
            for half, (a, b) in enumerate(((0, DA), (DA, D))):
                for k, n in enumerate(BLK):
                    bank, c = ps[2 * half + k // 4], k % 4 * P
                    last = nc.tensor.transpose(bank[0:b - a, c:c + n], h0[0:n, k, a:b], ident[0:n, 0:n])
            last.then_inc(s_x0Tp, 1)
            pe.wait_ge(s_x0T, 1)
            for k, n in enumerate(BLK):
                last = mm(nc, ps[4][0:n, k * NH:(k + 1) * NH], [(x0T[q][:, k * P:k * P + n], wgT[q][:, :]) for q in range(2)])
            last.then_inc(s_gl, 1)
            pe.wait_ge(s_gt, 2)

            def keys_values(m):
                for t, wT in enumerate((wkT, wvT)):
                    for n, (a, b) in enumerate(SPLIT):
                        if m:
                            pe.wait_ge(s_kvc, 4 * m - 3 + 2 * t + n)
                        mm(nc, ps[2 * t + n][:, 0:b - a], [(wT[q][:, m, :], x0T[q][:, a:b]) for q in range(2)]).then_inc(s_kv, 1)

            def bank_of(fill):
                if fill >= 4:
                    pe.wait_ge(s_evA if fill % 2 == 0 else s_evD, (fill - 4) // 2 + 1)
                return ps[4 + fill % 4]

            keys_values(0)
            for m in range(4):
                if m < 3:
                    keys_values(m + 1)
                pe.wait_ge(s_kvc, 4 * m + 4)
                for h in (2 * m, 2 * m + 1):
                    r = slice(h % 2 * DK, (h % 2 + 1) * DK)
                    for half, (a, b) in enumerate(SPLIT):
                        bank = bank_of(4 * h + 2 * half)
                        nc.tensor.matmul(bank[:, 0:b - a], wq[r, m, 0:DA], kvT[r, m, 0, a:b], start=True, stop=True).then_inc(s_bank, 1)
                        bank = bank_of(4 * h + 2 * half + 1)
                        nc.tensor.matmul(bank[DB * half:DB * half + DB, 0:b - a], wq[r, m, DA:D], kvT[r, m, 0, a:b],
                                         start=True, stop=True).then_inc(s_bank, 1)
            for h in range(NH):
                m, r = h // 2, slice(h % 2 * DK, (h % 2 + 1) * DK)
                for k, n in enumerate(BLK):
                    bank = bank_of(4 * NH + NB * h + k)
                    nc.tensor.matmul(bank[0:n, 0:D], kvT[r, m, 0, k * P:k * P + n], wq[r, m, :], start=True, stop=True)
                    nc.tensor.matmul(bank[0:n, D:2 * D], kvT[r, m, 1, k * P:k * P + n], woT[r, m, :], start=True, stop=True).then_inc(s_bank, 1)
    nc.clear_and_free_semaphores(sems)
    nc.all_engine_barrier()


NORM2 = 4
RING = 3


def done(c):
    return c + 1 + RING


def free(c):
    return c + 1


def tokens(nc, I, scratch, C, W):
    ctx = ExitStack()
    sems = []
    with ctx:
        def sb(name, shape, dt=F32):
            return ctx.enter_context(nc.sbuf_tensor(name, shape, dt))

        def ring(name, shape, dt=F32):
            return [sb(f"{name}_{n}", shape, dt) for n in range(RING)]

        def pb(name, shape, dt=F32):
            return ctx.enter_context(nc.psum_tensor(name, shape, dt))

        def sem(name):
            sems.append(nc.alloc_semaphore(name))
            return sems[-1]

        h = ring("h", [P, 2, D])
        x1 = ring("x1", [P, 2, D])
        hx = ring("hx", [P, 2, D])
        h2 = ring("h2s", [P, 2, D])
        x2 = ring("x2", [P, 2, D])
        x2r = ring("x2r", [P, 2, D])
        st1 = ring("st1", [P, 2, 6])
        mv1 = ring("mv1", [P, 2, 2])
        vp = ring("vp", [P, 4])
        rp = ring("rp", [P, 4])
        nb1 = ring("nb1", [P, 2])
        rq1 = ring("rq1", [P, 2])
        st2 = ring("st2", [P, 2, 6])
        mv2 = ring("mv2", [P, 2, 2])
        nb2 = ring("nb2", [P, 2])
        x1a = ring("x1a", [DA, 2 * P])
        x1b = ring("x1b", [DB, 2 * P])
        x2a = ring("x2a", [DA, 2 * P])
        x2b = ring("x2b", [DB, 2 * P])
        kqa = ring("kqa", [DA, P])
        kqb = ring("kqb", [DB, P])
        kqvo = ring("kqvo", [P, 2 * D])
        sc = ring("sc", [P, 2 * P])
        Ma = ring("Ma", [DA, D])
        Mb = ring("Mb", [DB, D])
        Msa = ring("Msa", [DA, D])
        Msb = ring("Msb", [DB, D])
        lg = ring("lg", [P, 2, NE + 1])
        mx = ring("mx", [P, 2, 8])
        ix = ring("ix", [P, 2, 8], U32)
        oh = ring("oh", [P, 4, NE])
        ohs = ring("ohs", [P, 2, NE], BF16)
        ld = ring("ld", [P, NE], BF16)
        ldc = ring("ldc", [P, NE])
        pb8 = ring("pb8", [P, 2, NE])
        prod = ring("prod", [P, 4, NE])
        slf = ring("slf", [P, 4])
        slu = ring("slu", [P, 4], U32)

        ps_x1, ps_sc, ps_o, ps_m, ps_x2, ps_lg, ps_pos = [pb(n, [P, 512]) for n in
                                                          ("ps_x1", "ps_sc", "ps_o", "ps_m", "ps_x2", "ps_lg", "ps_pos")]

        s_h_in = [sem(f"h_in{n}") for n in range(RING)]
        s_k_in = [sem(f"k_in{n}") for n in range(RING)]
        s_h2_out = [sem(f"h2_out{n}") for n in range(RING)]
        s_x2T_out = [sem(f"x2T_out{n}") for n in range(RING)]
        s_scat = [sem(f"scattered{n}") for n in range(RING)]
        s_init = sem("init")
        s_apart_dve, s_apart_pool = sem("apart_dve"), sem("apart_pool")
        s_st1, s_ag1, s_ve1, s_rs = sem("stats1"), sem("aggr1"), sem("var1"), sem("rstd")
        s_nb1, s_nb2 = sem("shift1"), sem("shift2")
        s_x1, s_hx = sem("x1"), sem("hx")
        s_x1Tp, s_x1T = sem("x1T_product"), sem("x1T")
        s_scp, s_sc = sem("score_product"), sem("scores")
        s_om, s_mp = sem("attention_product"), sem("write_product")
        s_Ms, s_M = sem("M_scaled"), sem("M")
        s_h2 = sem("h2_done")
        s_st2, s_ag2, s_ve2 = sem("stats2"), sem("aggr2"), sem("var2")
        s_x2, s_x2r = sem("x2_done"), sem("x2_rows")
        s_x2Tp, s_x2T = sem("x2T_product"), sem("x2T_copied")
        s_lgp, s_lg = sem("logit_product"), sem("logits")
        s_mx, s_ix = sem("top8"), sem("top8_index")
        s_oh, s_ohs = sem("onehot"), sem("onehot_sum")
        s_ld = sem("load_done")
        s_posp, s_pb8, s_prod, s_slf, s_slot = sem("pos_product"), sem("pos_base"), sem("pos_chosen"), sem("slot_float"), sem("slot")
        block = ctx.enter_context(nc.Block())
        ident = C["ident"]
        c16 = DECAY ** STEP
        hb = scratch["hbuf"]

        def at(dram, c):
            return dram[bass.ds(c, 1)].rearrange("c a b -> (c a) b")

        @block.sync
        def _(sp):
            def loads(c, b, r):
                sp.wait_ge(s_x1, free(c))
                sp.wait_ge(s_hx, free(c))
                src = hb[bass.ds(c * STEP, STEP), :, :].rearrange("t (k a) d -> (t k) (a d)", a=2)
                sp.dma_start(h[b][:, :, :].rearrange("p a d -> p (a d)"), src).then_inc(s_h_in[b], 16)

            def tables(c, b, r):
                sp.wait_ge(s_om, free(c))
                sp.dma_start(kqa[b][:, :], at(scratch["kqT"], c)[0:DA, :]).then_inc(s_k_in[b], 16)
                sp.dma_start(kqb[b][:, :], at(scratch["kqT"], c)[DA:D, :]).then_inc(s_k_in[b], 16)
                src = scratch["kqvo"][bass.ds(c * STEP, STEP), :, :].rearrange("s h d -> (s h) d")
                sp.dma_start(kqvo[b][:, :], src).then_inc(s_k_in[b], 16)

            def stores(c, b, r):
                sp.wait_ge(s_h2, done(c))
                sp.dma_start(at(scratch["h2"], c), h2[b][:, :, :].rearrange("p a d -> p (a d)")).then_inc(s_h2_out[b], 16)
                sp.wait_ge(s_x2T, done(c))
                sp.dma_start(at(scratch["x2T"], c)[0:DA, :], x2a[b][:, :]).then_inc(s_x2T_out[b], 16)
                sp.dma_start(at(scratch["x2T"], c)[DA:D, :], x2b[b][:, :]).then_inc(s_x2T_out[b], 16)
            for b in range(RING):
                sp.sem_inc(s_h2_out[b], 16)
                sp.sem_inc(s_x2T_out[b], 32)
            pipeline(sp, NCH, RING, [(0, loads), (6, stores), (1, tables)], peel=2)
            for b in range(RING):
                sp.wait_ge(s_h2_out[b], 16 * (NCH // RING) + 16)
                sp.wait_ge(s_x2T_out[b], 32 * (NCH // RING) + 32)

        @block.gpsimd
        def _(pool):
            pool.sem_inc(s_rs, RING)
            pool.wait_ge(s_init, 1)

            def norms(c, b, r):
                pair = not isinstance(c, int) or c + NORM2 < NCH
                q = (b + NORM2) % RING
                k = slice(0 if pair else 2, 4)
                pool.wait_ge(s_ve2, done(c))
                pool.wait_ge(s_x2, free(c))
                if pair:
                    pool.wait_ge(s_ve1, done(c + NORM2))
                pool.wait_ge(s_hx, done(c + NORM2 - RING) if pair else done(NCH - 1))
                nc.gpsimd.tensor_tensor(rp[q][:, k], vp[q][:, k], C["neghalf"][:, k], ALU.pow).then_inc(s_rs, 1)

            def first_norms(c, b, r):
                if isinstance(c, int) and c < NORM2:
                    pool.wait_ge(s_ve1, done(c))
                    pool.wait_ge(s_hx, free(c))
                    nc.gpsimd.tensor_tensor(rp[b][:, 0:2], vp[b][:, 0:2], C["neghalf"][:, 0:2], ALU.pow).then_inc(s_rs, 1)

            def scatter(c, b, r):
                pool.wait_ge(s_slot, done(c))
                pool.wait_ge(s_x2r, done(c))
                pool.sem_inc(s_apart_pool, 1)
                for j in range(4):
                    nc.gpsimd.indirect_dma_start(scratch["xs"], bass.IndirectOffsetOnAxis(ap=slu[b][:, j:j + 1], axis=0),
                                                 x2r[b][:, j // 2, :], None).then_inc(s_scat[b], 16)
            pipeline(pool, NCH, RING, [(8, scatter), (0, first_norms), (NORM2, norms)], peel=3)
            for b in range(RING):
                pool.wait_ge(s_scat[b], 64 * (NCH // RING))

        @block.scalar
        def _(act):
            for s in (s_x1T, s_x2T, s_x2r, s_Ms, s_x1, s_hx, s_x2):
                act.sem_inc(s, RING)
            act.wait_ge(s_init, 1)

            def decay_state(c, b, r):
                act.wait_ge(s_M, done(c - 1))
                nc.scalar.activation(Msa[b][:, :], Ma[b][:, :], ACT.Copy, scale=c16)
                nc.scalar.activation(Msb[b][:, :], Mb[b][:, :], ACT.Copy, scale=c16).then_inc(s_Ms, 1)

            def x2_columns(c, b, r):
                act.wait_ge(s_x2Tp, done(c))
                act.wait_ge(s_x2T_out[b], 32 * r + 32)
                nc.scalar.activation(x2a[b][:, :], ps_x2[:, 0:2 * P], ACT.Copy)
                nc.scalar.activation(x2b[b][:, :], ps_x2[0:DB, 2 * P:4 * P], ACT.Copy).then_inc(s_x2T, 1)

            def normed1(c, b, r):
                act.wait_ge(s_nb1, done(c))
                act.wait_ge(s_x1Tp, free(c))
                for half in range(2):
                    last = nc.scalar.activation(x1[b][:, half, :], h[b][:, half, :], ACT.Identity,
                                                bias=nb1[b][:, half:half + 1], scale=rp[b][:, half:half + 1])
                last.then_inc(s_x1, 1)

            def residual_own(c, b, r):
                act.wait_ge(s_h2, free(c))
                for half in range(2):
                    last = nc.scalar.activation(hx[b][:, half, :], h[b][:, half, :], ACT.Identity,
                                                bias=nb1[b][:, half:half + 1], scale=rq1[b][:, half:half + 1])
                last.then_inc(s_hx, 1)

            def normed2(c, b, r):
                act.wait_ge(s_nb2, done(c))
                act.wait_ge(s_x2r, free(c))
                act.wait_ge(s_x2Tp, free(c))
                for half in range(2):
                    last = nc.scalar.activation(x2[b][:, half, :], h2[b][:, half, :], ACT.Identity,
                                                bias=nb2[b][:, half:half + 1], scale=rp[(b + NORM2) % RING][:, 2 + half:3 + half])
                last.then_inc(s_x2, 1)

            def x2_rows(c, b, r):
                act.wait_ge(s_x2, done(c))
                if not (isinstance(r, int) and r == 0):
                    act.wait_ge(s_scat[b], 64 * r)
                nc.scalar.activation(x2r[b][:, :, :], x2[b][:, :, :], ACT.Copy).then_inc(s_x2r, 1)

            def x1_columns(c, b, r):
                act.wait_ge(s_x1Tp, done(c))
                act.wait_ge(s_om, free(c))
                nc.scalar.activation(x1a[b][:, :], ps_x1[:, 0:2 * P], ACT.Copy)
                nc.scalar.activation(x1b[b][:, :], ps_x1[0:DB, 2 * P:4 * P], ACT.Copy).then_inc(s_x1T, 1)
            pipeline(act, NCH, RING, [(1, normed1), (5, normed2), (2, decay_state), (1, residual_own), (1, x1_columns),
                                      (5, x2_columns), (6, x2_rows)], peel=3)

        @block.vector
        def _(dve):
            nc.vector.memset(Ma[0][:, :], 0.0)
            nc.vector.memset(Mb[0][:, :], 0.0)
            nc.vector.memset(ld[0][:, :], 0.0).then_inc(s_init, 1)
            dve.wait_ge(s_init, 1)
            for s in (s_nb1, s_nb2, s_st1, s_ag1, s_ve1, s_sc, s_M, s_h2, s_st2, s_ag2, s_ve2, s_lg, s_mx, s_ix,
                      s_oh, s_ohs, s_ld, s_pb8, s_prod, s_slf, s_slot):
                dve.sem_inc(s, RING)

            def stats1(c, b, r):
                dve.wait_ge(s_h_in[b], 16 * r + 16)
                nc.vector.bn_stats(st1[b][:, 0, :], h[b][:, 0, :])
                nc.vector.bn_stats(st1[b][:, 1, :], h[b][:, 1, :]).then_inc(s_st1, 1)

            def moments1(c, b, r):
                dve.wait_ge(s_st1, done(c))
                dve.sem_inc(s_apart_dve, 1)
                nc.vector.bn_aggr(mv1[b][:, 0, :], st1[b][:, 0, :])
                nc.vector.bn_aggr(mv1[b][:, 1, :], st1[b][:, 1, :]).then_inc(s_ag1, 1)

            def variance1(c, b, r):
                dve.wait_ge(s_ag1, done(c))
                dve.wait_ge(s_rs, free(c))
                nc.vector.tensor_scalar(vp[b][:, 0:2], mv1[b][:, :, 1], LN_EPS, None, ALU.add).then_inc(s_ve1, 1)

            def shift1(c, b, r):
                dve.wait_ge(s_rs, done(c))
                dve.wait_ge(s_hx, free(c))
                nc.vector.tensor_scalar(rq1[b][:, :], rp[b][:, 0:2], 1.0, None, ALU.add)
                nc.vector.scalar_tensor_tensor(out=nb1[b][:, :], in0=mv1[b][:, :, 0], scalar=-1.0, in1=rp[b][:, 0:2],
                                               op0=ALU.mult, op1=ALU.mult).then_inc(s_nb1, 1)

            def shift2(c, b, r):
                dve.wait_ge(s_rs, done(c + NORM2))
                dve.wait_ge(s_x2, free(c))
                nc.vector.scalar_tensor_tensor(out=nb2[b][:, :], in0=mv2[b][:, :, 0], scalar=-1.0,
                                               in1=rp[(b + NORM2) % RING][:, 2:4],
                                               op0=ALU.mult, op1=ALU.mult).then_inc(s_nb2, 1)

            def masked(c, b, r):
                dve.wait_ge(s_scp, done(c))
                nc.vector.tensor_tensor(sc[b][:, :], ps_sc[:, 0:2 * P], C["maskf"][:, :, :, :].rearrange("p a s b -> p (a s b)"),
                                        ALU.mult).then_inc(s_sc, 1)

            def state(c, b, r):
                dve.wait_ge(s_mp, done(c))
                dve.wait_ge(s_Ms, done(c))
                dve.wait_ge(s_om, done(c - 2))
                n = (b + 1) % RING
                nc.vector.scalar_tensor_tensor(out=Ma[n][:, :], in0=ps_m[:, 0:D], scalar=c16, in1=Msa[b][:, :],
                                               op0=ALU.mult, op1=ALU.add)
                nc.vector.scalar_tensor_tensor(out=Mb[n][:, :], in0=ps_m[0:DB, D:2 * D], scalar=c16, in1=Msb[b][:, :],
                                               op0=ALU.mult, op1=ALU.add).then_inc(s_M, 1)

            def residual(c, b, r):
                dve.wait_ge(s_om, done(c))
                dve.wait_ge(s_hx, done(c))
                dve.wait_ge(s_x2, free(c))
                dve.wait_ge(s_h2_out[b], 16 * r + 16)
                nc.vector.scalar_tensor_tensor(out=h2[b][:, :, :], in0=ps_o[:, 0:2 * D].rearrange("p (a d) -> p a d", a=2),
                                               scalar=C["decay"][:, 0:1], in1=hx[b][:, :, :],
                                               op0=ALU.mult, op1=ALU.add).then_inc(s_h2, 1)

            def stats2(c, b, r):
                dve.wait_ge(s_h2, done(c))
                nc.vector.bn_stats(st2[b][:, 0, :], h2[b][:, 0, :])
                nc.vector.bn_stats(st2[b][:, 1, :], h2[b][:, 1, :]).then_inc(s_st2, 1)

            def moments2(c, b, r):
                dve.wait_ge(s_st2, done(c))
                dve.sem_inc(s_apart_dve, 1)
                nc.vector.bn_aggr(mv2[b][:, 0, :], st2[b][:, 0, :])
                nc.vector.bn_aggr(mv2[b][:, 1, :], st2[b][:, 1, :]).then_inc(s_ag2, 1)

            def variance2(c, b, r):
                dve.wait_ge(s_ag2, done(c))
                dve.wait_ge(s_rs, free(c + NORM2))
                nc.vector.tensor_scalar(vp[(b + NORM2) % RING][:, 2:4], mv2[b][:, :, 1], LN_EPS, None, ALU.add).then_inc(s_ve2, 1)

            def logits_out(c, b, r):
                dve.wait_ge(s_lgp, done(c))
                nc.vector.tensor_copy(lg[b][:, :, :], ps_lg[:, 0:2 * (NE + 1)].rearrange("p (a e) -> p a e", a=2)).then_inc(s_lg, 1)

            def highest(c, b, r):
                dve.wait_ge(s_lg, done(c))
                dve.sem_inc(s_apart_dve, 1)
                nc.vector.max(mx[b][:, 0, :], lg[b][:, 0, 0:NE])
                nc.vector.max(mx[b][:, 1, :], lg[b][:, 1, 0:NE]).then_inc(s_mx, 1)

            def chosen(c, b, r):
                dve.wait_ge(s_mx, done(c))
                dve.sem_inc(s_apart_dve, 1)
                nc.vector.max_index(ix[b][:, 0, :], mx[b][:, 0, :], lg[b][:, 0, 0:NE])
                nc.vector.max_index(ix[b][:, 1, :], mx[b][:, 1, :], lg[b][:, 1, 0:NE]).then_inc(s_ix, 1)
                nc.vector.tensor_tensor(C["pre"][:, bass.ds(2 * c, 2), 0:1], mx[b][:, :, 0:1], mx[b][:, :, 1:2], ALU.subtract)
                nc.vector.tensor_scalar(C["pre"][:, bass.ds(2 * c, 2), 1:2], lg[b][:, :, NE:NE + 1], C["sgb"][:, 0:1], None, ALU.add)

            def onehot(c, b, r):
                dve.wait_ge(s_ix, done(c))
                nc.vector.tensor_tensor(oh[b][:, :, :].rearrange("p (a k) e -> p a k e", k=2),
                                        C["iota8"][:, :].unsqueeze(1).unsqueeze(1).to_broadcast([P, 2, 2, NE]),
                                        ix[b][:, :, 0:2].unsqueeze(3).to_broadcast([P, 2, 2, NE]),
                                        ALU.is_equal).then_inc(s_oh, 1)

            def onehot_sum(c, b, r):
                dve.wait_ge(s_oh, done(c))
                pair = oh[b][:, :, :].rearrange("p (a k) e -> p a k e", k=2)
                nc.vector.tensor_tensor(ohs[b][:, :, :], pair[:, :, 0, :], pair[:, :, 1, :], ALU.add).then_inc(s_ohs, 1)

            def load_chunk(c, b, r):
                dve.wait_ge(s_ohs, done(c))
                nc.vector.tensor_tensor(ldc[b][:, :], ohs[b][:, 0, :], ohs[b][:, 1, :], ALU.add).then_inc(s_ld, 1)

            def load_sum(c, b, r):
                n = (b + 1) % RING
                dve.wait_ge(s_ld, 2 * c + RING + 1)
                nc.vector.tensor_tensor(ld[n][:, :], ld[b][:, :], ldc[b][:, :], ALU.add).then_inc(s_ld, 1)

            def bases(c, b, r):
                dve.wait_ge(s_posp, done(c))
                nc.vector.tensor_tensor(pb8[b][:, :, :], ps_pos[:, 0:2 * NE].rearrange("p (a e) -> p a e", a=2),
                                        C["ebase"][:, :].unsqueeze(1).to_broadcast([P, 2, NE]), ALU.add).then_inc(s_pb8, 1)

            def chosen_bases(c, b, r):
                dve.wait_ge(s_pb8, done(c))
                nc.vector.tensor_tensor(prod[b][:, :, :].rearrange("p (a k) e -> p a k e", k=2),
                                        oh[b][:, :, :].rearrange("p (a k) e -> p a k e", k=2),
                                        pb8[b][:, :, :].unsqueeze(2).to_broadcast([P, 2, 2, NE]), ALU.mult).then_inc(s_prod, 1)

            def slot_sums(c, b, r):
                dve.wait_ge(s_prod, done(c))
                nc.vector.reduce_sum(slf[b][:, :], prod[b][:, :, :], AX.X).then_inc(s_slf, 1)

            def slots(c, b, r):
                dve.wait_ge(s_slf, done(c))
                nc.vector.tensor_copy(C["slots"][:, bass.ds(c, 1), :].rearrange("p c k -> p (c k)"), slf[b][:, :])
                if not (isinstance(r, int) and r == 0):
                    dve.wait_ge(s_scat[b], 64 * r)
                nc.vector.tensor_copy(slu[b][:, :], slf[b][:, :]).then_inc(s_slot, 1)
            pipeline(dve, NCH, RING, [(1, shift1), (5, shift2), (7, load_chunk), (4, residual), (7, load_sum), (0, stats1),
                                      (7, bases), (4, stats2), (6, logits_out), (7, chosen_bases), (0, moments1),
                                      (4, moments2), (6, highest), (7, slot_sums), (0, variance1), (4, variance2), (6, chosen),
                                      (7, slots), (2, masked), (6, onehot), (2, state),
                                      (6, onehot_sum)], peel=4)
            dve.wait_ge(s_ld, 2 * NCH + RING)
            nc.vector.tensor_copy(C["load"][:, :], ld[NCH % RING][:, :])

        @block.tensor
        def _(pe):
            for s in (s_x1Tp, s_scp, s_om, s_mp, s_x2Tp, s_lgp, s_posp):
                pe.sem_inc(s, RING)
            pe.wait_ge(s_init, 1)

            def columns(out, x, s):
                for half in range(2):
                    nc.tensor.transpose(out[:, half * P:(half + 1) * P], x[:, half, 0:DA], ident[:, :])
                    last = nc.tensor.transpose(out[0:DB, (2 + half) * P:(3 + half) * P], x[:, half, DA:D], ident[:, :])
                last.then_inc(s, 1)

            def x1_transposes(c, b, r):
                pe.wait_ge(s_x1, done(c))
                pe.wait_ge(s_x1T, done(c - 1))
                columns(ps_x1, x1[b], s_x1Tp)

            def scores(c, b, r):
                pe.wait_ge(s_x1T, done(c))
                pe.wait_ge(s_k_in[b], 48 * r + 48)
                pe.wait_ge(s_sc, done(c - 1))
                mm(nc, ps_sc[:, 0:2 * P], [(kqa[b][:, :], x1a[b][:, :]), (kqb[b][:, :], x1b[b][:, :])]).then_inc(s_scp, 1)

            def attend(c, b, r):
                pe.wait_ge(s_sc, done(c))
                pe.wait_ge(s_M, done(c - 1))
                pe.wait_ge(s_h2, done(c - 1))
                for half in range(2):
                    t = slice(half * P, (half + 1) * P)
                    last = mm(nc, ps_o[:, half * D:(half + 1) * D],
                       [(sc[b][:, t], kqvo[b][:, D:2 * D]), (x1a[b][:, t], Ma[b][:, :]), (x1b[b][:, t], Mb[b][:, :])])
                last.then_inc(s_om, 1)

            def writes(c, b, r):
                pe.wait_ge(s_k_in[b], 48 * r + 48)
                pe.wait_ge(s_M, done(c - 1))
                mm(nc, ps_m[:, 0:D], [(kqvo[b][:, 0:DA], kqvo[b][:, D:2 * D])])
                mm(nc, ps_m[0:DB, D:2 * D], [(kqvo[b][:, DA:D], kqvo[b][:, D:2 * D])]).then_inc(s_mp, 1)

            def x2_transposes(c, b, r):
                pe.wait_ge(s_x2, done(c))
                pe.wait_ge(s_x2T, done(c - 1))
                columns(ps_x2, x2[b], s_x2Tp)

            def logits(c, b, r):
                pe.wait_ge(s_x2T, done(c))
                pe.wait_ge(s_lg, done(c - 1))
                for half in range(2):
                    t = slice(half * P, (half + 1) * P)
                    last = mm(nc, ps_lg[:, half * (NE + 1):(half + 1) * (NE + 1)],
                              [(x2a[b][:, t], W["rw_a"][:, :]), (x2b[b][:, t], W["rw_b"][:, :])])
                last.then_inc(s_lgp, 1)

            def positions(c, b, r):
                pe.wait_ge(s_ohs, done(c))
                pe.wait_ge(s_ld, 2 * c + RING)
                pe.wait_ge(s_pb8, done(c - 1))
                mm(nc, ps_pos[:, 0:NE], [(C["tri"][:, :], ohs[b][:, 0, :]), (C["ones"][:, :], ld[b][:, :])])
                mm(nc, ps_pos[:, NE:2 * NE], [(C["tri"][:, :], ohs[b][:, 1, :]), (C["ones"][:, :], ohs[b][:, 0, :]),
                                              (C["ones"][:, :], ld[b][:, :])]).then_inc(s_posp, 1)
            pipeline(pe, NCH, RING, [(6, logits), (7, positions), (2, scores), (2, writes), (1, x1_transposes), (5, x2_transposes),
                                (3, attend)], peel=3)
    nc.clear_and_free_semaphores(sems)
    nc.all_engine_barrier()


TURN = 4
GATE_UP, DOWN = 2, 5
FIELDS = TURN + DOWN - GATE_UP
EBITS = NE.bit_length() - 1
TURNS = NTILE // TURN + 2


def tile_done(t):
    return t + 1 + TURN


def experts(nc, scratch, C, W):
    ctx = ExitStack()
    sems = []
    with ctx:
        def sb(name, shape, dt=F32):
            return ctx.enter_context(nc.sbuf_tensor(name, shape, dt))

        def pair(name, shape, dt=F32):
            return [sb(f"{name}_{n}", shape, dt) for n in range(2)]

        def pb(name, shape, dt=F32):
            return ctx.enter_context(nc.psum_tensor(name, shape, dt))

        def sem(name):
            sems.append(nc.alloc_semaphore(name))
            return sems[-1]

        zrow = sb("zrow", [P, D])
        ident_r = sb("ident_r", [P, P], F32R)
        cnt = sb("cnt", [P, NE])
        padf = sb("padf", [P, NE])
        padu = sb("padu", [P, NE], U32)
        nti = sb("nti", [P, NE], I32)
        ntf = sb("ntf", [P, NE])
        ends = sb("ends", [1, NE])
        tno = sb("tno", [1, NTILE])
        past = sb("past", [1, NE, NTILE])
        leap = sb("leap", [1, NE, NTILE])
        ef = sb("ef", [1, NTILE])
        rf = sb("rf", [1, NTILE])
        efp = sb("efp", [1, 2 + TURNS, TURN])
        pack = sb("pack", [1, TURNS])
        turn_e = sb("turn_e", [1, TURNS], I32)
        tile_row = sb("tile_row", [1, NTILE], I32)
        xt = [sb(f"xt_{n}", [P, D]) for n in range(TURN)]
        xs2 = pair("xs2", [P, 2 * D], F32R)
        xc = pair("xc", [P, 3, P], F32R)
        sg = pair("sg", [P, HE])
        hm = pair("hm", [P, HE])
        hs2 = pair("hs2", [P, 2 * HE], F32R)
        hc = pair("hc", [P, 3, P], F32R)
        y = [sb(f"y_{n}", [P, D]) for n in range(TURN)]
        ps_xT = [pb(f"ps_xT{n}", [P, 512]) for n in range(2)]
        ps_gu = [pb(f"ps_gu{n}", [P, 512]) for n in range(2)]
        ps_hT = [pb(f"ps_hT{n}", [P, 512]) for n in range(2)]
        ps_y = [pb(f"ps_y{n}", [P, 512]) for n in range(2)]

        s_cntp, s_step, s_iota, s_pad, s_padded, s_rows, s_table = (sem(n) for n in
                                                            ("count_product", "table_step", "tile_numbers", "pad_rows", "padded", "tile_rows", "table"))
        s_zrow = sem("zero_row")
        s_x_in = [sem(f"x_in{n}") for n in range(TURN)]
        s_y_out = [sem(f"y_out{n}") for n in range(TURN)]
        s_xh, s_xl, s_xT, s_xc, s_gu, s_sg, s_hm = (sem(n) for n in
                                                    ("x_lead", "x_rest", "xT", "x_copied", "gate_up", "silu", "hidden"))
        s_hh, s_hl, s_hT, s_hc, s_yp, s_y1, s_y = (sem(n) for n in
                                                   ("h_lead", "h_rest", "hT", "h_copied", "down", "y_copied", "y_added"))
        block = ctx.enter_context(nc.Block())

        def rest(eng, split, whole):
            lead = split[:, 0:D].bitcast(F32)
            eng.tensor_tensor(split[:, D:2 * P], whole[:, DA:D], lead[:, DA:D], ALU.subtract)
            return eng.tensor_tensor(split[:, 2 * P:2 * D], whole[:, 0:DA], lead[:, 0:DA], ALU.subtract)

        @block.gpsimd
        def _(pool):
            nc.gpsimd.iota(tno[:, :], pattern=[[1, NTILE]], base=0, channel_multiplier=0,
                           allow_small_or_imprecise_dtypes=True).then_inc(s_iota, 1)
            nc.gpsimd.memset(zrow[:, :], 0.0).then_inc(s_zrow, 1)
            pool.wait_ge(s_zrow, 1)
            pool.wait_ge(s_pad, 1)
            for e in range(NE):
                nc.gpsimd.indirect_dma_start(scratch["xs"], bass.IndirectOffsetOnAxis(ap=padu[:, e:e + 1], axis=0),
                                             zrow[:, :], None).then_inc(s_padded, 16)
            pool.wait_ge(s_padded, 16 * NE)
            pool.sem_inc(s_xl, TURN)

            def x_rest(t, b, r):
                pool.wait_ge(s_xh, tile_done(t))
                rest(nc.gpsimd, xs2[b % 2], xt[b]).then_inc(s_xl, 1)
            pipeline(pool, NTILE, TURN, [(0, x_rest)])

        @block.sync
        def _(sp):
            for n in range(TURN):
                sp.sem_inc(s_y_out[n], 16)
            sp.wait_ge(s_padded, 16 * NE)
            sp.wait_ge(s_rows, 1)

            def load(t, b, r):
                if not (isinstance(t, int) and t < TURN):
                    sp.wait_ge(s_xl, tile_done(t - TURN))
                row = sp.value_load(tile_row[0:1, bass.ds(t, 1)], min_val=0, max_val=ROWS - P)
                sp.dma_start(xt[b][:, :], scratch["xs"][bass.ds(row, P), :]).then_inc(s_x_in[b], 16)

            def store(t, b, r):
                sp.wait_ge(s_y, tile_done(t))
                sp.dma_start(scratch["ys"][bass.ds(t * P, P), :], y[b][:, :]).then_inc(s_y_out[b], 16)
            pipeline(sp, NTILE, TURN, [(8, store), (0, load)], peel=2)
            for n in range(TURN):
                sp.wait_ge(s_y_out[n], 16 * (NTILE // TURN) + 16)

        @block.scalar
        def _(act):
            for s in (s_xh, s_sg, s_hh, s_hc, s_y1):
                act.sem_inc(s, TURN)

            def x_lead(t, b, r):
                act.wait_ge(s_x_in[b], 16 * r + 16)
                act.wait_ge(s_xT, tile_done(t - 2))
                nc.scalar.activation(xs2[b % 2][:, 0:D], xt[b][:, :], ACT.Copy).then_inc(s_xh, 1)

            def silu(t, b, r):
                act.wait_ge(s_gu, tile_done(t))
                act.wait_ge(s_hm, tile_done(t - 2))
                nc.scalar.activation(sg[b % 2][:, :], ps_gu[b % 2][:, 0:HE], ACT.Silu).then_inc(s_sg, 1)

            def h_lead(t, b, r):
                act.wait_ge(s_hm, tile_done(t))
                act.wait_ge(s_hT, tile_done(t - 2))
                nc.scalar.activation(hs2[b % 2][:, 0:HE], hm[b % 2][:, :], ACT.Copy).then_inc(s_hh, 1)

            def h_copy(t, b, r):
                act.wait_ge(s_hT, tile_done(t))
                act.wait_ge(s_yp, tile_done(t - 2))
                nc.scalar.activation(hc[b % 2][:, :, :].rearrange("p a n -> p (a n)"), ps_hT[b % 2][:, 0:3 * P], ACT.Copy).then_inc(s_hc, 1)

            def y_copy(t, b, r):
                act.wait_ge(s_yp, tile_done(t))
                act.wait_ge(s_y_out[b], 16 * r + 16)
                nc.scalar.activation(y[b][:, :], ps_y[b % 2][:, 0:D], ACT.Copy).then_inc(s_y1, 1)
            pipeline(act, NTILE, TURN, [(3, h_lead), (0, x_lead), (2, silu), (5, y_copy), (4, h_copy)], peel=2)

        @block.vector
        def _(dve):
            n = [0]

            def step(ins):
                n[0] += 1
                ins.then_inc(s_step, 1)
                dve.wait_ge(s_step, n[0])
            step(nc.vector.tensor_copy(ident_r[:, :], C["ident"][:, :]))
            dve.wait_ge(s_cntp, 1)
            step(nc.vector.tensor_copy(cnt[:, :], ps_xT[0][:, 0:NE]))
            step(nc.vector.tensor_tensor(padf[:, :], cnt[:, :], C["ebase"][:, :], ALU.add))
            nc.vector.tensor_scalar(padu[:, :], padf[:, :], C["partf"][:, 0:1], None, ALU.add).then_inc(s_pad, 1)
            step(nc.vector.tensor_scalar(nti[:, :], cnt[:, :], float(P - 1), None, ALU.add))
            step(nc.vector.tensor_scalar(nti[:, :], nti[:, :], P.bit_length() - 1, None, ALU.arith_shift_right))
            step(nc.vector.tensor_copy(ntf[:, :], nti[:, :]))
            step(nc.vector.tensor_copy(ends[:, :], ntf[0:1, :]))
            for e in range(1, NE):
                step(nc.vector.tensor_tensor(ends[:, e:e + 1], ends[:, e:e + 1], ends[:, e - 1:e], ALU.add))
            step(nc.vector.tensor_scalar(C["jump"][:, :], ntf[:, :], -float(P), float(CAP), ALU.mult, ALU.add))
            dve.wait_ge(s_iota, 1)
            step(nc.vector.tensor_tensor(past[:, :, :], tno[:, :].unsqueeze(1).to_broadcast([1, NE, NTILE]),
                                         ends[:, :].unsqueeze(2).to_broadcast([1, NE, NTILE]), ALU.is_ge))
            step(nc.vector.tensor_tensor(leap[:, :, :], past[:, :, :], C["jump"][0:1, :].unsqueeze(2).to_broadcast([1, NE, NTILE]), ALU.mult))
            step(nc.vector.reduce_sum(rf[:, :], leap[:, :, :].rearrange("p e t -> p t e"), AX.X))
            step(nc.vector.scalar_tensor_tensor(out=rf[:, :], in0=tno[:, :], scalar=float(P), in1=rf[:, :], op0=ALU.mult, op1=ALU.add))
            nc.vector.tensor_copy(tile_row[:, :], rf[:, :]).then_inc(s_rows, 1)
            step(nc.vector.reduce_sum(ef[:, :], past[:, :, :].rearrange("p e t -> p t e"), AX.X))
            nc.vector.memset(efp[:, :, :], 0.0)
            step(nc.vector.memset(pack[:, :], 0.0))
            step(nc.vector.tensor_scalar(efp[:, 2:2 + NTILE // TURN, :].rearrange("p q f -> p (q f)"), ef[:, :],
                                         float(NE - 1), None, ALU.min))
            for k in reversed(range(FIELDS)):
                q, f = divmod(2 * TURN - DOWN + k, TURN)
                step(nc.vector.scalar_tensor_tensor(out=pack[:, :].unsqueeze(2), in0=pack[:, :].unsqueeze(2), scalar=float(NE),
                                                    in1=efp[:, q:q + TURNS, f:f + 1], op0=ALU.mult, op1=ALU.add))
            nc.vector.tensor_copy(turn_e[:, :], pack[:, :]).then_inc(s_table, 1)
            for s in (s_xc, s_hm, s_hl, s_y):
                dve.sem_inc(s, TURN)

            def x_copy(t, b, r):
                dve.wait_ge(s_xT, tile_done(t))
                dve.wait_ge(s_gu, tile_done(t - 2))
                nc.vector.tensor_copy(xc[b % 2][:, :, :].rearrange("p a n -> p (a n)"), ps_xT[b % 2][:, 0:3 * P]).then_inc(s_xc, 1)

            def hidden(t, b, r):
                dve.wait_ge(s_sg, tile_done(t))
                dve.wait_ge(s_hl, tile_done(t - 2))
                nc.vector.tensor_tensor(hm[b % 2][:, :], sg[b % 2][:, :], ps_gu[b % 2][:, HE:2 * HE], ALU.mult).then_inc(s_hm, 1)

            def h_rest(t, b, r):
                dve.wait_ge(s_hh, tile_done(t))
                rest(nc.vector, hs2[b % 2], hm[b % 2]).then_inc(s_hl, 1)

            def y_add(t, b, r):
                dve.wait_ge(s_y1, tile_done(t))
                nc.vector.tensor_tensor(y[b][:, :], ps_y[b % 2][:, D:2 * D], y[b][:, :], ALU.add).then_inc(s_y, 1)
            pipeline(dve, NTILE, TURN, [(3, h_rest), (6, y_add), (1, x_copy), (2, hidden)], peel=2)

        @block.tensor
        def _(pe):
            mm(nc, ps_xT[0][:, 0:NE], [(C["ones"][:, :], C["load"][:, :])]).then_inc(s_cntp, 1)
            for s in (s_xT, s_gu, s_hT, s_yp):
                pe.sem_inc(s, TURN)
            pe.wait_ge(s_table, 1)

            def columns(out, split, s):
                for k in range(3):
                    last = mm(nc, out[:, k * P:(k + 1) * P], [(split[:, k * P:(k + 1) * P], ident_r[:, :])])
                last.then_inc(s, 1)

            def product(out, x, wa, wb, at, s):
                mm(nc, out, [(x[:, 0, :], wa[0][:, at]), (x[:, 0, :], wa[1][:, at]), (x[:, 2, :], wa[0][:, at]),
                             (x[:, 1, :], wb[0][:, at]), (x[:, 1, :], wb[1][:, at])]).then_inc(s, 1)

            def x_columns(t, b, r):
                pe.wait_ge(s_xl, tile_done(t))
                pe.wait_ge(s_xc, tile_done(t - 2))
                columns(ps_xT[b % 2], xs2[b % 2], s_xT)

            held = []

            def load_experts(i):
                held[:] = [pe.value_load(turn_e[0:1, bass.ds(i, 1)], min_val=0, max_val=NE ** FIELDS - 1)]

            def expert(b, lag):
                field = (b + lag) % TURN + DOWN - lag
                return (held[0] >> (EBITS * field)) & (NE - 1)

            def gate_up(t, b, r):
                e = expert(b, GATE_UP)
                pe.wait_ge(s_xc, tile_done(t))
                pe.wait_ge(s_hm, tile_done(t - 2))
                product(ps_gu[b % 2][:, 0:2 * HE], xc[b % 2], W["gu_a"], W["gu_b"], bass.ds(e * (2 * HE), 2 * HE), s_gu)

            def h_columns(t, b, r):
                pe.wait_ge(s_hl, tile_done(t))
                pe.wait_ge(s_hc, tile_done(t - 2))
                columns(ps_hT[b % 2], hs2[b % 2], s_hT)

            def down(t, b, r):
                e = expert(b, DOWN)
                pe.wait_ge(s_hc, tile_done(t))
                pe.wait_ge(s_y, tile_done(t - 2))
                x, out = hc[b % 2], ps_y[b % 2]
                nc.tensor.matmul(out[:, 0:2 * D], x[:, 0, :], W["dn_a"][:, bass.ds(e * (2 * D), 2 * D)], start=True, stop=False)
                nc.tensor.matmul(out[:, 0:2 * D], x[:, 1, :], W["dn_b"][:, bass.ds(e * (2 * D), 2 * D)], start=False, stop=False)
                nc.tensor.matmul(out[:, 0:D], x[:, 2, :], W["dn_a"][:, bass.ds(e * (2 * D), D)], start=False, stop=True).then_inc(s_yp, 1)
            pipeline(pe, NTILE, TURN, [(1, x_columns), (GATE_UP, gate_up), (DOWN, down), (4, h_columns)], peel=2,
                     turn=load_experts)
    nc.clear_and_free_semaphores(sems)
    nc.all_engine_barrier()


def combine(nc, scratch, C, W, out):
    ctx = ExitStack()
    sems = []
    MP = HS // (2 * P)
    with ctx:
        def sb(name, shape, dt=F32):
            return ctx.enter_context(nc.sbuf_tensor(name, shape, dt))

        def ring(name, shape, dt=F32):
            return [sb(f"{name}_{n}", shape, dt) for n in range(RING)]

        def pb(name, shape, dt=F32):
            return ctx.enter_context(nc.psum_tensor(name, shape, dt))

        def sem(name):
            sems.append(nc.alloc_semaphore(name))
            return sems[-1]

        th = sb("th", [P, 2 * NCH, 2])
        beta = sb("beta", [P, 2 * NCH])
        gg = sb("gg", [P, 2 * NCH, 2])
        xa = ring("xa", [P, 2 * P])
        xb = ring("xb", [P, 2 * P])
        h2 = ring("h2c", [P, 2, D])
        xah = ring("xah", [P, 2 * P], F32R)
        xal = ring("xal", [P, 2 * P], F32R)
        xbh = ring("xbh", [P, 2 * P], F32R)
        sg = [sb(f"sgs_{n}", [P, 4 * P]) for n in range(MP)]
        pm = [sb(f"pm_{n}", [P, 4 * P]) for n in range(MP)]
        ph = ring("ph", [P, MP, 4 * P], F32R)
        pl = ring("pl", [P, MP, 4 * P], F32R)
        over = sb("over", [P, NE, NCH * 4])
        gidx = sb("gidx", [P, NCH, 4], U32)
        slu = ring("sluc", [P, 4], U32)
        yy = ring("yy", [P, 4, D])
        oo = ring("oo", [P, 2, D])
        ps_g = [pb(f"ps_g{n}", [P, 512]) for n in range(MP)]
        ps_u = [pb(f"ps_u{n}", [P, 512]) for n in range(MP)]
        ps_d = [pb(f"ps_d{n}", [P, 512]) for n in range(2)]

        s_th, s_gs, s_gates = sem("gate_tanhs"), sem("gate_step"), sem("gates_done")
        s_x_in = [sem(f"xc_in{n}") for n in range(RING)]
        s_h2_in = [sem(f"h2c_in{n}") for n in range(RING)]
        s_y_in = [sem(f"yc_in{n}") for n in range(RING)]
        s_o_out = [sem(f"o_out{n}") for n in range(RING)]
        s_over, s_gidx = sem("jumps_chosen"), sem("gather_rows")
        s_slu, s_apart = sem("slots_copied"), sem("apart_c")
        s_xh, s_xl = sem("xc_lead"), sem("xc_rest")
        s_g, s_sg, s_pm, s_ph, s_pl = (sem(n) for n in ("shared_gate_up", "shared_silu", "shared_hidden", "hidden_lead", "hidden_rest"))
        s_d, s_o1, s_ob, s_o2, s_o = sem("shared_down"), sem("sum1"), sem("sum1_rest"), sem("sum2"), sem("sum3")
        block = ctx.enter_context(nc.Block())

        def at(dram, c):
            return dram[bass.ds(c, 1)].rearrange("c a b -> (c a) b")

        def done3(c, m):
            return MP * c + m + 1 + MP

        @block.sync
        def _(sp):
            def loads(c, b, r):
                sp.wait_ge(s_xl, free(c))
                sp.dma_start(xa[b][:, :], at(scratch["x2T"], c)[0:DA, :]).then_inc(s_x_in[b], 16)
                for q in (0, DB):
                    sp.dma_start(xb[b][q:q + DB, :], at(scratch["x2T"], c)[DA:D, :]).then_inc(s_x_in[b], 16)
                sp.wait_ge(s_o1, free(c))
                sp.dma_start(h2[b][:, :, :].rearrange("p a d -> p (a d)"), at(scratch["h2"], c)).then_inc(s_h2_in[b], 16)

            def store(c, b, r):
                sp.wait_ge(s_o, done(c))
                steps = T - c * STEP if isinstance(c, int) and c == NCH - 1 else STEP
                for half in range(2):
                    dst = out.rearrange("(k a) t d -> a t k d", a=2)[half, bass.ds(c * STEP, steps), :, :]
                    sp.dma_start(dst, oo[b][0:steps * HB, half, :]).then_inc(s_o_out[b], 16)
            for b in range(RING):
                sp.sem_inc(s_o_out[b], 32)
            pipeline(sp, NCH, RING, [(0, loads), (5, store)], peel=2)
            for b in range(RING):
                sp.wait_ge(s_o_out[b], 32 * (NCH // RING) + 32)

        @block.gpsimd
        def _(pool):
            pool.sem_inc(s_slu, RING)
            pool.wait_ge(s_gidx, 1)

            def gather(c, b, r):
                pool.wait_ge(s_o, free(c))
                nc.gpsimd.tensor_copy(slu[b][:, :], gidx[:, bass.ds(c, 1), :].rearrange("p c k -> p (c k)")).then_inc(s_slu, 1)
                pool.wait_ge(s_slu, done(c))
                pool.sem_inc(s_apart, 1)
                for j in range(4):
                    nc.gpsimd.indirect_dma_start(yy[b][:, j, :], None, scratch["ys"],
                                                 bass.IndirectOffsetOnAxis(ap=slu[b][:, j:j + 1], axis=0)).then_inc(s_y_in[b], 16)
            pipeline(pool, NCH, RING, [(0, gather)])

        @block.scalar
        def _(act):
            nc.scalar.activation(th[:, :, :], C["pre"][:, :, :], ACT.Tanh, scale=0.5).then_inc(s_th, 1)
            act.sem_inc(s_xh, RING)
            for s in (s_sg, s_ph):
                act.sem_inc(s, MP)

            def x_lead(c, b, r):
                act.wait_ge(s_x_in[b], 48 * r + 48)
                act.wait_ge(s_g, done3(c - RING, MP - 1) if not isinstance(c, int) or c >= RING else 1)
                nc.scalar.activation(xah[b][:, :], xa[b][:, :], ACT.Copy)
                nc.scalar.activation(xbh[b][:, :], xb[b][:, :], ACT.Copy).then_inc(s_xh, 1)

            def silus(c, b, r):
                for m in range(MP + 1):
                    if m < MP:
                        act.wait_ge(s_g, done3(c, m))
                        act.wait_ge(s_pm, done3(c - 1, m))
                        nc.scalar.activation(sg[m][:, :], ps_g[m][:, :], ACT.Silu).then_inc(s_sg, 1)
                    if m == 1:
                        act.wait_ge(s_d, free(c))
                    if m > 0:
                        act.wait_ge(s_pm, done3(c, m - 1))
                        nc.scalar.activation(ph[b][:, m - 1, :], pm[m - 1][:, :], ACT.Copy).then_inc(s_ph, 1)

            pipeline(act, NCH, RING, [(0, x_lead), (1, silus)])

        @block.vector
        def _(dve):
            for s in (s_xl, s_o1, s_ob, s_o2, s_o):
                dve.sem_inc(s, RING)
            for s in (s_pm, s_pl):
                dve.sem_inc(s, MP)
            flat = C["slots"][:, :, :].rearrange("p c k -> p (c k)")
            for e in range(1, NE):
                last = nc.vector.tensor_scalar(over[:, e, :], flat, float(e * CAP), C["jump"][:, e - 1:e], ALU.is_ge, ALU.mult)
            last.then_inc(s_over, 1)
            dve.wait_ge(s_over, 1)
            nc.vector.reduce_sum(over[:, 0, :], over[:, 1:NE, :].rearrange("p e n -> p n e"), AX.X).then_inc(s_over, 1)
            dve.wait_ge(s_over, 2)
            nc.vector.tensor_tensor(gidx[:, :, :].rearrange("p c k -> p (c k)"), flat, over[:, 0, :], ALU.subtract).then_inc(s_gidx, 1)
            dve.wait_ge(s_th, 1)
            nc.vector.tensor_scalar(C["gates"][:, :, 2:3], th[:, :, 1:2], 0.5, 0.5, ALU.mult, ALU.add)
            nc.vector.tensor_scalar(beta[:, :].unsqueeze(2), th[:, :, 1:2], -0.5, 0.5, ALU.mult, ALU.add)
            nc.vector.tensor_scalar(gg[:, :, 0:1], th[:, :, 0:1], 0.5, 0.5, ALU.mult, ALU.add)
            nc.vector.tensor_scalar(gg[:, :, 1:2], th[:, :, 0:1], -0.5, 0.5, ALU.mult, ALU.add).then_inc(s_gs, 1)
            dve.wait_ge(s_gs, 1)
            nc.vector.tensor_tensor(C["gates"][:, :, 0:2], gg[:, :, :], beta[:, :].unsqueeze(2).to_broadcast([P, 2 * NCH, 2]),
                                    ALU.mult).then_inc(s_gates, 1)
            dve.wait_ge(s_gates, 1)

            def x_rest(c, b, r):
                dve.wait_ge(s_xh, done(c))
                nc.vector.tensor_tensor(xal[b][:, :], xa[b][:, :], xah[b][:, :].bitcast(F32), ALU.subtract)
                nc.vector.tensor_tensor(xbh[b][DB:P, :], xb[b][DB:P, :], xbh[b][DB:P, :].bitcast(F32), ALU.subtract).then_inc(s_xl, 1)

            def hiddens(c, b, r):
                for m in range(MP + 1):
                    if m < MP:
                        dve.wait_ge(s_sg, done3(c, m))
                        dve.wait_ge(s_pl, done3(c - 1, m))
                        nc.vector.tensor_tensor(pm[m][:, :], sg[m][:, :], ps_u[m][:, :], ALU.mult).then_inc(s_pm, 1)
                    if m > 0:
                        dve.wait_ge(s_ph, done3(c, m - 1))
                        nc.vector.tensor_tensor(pl[b][:, m - 1, :], pm[m - 1][:, :], ph[b][:, m - 1, :].bitcast(F32),
                                                ALU.subtract).then_inc(s_pl, 1)

            def sums(c, b, r):
                dve.wait_ge(s_h2_in[b], 16 * r + 16)
                dve.wait_ge(s_d, done(c))
                dve.wait_ge(s_o_out[b], 32 * r + 32)
                for half in range(2):
                    last = nc.vector.scalar_tensor_tensor(
                        out=oo[b][:, half, :], in0=ps_d[half][:, 0:D],
                        scalar=C["gates"][:, bass.ds(2 * c + half, 1), 2:3].rearrange("p a k -> p (a k)"), in1=h2[b][:, half, :],
                        op0=ALU.mult, op1=ALU.add)
                last.then_inc(s_o1, 1)
                dve.wait_ge(s_o1, done(c))
                for half in range(2):
                    last = nc.vector.scalar_tensor_tensor(
                        out=oo[b][:, half, :], in0=ps_d[half][:, D:2 * D],
                        scalar=C["gates"][:, bass.ds(2 * c + half, 1), 2:3].rearrange("p a k -> p (a k)"), in1=oo[b][:, half, :],
                        op0=ALU.mult, op1=ALU.add)
                last.then_inc(s_ob, 1)
                dve.wait_ge(s_y_in[b], 64 * r + 64)
                for k, s_in, s_out in ((0, s_ob, s_o2), (1, s_o2, s_o)):
                    dve.wait_ge(s_in, done(c))
                    for half in range(2):
                        last = nc.vector.scalar_tensor_tensor(
                            out=oo[b][:, half, :], in0=yy[b][:, 2 * half + k, :],
                            scalar=C["gates"][:, bass.ds(2 * c + half, 1), k:k + 1].rearrange("p a k -> p (a k)"), in1=oo[b][:, half, :],
                            op0=ALU.mult, op1=ALU.add)
                    last.then_inc(s_out, 1)
            pipeline(dve, NCH, RING, [(3, sums), (0, x_rest), (1, hiddens)])

        @block.tensor
        def _(pe):
            pe.sem_inc(s_g, MP)
            pe.sem_inc(s_d, RING)

            def gate_up(c, b, r):
                pe.wait_ge(s_xl, done(c))
                (wah, wal), (wbh, wbl) = W["sgu_a"], W["sgu_b"]
                for m in range(MP):
                    pe.wait_ge(s_pm, done3(c - 1, m))
                    for bank, w0 in ((ps_g[m], 0), (ps_u[m], HS)):
                        for k in range(2):
                            f = slice(w0 + (2 * m + k) * P, w0 + (2 * m + k + 1) * P)
                            last = mm(nc, bank[:, k * 2 * P:(k + 1) * 2 * P],
                                      [(wah[:, f], xah[b][:, :]), (wah[:, f], xal[b][:, :]), (wal[:, f], xah[b][:, :]),
                                       (wbh[:, f], xbh[b][:, :]), (wbl[:, f], xbh[b][:, :])])
                    last.then_inc(s_g, 1)

            def down(c, b, r):
                pe.wait_ge(s_pl, done3(c, MP - 1))
                pe.wait_ge(s_ob, done(c - 1))
                for half in range(2):
                    for m in range(2 * MP):
                        t = slice(m % 2 * 2 * P + half * P, m % 2 * 2 * P + (half + 1) * P)
                        nc.tensor.matmul(ps_d[half][:, 0:2 * D], ph[b][:, m // 2, t], W["sdn"][:, 2 * m * D:(2 * m + 2) * D],
                                         start=m == 0, stop=False)
                        last = nc.tensor.matmul(ps_d[half][:, 0:D], pl[b][:, m // 2, t], W["sdn"][:, 2 * m * D:(2 * m + 1) * D],
                                                start=False, stop=m == 2 * MP - 1)
                last.then_inc(s_d, 1)
            pipeline(pe, NCH, RING, [(1, gate_up), (2, down)])
    nc.clear_and_free_semaphores(sems)
    nc.all_engine_barrier()


def launch_program(nc, I, out):
    scratch = {
        "hbuf": nc.dram_tensor("hbuf", (TPAD, B, D), F32, kind="Internal").ap(),
        "kqT": nc.dram_tensor("kqT", (NCH, D, P), F32, kind="Internal").ap(),
        "kqvo": nc.dram_tensor("kqvo", (TPAD, NH, 2 * D), F32, kind="Internal").ap(),
        "x2T": nc.dram_tensor("x2T", (NCH, D, 2 * P), F32, kind="Internal").ap(),
        "h2": nc.dram_tensor("h2", (NCH, P, 2 * D), F32, kind="Internal").ap(),
        "xs": nc.dram_tensor("xs", (ROWS, D), F32, kind="Internal").ap(),
        "ys": nc.dram_tensor("ys", (NTILE * P, D), F32, kind="Internal").ap(),
    }
    ctx = ExitStack()
    with ctx:
        def sb(name, shape, dt=F32):
            return ctx.enter_context(nc.sbuf_tensor(name, shape, dt))

        W = {name: (sb(name + "_hi", [P, n], F32R), sb(name + "_lo", [P, n], F32R))
             for name, n in (("gu_a", NE * 2 * HE), ("gu_b", NE * 2 * HE), ("sgu_a", 2 * HS), ("sgu_b", 2 * HS))}
        for name, n in (("dn_a", NE), ("dn_b", NE), ("sdn", HS // P)):
            W[name] = sb(name, [P, n * 2 * D], F32R)
        W["rw_a"] = sb("rw_a", [DA, NE + 1])
        W["rw_b"] = sb("rw_b", [DB, NE + 1])
        C = {"ident": sb("ident", [P, P]), "tri": sb("tri", [P, P], BF16), "ones": sb("ones", [P, P], BF16),
             "neghalf": sb("neghalf", [P, 8]), "iota8": sb("iota8", [P, NE]), "ebase": sb("ebase", [P, NE]),
             "partf": sb("partf", [P, 1]), "maskf": sb("maskf", [P, 2, STEP, HB]), "decay": sb("decay", [P, 2]),
             "sgb": sb("sgb", [P, 1]),
             "slots": sb("slots", [P, NCH, 4]), "jump": sb("jump", [P, NE]), "pre": sb("pre", [P, 2 * NCH, 2]), "gates": sb("gates", [P, 2 * NCH, 3]),
             "load": sb("load", [P, NE], BF16)}
        prepare(nc, I, scratch, W, C)
        attention_tables(nc, I, scratch, C)
        tokens(nc, I, scratch, C, W)
        experts(nc, scratch, C, W)
        combine(nc, scratch, C, W, out)


_INS = ['x', 'x_txt', 'L0_tok_W', 'L0_tok_b', 'L0_tok_cls', 'L0_tok_pos_embed', 'L0_txt_basin_coords', 'L0_txt_proj_w',
        'L0_txt_norm_w', 'L0_attn_w_key', 'L0_attn_w_value', 'L0_attn_w_query', 'L0_attn_w_gate', 'L0_attn_w_out',
        'L0_ffn_router_w', 'L0_ffn_w_gate', 'L0_ffn_w_up', 'L0_ffn_w_down', 'L0_ffn_ws_gate', 'L0_ffn_ws_up',
        'L0_ffn_ws_down', 'L0_ffn_sg_w', 'L0_ffn_sg_b']


def kernel(**inputs):
    import numpy as _np
    import concourse.bacc as _bacc
    from concourse import mybir as _mybir
    from concourse.bass_utils import run_bass_kernel_spmd as _run

    nc = _bacc.Bacc("TRN2", target_bir_lowering=False, num_devices=1)
    arrays, args = {}, {}
    for name in _INS:
        a = _np.ascontiguousarray(inputs[name])
        arrays[f"in_{name}"] = a
        args[name] = nc.dram_tensor(f"in_{name}", a.shape, _mybir.dt.from_np(a.dtype), kind="ExternalInput").ap()
    out = nc.dram_tensor("out_0", (B, T, D), _mybir.dt.float32, kind="ExternalOutput").ap()
    launch_program(nc, args, out)
    r = _run(nc, [arrays], core_ids=[0])
    return r.results[0]["out_0"]
```
